# Optimizing a Trainium2 kernel written in Bass

```python
import numpy as np
import jax
import jax.numpy as jnp

def _softmax(x, axis=-1):
    return jax.nn.softmax(x, axis=axis)

def _gelu(x):
    return jax.nn.gelu(x, approximate=True)

def _silu(x):
    return jax.nn.silu(x)

def _sigmoid(x):
    return jax.nn.sigmoid(x)

def _layernorm(x, axis=-1, eps=1e-05):
    m = jnp.mean(x, axis=axis, keepdims=True)
    v = jnp.var(x, axis=axis, keepdims=True)
    return (x - m) / jnp.sqrt(v + eps)

def _scatter_add(tgt, idx, src, axis=0):
    return tgt.at[idx].add(src)

def _segment_sum(src, seg, n):
    return jax.ops.segment_sum(src, seg, n)
kernel_name = 'mk_decoder_preln_d2_seqx_r8_7d9336'

def setup_inputs(seed: int=0):
    np.random.seed(seed)
    _w = jnp.asarray

    def _rec_inputs():
        import jax
        import jax.numpy as jnp
        _rk = jax.random.key(seed)
        x = -0.000125 + 0.9999 * jax.random.normal(jax.random.fold_in(_rk, 1), (4, 256, 256), jnp.float32)
        _lenS = 256 - jax.random.randint(jax.random.fold_in(_rk, 7), (4,), 0, max(1, 256 // 4) + 1, jnp.int32)
        _lenS2 = 256 - jax.random.randint(jax.random.fold_in(_rk, 8), (4,), 0, max(1, 256 // 4) + 1, jnp.int32)
        itok_BxS_13_99985 = jax.random.randint(jax.random.fold_in(_rk, 11), (4, 256), 13, 99986, jnp.int32)
        _ctx_2048P = jax.random.normal(jax.random.fold_in(_rk, 12), (4, 16, 256), jnp.float32)
        _ctx_2048c = jax.random.dirichlet(jax.random.fold_in(_rk, 512), 0.3 * jnp.ones((16,), jnp.float32), (4, 256))
        _ctx_2048t = jnp.einsum('bsk,bkd->bsd', _ctx_2048c, _ctx_2048P)
        _ctx_2048t = _ctx_2048t * jax.lax.rsqrt(jnp.mean(jnp.square(_ctx_2048t)) + 1e-12) * 0.953939
        ctx_2048 = 6.82029e-06 + 0.0200006 * (_ctx_2048t + 0.3 * jax.random.normal(jax.random.fold_in(_rk, 612), (4, 256, 256), jnp.float32))
        return (x, itok_BxS_13_99985, ctx_2048)
    x, itok_BxS_13_99985, ctx_2048 = _rec_inputs()

    def _L0_attn_setup():
        import jax, jax.numpy as jnp
        import numpy as np
        H = 16
        EPS_DEN = 1e-06

        def _decay_scan(x, decay, init):
            xT = jnp.moveaxis(x, 2, 0)

            def step(s, xt):
                s = decay * s + xt
                return (s, s)
            _, ys = jax.lax.scan(step, init, xT)
            return jnp.moveaxis(ys, 0, 2)

        def _phi(z):
            return jax.nn.elu(z) + 1.0

        def _reference_tuple_inner(x, w_qkv, w_out, decay_param):
            B, T, Hid = x.shape
            D = Hid // H
            qkv = x @ w_qkv
            q, k, v = jnp.split(qkv, 3, axis=-1)

            def to_bhtd(t):
                return t.reshape(B, T, H, D).transpose(0, 2, 1, 3)
            q = _phi(to_bhtd(q))
            k = _phi(to_bhtd(k))
            v = to_bhtd(v)
            decay = jax.nn.sigmoid(decay_param).reshape(1, H, 1)
            init = jnp.zeros((B, H, D), dtype=x.dtype)
            running_kv = _decay_scan(k * v, decay, init)
            running_ksum = _decay_scan(k, decay, init)
            den = jnp.clip(jnp.sum(q * running_ksum, axis=-1, keepdims=True), EPS_DEN, None)
            out = q * running_kv / den
            out = out.transpose(0, 2, 1, 3).reshape(B, T, Hid) @ w_out
            new_kv = running_kv[:, :, -1, :]
            new_ksum = running_ksum[:, :, -1, :]
            return (out, new_kv, new_ksum)
        key = jax.random.key(seed)
        k1, k2, k3 = jax.random.split(key, 3)
        x = jax.random.normal(k1, (2, 512, 256), dtype=jnp.float32)
        w_qkv = jax.random.normal(k2, (256, 768), dtype=jnp.float32) * 0.02
        w_out = jax.random.normal(k3, (256, 256), dtype=jnp.float32) * 0.02
        decay_param = jnp.full((H,), 0.95, dtype=jnp.float32)
        return {'x': x, 'w_qkv': w_qkv, 'w_out': w_out, 'decay_param': decay_param}
    _L0_attn_all = _L0_attn_setup()
    _L0_attn_in = {k: v for k, v in _L0_attn_all.items() if k in ('w_qkv', 'w_out', 'decay_param')}
    del _L0_attn_all

    def _L0_xattn_setup():
        import jax, jax.numpy as jnp
        import numpy as np
        B, S, D = (4, 512, 256)
        E = 4
        F = 1024 // E
        VOCAB = 12500
        key = jax.random.key(seed)
        k1, k2, k3, k4, k5 = jax.random.split(key, 5)
        hidden_states = jax.random.normal(k1, (B, S, D), dtype=jnp.float32)
        token_ids = jax.random.randint(k2, (B, S), 0, VOCAB, dtype=jnp.int64)
        Wg = jax.random.normal(k3, (E, F, D), dtype=jnp.float32) * 0.02
        Wu = jax.random.normal(k4, (E, F, D), dtype=jnp.float32) * 0.02
        Wd = jax.random.normal(k5, (E, D, F), dtype=jnp.float32) * 0.02
        return {'hidden_states': hidden_states, 'token_ids': token_ids, 'Wg': Wg, 'Wu': Wu, 'Wd': Wd}
    _L0_xattn_all = _L0_xattn_setup()
    _L0_xattn_in = {k: v for k, v in _L0_xattn_all.items() if k in ()}
    del _L0_xattn_all

    def _L0_ffn_setup():
        import jax, jax.numpy as jnp
        import numpy as np
        from jax import lax
        D_MODEL = 256
        D_CROSS = 1024
        D_RETR = 128
        D_PRIV = 128
        N_EXPERTS = 2048
        N_HEADS = 8
        K_PER_HEAD = 8
        NUM_KEYS = int(np.sqrt(N_EXPERTS))
        BATCH, SEQ = (2, 256)
        key = jax.random.key(seed)
        ks = jax.random.split(key, 10)
        s = 0.02
        return {'hidden_states': jax.random.normal(ks[0], (BATCH, SEQ, D_MODEL), jnp.float32), 'W_up': jax.random.normal(ks[1], (D_CROSS, D_MODEL), jnp.float32) * s, 'b_up': jnp.zeros((D_CROSS,), jnp.float32), 'W_down': jax.random.normal(ks[2], (D_PRIV, D_CROSS), jnp.float32) * s, 'b_down': jnp.zeros((D_PRIV,), jnp.float32), 'W_q': jax.random.normal(ks[3], (D_RETR * N_HEADS, D_PRIV), jnp.float32) * s, 'keys': jax.random.normal(ks[4], (N_HEADS, NUM_KEYS, 2, D_RETR // 2), jnp.float32) * s, 'down_embed': jax.random.normal(ks[5], (N_EXPERTS, D_PRIV), jnp.float32) * s, 'up_embed': jax.random.normal(ks[6], (N_EXPERTS, D_MODEL), jnp.float32) * s}
    _L0_ffn_all = _L0_ffn_setup()
    _L0_ffn_in = {k: v for k, v in _L0_ffn_all.items() if k in ('W_up', 'b_up', 'W_down', 'b_down', 'W_q', 'keys', 'down_embed', 'up_embed')}
    del _L0_ffn_all

    def _L1_attn_setup():
        import jax, jax.numpy as jnp
        import numpy as np
        from jax import lax
        BLOCKS = 16
        NUM_HEADS = 8
        KEY_DIM = 64
        WIDTH = 64
        D_MODEL = 256

        def _forward(x, conv_w, conv_b, wq, bq, wk, bk, wv, bv, wo, bo, proj_w, proj_b):
            N, T, D = x.shape
            xp = jnp.pad(x, ((0, 0), (2, 0), (0, 0)))
            qkv = lax.conv_general_dilated(xp, conv_w, window_strides=(1,), padding='VALID', dimension_numbers=('NWC', 'WIO', 'NWC')) + conv_b
            q, k, v = jnp.split(qkv, 3, axis=-1)
            block_len = T // BLOCKS
            qb = q.reshape(N * BLOCKS, block_len, WIDTH)
            kb = k.reshape(N * BLOCKS, block_len, WIDTH)
            vb = v.reshape(N * BLOCKS, block_len, WIDTH)
            qh = jnp.einsum('bsd,dhk->bshk', qb, wq) + bq
            kh = jnp.einsum('bsd,dhk->bshk', kb, wk) + bk
            vh = jnp.einsum('bsd,dhk->bshk', vb, wv) + bv
            scale = 1.0 / jnp.sqrt(jnp.asarray(KEY_DIM, qh.dtype))
            scores = jnp.einsum('bqhk,bshk->bhqs', qh * scale, kh)
            causal = jnp.tril(jnp.ones((block_len, block_len), bool))
            scores = jnp.where(causal[None, None], scores, jnp.asarray(-1000000000.0, scores.dtype))
            attn = jax.nn.softmax(scores, axis=-1)
            ctx = jnp.einsum('bhqs,bshk->bqhk', attn, vh)
            mha_out = jnp.einsum('bqhk,hko->bqo', ctx, wo) + bo
            mha_out = mha_out.reshape(N, T, WIDTH)
            out = mha_out @ proj_w + proj_b
            return out
        key = jax.random.key(seed)
        ks = jax.random.split(key, 8)
        N, T = (4, 512)
        s = lambda *sh: 0.02
        x = jax.random.normal(ks[0], (N, T, D_MODEL), jnp.float32)
        conv_w = jax.random.normal(ks[1], (3, D_MODEL, 3 * WIDTH), jnp.float32) * 0.02
        conv_b = jnp.zeros((3 * WIDTH,), jnp.float32)
        wq = jax.random.normal(ks[2], (WIDTH, NUM_HEADS, KEY_DIM), jnp.float32) * 0.05
        wk = jax.random.normal(ks[3], (WIDTH, NUM_HEADS, KEY_DIM), jnp.float32) * 0.05
        wv = jax.random.normal(ks[4], (WIDTH, NUM_HEADS, KEY_DIM), jnp.float32) * 0.05
        bq = jnp.zeros((NUM_HEADS, KEY_DIM), jnp.float32)
        bk = jnp.zeros((NUM_HEADS, KEY_DIM), jnp.float32)
        bv = jnp.zeros((NUM_HEADS, KEY_DIM), jnp.float32)
        wo = jax.random.normal(ks[5], (NUM_HEADS, KEY_DIM, WIDTH), jnp.float32) * 0.05
        bo = jnp.zeros((WIDTH,), jnp.float32)
        proj_w = jax.random.normal(ks[6], (WIDTH, D_MODEL), jnp.float32) * 0.05
        proj_b = jnp.zeros((D_MODEL,), jnp.float32)
        return dict(x=x, conv_w=conv_w, conv_b=conv_b, wq=wq, bq=bq, wk=wk, bk=bk, wv=wv, bv=bv, wo=wo, bo=bo, proj_w=proj_w, proj_b=proj_b)
    _L1_attn_all = _L1_attn_setup()
    _L1_attn_in = {k: v for k, v in _L1_attn_all.items() if k in ('conv_w', 'conv_b', 'wq', 'bq', 'wk', 'bk', 'wv', 'bv', 'wo', 'bo', 'proj_w', 'proj_b')}
    del _L1_attn_all

    def _L1_xattn_setup():
        import jax, jax.numpy as jnp
        import numpy as np
        D_MODEL = 256
        NUM_HEADS = 16
        HEAD_DIM = D_MODEL // NUM_HEADS

        def _fq_sym(x, axis):
            s = jnp.max(jnp.abs(x), axis=axis, keepdims=True) / 127.0
            s = jnp.maximum(s, 1e-08)
            q = jnp.clip(jnp.round(x / s), -127.0, 127.0) * s
            return x + jax.lax.stop_gradient(q - x)

        def _fq_unsigned(x, axis):
            s = jnp.max(x, axis=axis, keepdims=True) / 255.0
            s = jnp.maximum(s, 1e-08)
            q = jnp.clip(jnp.round(x / s), 0.0, 255.0) * s
            return x + jax.lax.stop_gradient(q - x)
        key = jax.random.key(seed)
        ks = jax.random.split(key, 8)
        B, N, M, C = (2, 256, 64, D_MODEL)
        return {'x': jax.random.normal(ks[0], (B, N, C), jnp.float32), 'cond': jax.random.normal(ks[1], (B, M, C), jnp.float32), 'Wq': jax.random.normal(ks[2], (C, C), jnp.float32) * 0.02, 'bq': jnp.zeros((C,), jnp.float32), 'Wkv': jax.random.normal(ks[3], (C, 2 * C), jnp.float32) * 0.02, 'bkv': jnp.zeros((2 * C,), jnp.float32), 'Wp': jax.random.normal(ks[4], (C, C), jnp.float32) * 0.02, 'bp': jnp.zeros((C,), jnp.float32)}
    _L1_xattn_all = _L1_xattn_setup()
    _L1_xattn_in = {k: v for k, v in _L1_xattn_all.items() if k in ('Wq', 'bq', 'Wkv', 'bkv', 'Wp', 'bp')}
    del _L1_xattn_all

    def _L1_ffn_setup():
        import jax, jax.numpy as jnp
        import numpy as np
        B, S, H = (4, 256, 256)
        I, E, K = (176, 16, 2)

        def _swiglu(x, a, b, c):
            return jax.nn.silu(x @ a.T) * (x @ b.T) @ c.T
        key = jax.random.key(seed)
        ks = jax.random.split(key, 8)
        sc = 0.02
        return {'hidden_states': jax.random.normal(ks[0], (B, S, H), jnp.float32), 'gate_w': jax.random.normal(ks[1], (E, H), jnp.float32) * sc, 'bias': jnp.zeros((E,), jnp.float32), 'shared_w1': jax.random.normal(ks[2], (I, H), jnp.float32) * sc, 'shared_w3': jax.random.normal(ks[3], (I, H), jnp.float32) * sc, 'shared_w2': jax.random.normal(ks[4], (H, I), jnp.float32) * sc, 'w1': jax.random.normal(ks[5], (E, I, H), jnp.float32) * sc, 'w3': jax.random.normal(ks[6], (E, I, H), jnp.float32) * sc, 'w2': jax.random.normal(ks[7], (E, H, I), jnp.float32) * sc}
    _L1_ffn_all = _L1_ffn_setup()
    _L1_ffn_in = {k: v for k, v in _L1_ffn_all.items() if k in ('gate_w', 'bias', 'shared_w1', 'shared_w3', 'shared_w2', 'w1', 'w3', 'w2')}
    del _L1_ffn_all
    return {'x': x, 'itok_BxS_13_99985': itok_BxS_13_99985, 'ctx_2048': ctx_2048, 'L0_attn_w_qkv': _L0_attn_in['w_qkv'], 'L0_attn_w_out': _L0_attn_in['w_out'], 'L0_attn_decay_param': _L0_attn_in['decay_param'], 'L0_ffn_W_up': _L0_ffn_in['W_up'], 'L0_ffn_b_up': _L0_ffn_in['b_up'], 'L0_ffn_W_down': _L0_ffn_in['W_down'], 'L0_ffn_b_down': _L0_ffn_in['b_down'], 'L0_ffn_W_q': _L0_ffn_in['W_q'], 'L0_ffn_keys': _L0_ffn_in['keys'], 'L0_ffn_down_embed': _L0_ffn_in['down_embed'], 'L0_ffn_up_embed': _L0_ffn_in['up_embed'], 'L1_attn_conv_w': _L1_attn_in['conv_w'], 'L1_attn_conv_b': _L1_attn_in['conv_b'], 'L1_attn_wq': _L1_attn_in['wq'], 'L1_attn_bq': _L1_attn_in['bq'], 'L1_attn_wk': _L1_attn_in['wk'], 'L1_attn_bk': _L1_attn_in['bk'], 'L1_attn_wv': _L1_attn_in['wv'], 'L1_attn_bv': _L1_attn_in['bv'], 'L1_attn_wo': _L1_attn_in['wo'], 'L1_attn_bo': _L1_attn_in['bo'], 'L1_attn_proj_w': _L1_attn_in['proj_w'], 'L1_attn_proj_b': _L1_attn_in['proj_b'], 'L1_xattn_Wq': _L1_xattn_in['Wq'], 'L1_xattn_bq': _L1_xattn_in['bq'], 'L1_xattn_Wkv': _L1_xattn_in['Wkv'], 'L1_xattn_bkv': _L1_xattn_in['bkv'], 'L1_xattn_Wp': _L1_xattn_in['Wp'], 'L1_xattn_bp': _L1_xattn_in['bp'], 'L1_ffn_gate_w': _L1_ffn_in['gate_w'], 'L1_ffn_bias': _L1_ffn_in['bias'], 'L1_ffn_shared_w1': _L1_ffn_in['shared_w1'], 'L1_ffn_shared_w3': _L1_ffn_in['shared_w3'], 'L1_ffn_shared_w2': _L1_ffn_in['shared_w2'], 'L1_ffn_w1': _L1_ffn_in['w1'], 'L1_ffn_w3': _L1_ffn_in['w3'], 'L1_ffn_w2': _L1_ffn_in['w2']}

def reference(x, itok_BxS_13_99985, ctx_2048, L0_attn_w_qkv, L0_attn_w_out, L0_attn_decay_param, L0_ffn_W_up, L0_ffn_b_up, L0_ffn_W_down, L0_ffn_b_down, L0_ffn_W_q, L0_ffn_keys, L0_ffn_down_embed, L0_ffn_up_embed, L1_attn_conv_w, L1_attn_conv_b, L1_attn_wq, L1_attn_bq, L1_attn_wk, L1_attn_bk, L1_attn_wv, L1_attn_bv, L1_attn_wo, L1_attn_bo, L1_attn_proj_w, L1_attn_proj_b, L1_xattn_Wq, L1_xattn_bq, L1_xattn_Wkv, L1_xattn_bkv, L1_xattn_Wp, L1_xattn_bp, L1_ffn_gate_w, L1_ffn_bias, L1_ffn_shared_w1, L1_ffn_shared_w3, L1_ffn_shared_w2, L1_ffn_w1, L1_ffn_w3, L1_ffn_w2):
    import jax
    import jax.numpy as jnp

    def _L0_attn_ref(x, w_qkv, w_out, decay_param):
        import jax, jax.numpy as jnp
        import numpy as np
        H = 16
        EPS_DEN = 1e-06

        def _decay_scan(x, decay, init):
            xT = jnp.moveaxis(x, 2, 0)

            def step(s, xt):
                s = decay * s + xt
                return (s, s)
            _, ys = jax.lax.scan(step, init, xT)
            return jnp.moveaxis(ys, 0, 2)

        def _phi(z):
            return jax.nn.elu(z) + 1.0

        def _reference_tuple_inner(x, w_qkv, w_out, decay_param):
            B, T, Hid = x.shape
            D = Hid // H
            qkv = x @ w_qkv
            q, k, v = jnp.split(qkv, 3, axis=-1)

            def to_bhtd(t):
                return t.reshape(B, T, H, D).transpose(0, 2, 1, 3)
            q = _phi(to_bhtd(q))
            k = _phi(to_bhtd(k))
            v = to_bhtd(v)
            decay = jax.nn.sigmoid(decay_param).reshape(1, H, 1)
            init = jnp.zeros((B, H, D), dtype=x.dtype)
            running_kv = _decay_scan(k * v, decay, init)
            running_ksum = _decay_scan(k, decay, init)
            den = jnp.clip(jnp.sum(q * running_ksum, axis=-1, keepdims=True), EPS_DEN, None)
            out = q * running_kv / den
            out = out.transpose(0, 2, 1, 3).reshape(B, T, Hid) @ w_out
            new_kv = running_kv[:, :, -1, :]
            new_ksum = running_ksum[:, :, -1, :]
            return (out, new_kv, new_ksum)
        return _reference_tuple_inner(x, w_qkv, w_out, decay_param)[0]

    def _L0_xattn_ref(hidden_states, token_ids, Wg, Wu, Wd):
        import jax, jax.numpy as jnp
        import numpy as np
        B, S, D = (4, 512, 256)
        E = 4
        F = 1024 // E
        VOCAB = 12500
        tokens_per_expert = VOCAB // E
        tid = jnp.clip(token_ids, 0, VOCAB - 1)
        expert_ids = jnp.minimum(tid // tokens_per_expert, E - 1)
        out = jnp.zeros_like(hidden_states)
        for e in range(E):
            g = jax.nn.silu(jnp.einsum('bsd,fd->bsf', hidden_states, Wg[e]))
            u = jnp.einsum('bsd,fd->bsf', hidden_states, Wu[e])
            y = jnp.einsum('bsf,df->bsd', g * u, Wd[e])
            out = jnp.where((expert_ids == e)[..., None], y, out)
        return out

    def _L0_ffn_ref(hidden_states, W_up, b_up, W_down, b_down, W_q, keys, down_embed, up_embed):
        import jax, jax.numpy as jnp
        import numpy as np
        from jax import lax
        D_MODEL = 256
        D_CROSS = 1024
        D_RETR = 128
        D_PRIV = 128
        N_EXPERTS = 2048
        N_HEADS = 8
        K_PER_HEAD = 8
        NUM_KEYS = int(np.sqrt(N_EXPERTS))
        BATCH, SEQ = (2, 256)
        b, t, _ = hidden_states.shape
        act = jax.nn.silu
        h = act(jnp.einsum('btd,cd->btc', hidden_states, W_up) + b_up)
        h = jnp.einsum('btc,pc->btp', h, W_down) + b_down
        q = jnp.einsum('btp,rp->btr', h, W_q)
        q = q.reshape(b, t, 2, N_HEADS, D_RETR // 2).transpose(2, 0, 1, 3, 4)
        sim = jnp.einsum('pbthn,hkpn->pbthk', q, keys)
        scores, idx = lax.top_k(sim, K_PER_HEAD)
        sx, sy = (scores[0], scores[1])
        ix, iy = (idx[0], idx[1])
        all_scores = (sx[..., :, None] + sy[..., None, :]).reshape(b, t, N_HEADS, K_PER_HEAD * K_PER_HEAD)
        all_indices = (ix[..., :, None] * NUM_KEYS + iy[..., None, :]).reshape(b, t, N_HEADS, K_PER_HEAD * K_PER_HEAD)
        sc, pk = lax.top_k(all_scores, K_PER_HEAD)
        indices = jnp.take_along_axis(all_indices, pk, axis=-1)
        de = down_embed[indices]
        ue = up_embed[indices]
        z = jnp.einsum('btd,bthkd->bthk', h, de)
        z = act(z * jax.nn.softmax(sc, axis=-1))
        out = jnp.einsum('bthk,bthkd->btd', z, ue)
        return out

    def _L1_attn_ref(x, conv_w, conv_b, wq, bq, wk, bk, wv, bv, wo, bo, proj_w, proj_b):
        import jax, jax.numpy as jnp
        import numpy as np
        from jax import lax
        BLOCKS = 16
        NUM_HEADS = 8
        KEY_DIM = 64
        WIDTH = 64
        D_MODEL = 256

        def _forward(x, conv_w, conv_b, wq, bq, wk, bk, wv, bv, wo, bo, proj_w, proj_b):
            N, T, D = x.shape
            xp = jnp.pad(x, ((0, 0), (2, 0), (0, 0)))
            qkv = lax.conv_general_dilated(xp, conv_w, window_strides=(1,), padding='VALID', dimension_numbers=('NWC', 'WIO', 'NWC')) + conv_b
            q, k, v = jnp.split(qkv, 3, axis=-1)
            block_len = T // BLOCKS
            qb = q.reshape(N * BLOCKS, block_len, WIDTH)
            kb = k.reshape(N * BLOCKS, block_len, WIDTH)
            vb = v.reshape(N * BLOCKS, block_len, WIDTH)
            qh = jnp.einsum('bsd,dhk->bshk', qb, wq) + bq
            kh = jnp.einsum('bsd,dhk->bshk', kb, wk) + bk
            vh = jnp.einsum('bsd,dhk->bshk', vb, wv) + bv
            scale = 1.0 / jnp.sqrt(jnp.asarray(KEY_DIM, qh.dtype))
            scores = jnp.einsum('bqhk,bshk->bhqs', qh * scale, kh)
            causal = jnp.tril(jnp.ones((block_len, block_len), bool))
            scores = jnp.where(causal[None, None], scores, jnp.asarray(-1000000000.0, scores.dtype))
            attn = jax.nn.softmax(scores, axis=-1)
            ctx = jnp.einsum('bhqs,bshk->bqhk', attn, vh)
            mha_out = jnp.einsum('bqhk,hko->bqo', ctx, wo) + bo
            mha_out = mha_out.reshape(N, T, WIDTH)
            out = mha_out @ proj_w + proj_b
            return out
        return _forward(x, conv_w, conv_b, wq, bq, wk, bk, wv, bv, wo, bo, proj_w, proj_b)

    def _L1_xattn_ref(x, cond, Wq, bq, Wkv, bkv, Wp, bp):
        import jax, jax.numpy as jnp
        import numpy as np
        D_MODEL = 256
        NUM_HEADS = 16
        HEAD_DIM = D_MODEL // NUM_HEADS

        def _fq_sym(x, axis):
            s = jnp.max(jnp.abs(x), axis=axis, keepdims=True) / 127.0
            s = jnp.maximum(s, 1e-08)
            q = jnp.clip(jnp.round(x / s), -127.0, 127.0) * s
            return x + jax.lax.stop_gradient(q - x)

        def _fq_unsigned(x, axis):
            s = jnp.max(x, axis=axis, keepdims=True) / 255.0
            s = jnp.maximum(s, 1e-08)
            q = jnp.clip(jnp.round(x / s), 0.0, 255.0) * s
            return x + jax.lax.stop_gradient(q - x)
        B, N, C = x.shape
        H, hd = (NUM_HEADS, HEAD_DIM)
        q = (x @ Wq + bq).reshape(1, B * N, H, hd)
        kv = (cond @ Wkv + bkv).reshape(1, -1, 2, H, hd)
        k, v = (kv[:, :, 0], kv[:, :, 1])
        scale = 1.0 / np.sqrt(hd).astype(np.float32)
        q = jnp.transpose(q * scale, (0, 2, 1, 3))
        k = jnp.transpose(k, (0, 2, 1, 3))
        v = jnp.transpose(v, (0, 2, 1, 3))
        q = _fq_sym(q, axis=-1)
        k = _fq_sym(k, axis=-1)
        v = _fq_sym(v, axis=2)
        attn = jnp.einsum('bhqd,bhkd->bhqk', q, k)
        attn = jax.nn.softmax(attn.astype(jnp.float32), axis=-1)
        attn = _fq_unsigned(attn, axis=-1)
        out = jnp.einsum('bhqk,bhkd->bhqd', attn, v)
        out = jnp.transpose(out, (0, 2, 1, 3)).reshape(B, N, C)
        return out @ Wp + bp

    def _L1_ffn_ref(hidden_states, gate_w, bias, shared_w1, shared_w3, shared_w2, w1, w3, w2):
        import jax, jax.numpy as jnp
        import numpy as np
        B, S, H = (4, 256, 256)
        I, E, K = (176, 16, 2)

        def _swiglu(x, a, b, c):
            return jax.nn.silu(x @ a.T) * (x @ b.T) @ c.T
        orig_shape = hidden_states.shape
        x = hidden_states.reshape(-1, orig_shape[-1])
        T = x.shape[0]
        shared_output = _swiglu(x, shared_w1, shared_w3, shared_w2)
        logits = x @ gate_w.T
        scores = jax.nn.sigmoid(logits)
        routing_scores = scores + bias
        _, topk_idx = jax.lax.top_k(routing_scores, K)
        sel = jnp.take_along_axis(scores, topk_idx, axis=1)
        gating = sel / sel.sum(axis=-1, keepdims=True)
        combine = jnp.zeros((T, E), x.dtype).at[jnp.arange(T)[:, None], topk_idx].add(gating)
        routed_output = jnp.zeros_like(x)
        for e in range(E):
            y = _swiglu(x, w1[e], w3[e], w2[e])
            routed_output = routed_output + combine[:, e:e + 1] * y
        return (shared_output + routed_output).reshape(orig_shape)
    x = x + _L0_attn_ref(_layernorm(x, axis=-1), L0_attn_w_qkv, L0_attn_w_out, L0_attn_decay_param)
    x = x + _L0_xattn_ref(_layernorm(x, axis=-1), itok_BxS_13_99985, ctx_2048, ctx_2048, ctx_2048)
    x = x + _L0_ffn_ref(_layernorm(x, axis=-1), L0_ffn_W_up, L0_ffn_b_up, L0_ffn_W_down, L0_ffn_b_down, L0_ffn_W_q, L0_ffn_keys, L0_ffn_down_embed, L0_ffn_up_embed)
    x = x + _L1_attn_ref(_layernorm(x, axis=-1), L1_attn_conv_w, L1_attn_conv_b, L1_attn_wq, L1_attn_bq, L1_attn_wk, L1_attn_bk, L1_attn_wv, L1_attn_bv, L1_attn_wo, L1_attn_bo, L1_attn_proj_w, L1_attn_proj_b)
    x = x + _L1_xattn_ref(_layernorm(x, axis=-1), ctx_2048, L1_xattn_Wq, L1_xattn_bq, L1_xattn_Wkv, L1_xattn_bkv, L1_xattn_Wp, L1_xattn_bp)
    x = x + _L1_ffn_ref(_layernorm(x, axis=-1), L1_ffn_gate_w, L1_ffn_bias, L1_ffn_shared_w1, L1_ffn_shared_w3, L1_ffn_shared_w2, L1_ffn_w1, L1_ffn_w3, L1_ffn_w2)
    return x

_drawn_inputs = setup_inputs


def setup_inputs(seed=0):
    import zlib

    import numpy as np

    out = dict(_drawn_inputs(seed))
    spreads = {'L0_attn_decay_param': (0.949999988079071, 0.6),
     'L0_ffn_b_up': (0.0, 0.8),
     'L0_ffn_b_down': (0.0, 0.8),
     'L1_attn_conv_b': (0.0, 0.523),
     'L1_attn_bq': (0.0, 2.0),
     'L1_attn_bk': (0.0, 2.0),
     'L1_attn_bv': (0.0, 0.1),
     'L1_attn_bo': (0.0, 0.389),
     'L1_attn_proj_b': (0.0, 0.1),
     'L1_xattn_bq': (0.0, 2.0),
     'L1_xattn_bkv': (0.0, 0.276),
     'L1_xattn_bp': (0.0, 0.1),
     'L1_ffn_bias': (0.0, 0.8)}
    factors = {'L0_attn_w_qkv': 8.0,
     'L0_attn_w_out': 8.0,
     'L0_ffn_W_up': 8.0,
     'L0_ffn_W_down': 8.0,
     'L0_ffn_W_q': 8.0,
     'L0_ffn_keys': 8.0,
     'L0_ffn_down_embed': 8.0,
     'L0_ffn_up_embed': 8.0,
     'L1_attn_wq': 8.0,
     'L1_attn_wk': 8.0,
     'L1_xattn_Wq': 64.0,
     'L1_xattn_Wkv': 64.0,
     'L1_ffn_gate_w': 6.805,
     'L1_ffn_shared_w1': 4.103,
     'L1_ffn_shared_w3': 4.064,
     'L1_ffn_shared_w2': 4.065,
     'L1_ffn_w1': 5.848,
     'L1_ffn_w3': 5.732,
     'L1_ffn_w2': 5.754}
    for name, (base, spread) in spreads.items():
        noise = np.random.default_rng([zlib.crc32(name.encode()), seed]).standard_normal(out[name].shape)
        drawn = base * np.exp(spread * noise) if base else spread * noise
        out[name] = jnp.asarray(drawn.astype(out[name].dtype))
    for name, factor in factors.items():
        out[name] = (out[name] * factor).astype(out[name].dtype)
    return out
```

```python
from contextlib import ExitStack

import numpy as np
import concourse.bass as bass
from concourse import mybir

F32 = mybir.dt.float32
BF16 = mybir.dt.bfloat16
I32 = mybir.dt.int32
I16 = mybir.dt.int16
U32 = mybir.dt.uint32
ALU = mybir.AluOpType
ACT = mybir.ActivationFunctionType
AX = mybir.AxisListType

P = 128
B, T, D = 4, 256, 256
N = B * T
NT = N // P
DC = D // P
HALF = 512
NH = N // HALF
LN_EPS = 1e-5
ROUND = 12582912.0


class Buffers:
    pass


class Chain:

    def __init__(self, engine, semaphore):
        self.engine, self.semaphore, self.count = engine, semaphore, 0

    def step(self, instruction):
        self.count += 1
        instruction.then_inc(self.semaphore, 1)
        self.engine.wait_ge(self.semaphore, self.count)


def scope(nc, ctx, prefix):
    def sb(name, shape, dt=F32):
        return ctx.enter_context(nc.sbuf_tensor(prefix + name, shape, dt))

    def ps(name, shape, dt=F32):
        return ctx.enter_context(nc.psum_tensor(prefix + name, shape, dt))

    def sem(name):
        return ctx.enter_context(nc.semaphore(prefix + name))
    return sb, ps, sem





def norm_buffers(sb, ps, sem):
    ln = Buffers()
    ln.stats = sb("ln_stats", [P, NT, 6])
    ln.mv = sb("ln_mv", [P, NT, 2])
    ln.rstd = sb("ln_rstd", [P, NT])
    ln.minus_half = sb("ln_minus_half", [P, NT])
    ln.xn = sb("ln_xn", [P, NT, D])
    ln.turned = ps("ln_turned", [P, 2, HALF])
    ln.var_ready = sem("ln_var_ready")
    ln.rstd_ready = sem("ln_rstd_ready")
    ln.normed = sem("ln_normed")
    ln.turned_ready = sem("ln_turned_ready")
    ln.copied = sem("ln_copied")
    return ln


def norm_vector(nc, eng, ln, x, chain):
    for t in range(NT):
        last = nc.vector.bn_stats(ln.stats[:, t, :], x[:, t, :])
    chain.step(last)
    for t in range(NT):
        last = nc.vector.bn_aggr(ln.mv[:, t, :], ln.stats[:, t, :])
    chain.step(last)
    nc.vector.memset(ln.minus_half[:, :], -0.5)
    nc.vector.tensor_scalar(ln.rstd[:, :], ln.mv[:, :, 1], LN_EPS, None, ALU.add).then_inc(ln.var_ready, 1)
    eng.wait_ge(ln.rstd_ready, 1)
    for t in range(NT):
        nc.vector.tensor_scalar(ln.xn[:, t, :], x[:, t, :], ln.mv[:, t, 0:1], ln.rstd[:, t:t + 1],
                                ALU.subtract, ALU.mult).then_inc(ln.normed, 1)


def norm_pool(nc, pool, ln):
    pool.wait_ge(ln.var_ready, 1)
    nc.gpsimd.tensor_tensor(ln.rstd[:, :], ln.rstd[:, :], ln.minus_half[:, :], ALU.pow).then_inc(ln.rstd_ready, 1)


def norm_tensor(nc, pe, ln, ident):
    for t in range(NT):
        pe.wait_ge(ln.normed, t + 1)
        if t >= 2:
            pe.wait_ge(ln.copied, t - 1)
        for c in range(DC):
            last = nc.tensor.transpose(ln.turned[:, t % 2, c * P:(c + 1) * P], ln.xn[:, t, c * P:(c + 1) * P], ident[:, :])
        last.then_inc(ln.turned_ready, 1)


def norm_scalar(nc, act, ln, place):
    for t in range(NT):
        act.wait_ge(ln.turned_ready, t + 1)
        nc.scalar.copy(place(t), ln.turned[:, t % 2, 0:D].rearrange("p (c n) -> p c n", c=DC)).then_inc(ln.copied, 1)



def start_stage(nc, x, ident, x_dram):
    with ExitStack() as ctx:
        sb, ps, sem = scope(nc, ctx, "st_")
        loaded, zeroed = sem("loaded"), sem("zeroed")
        block = ctx.enter_context(nc.Block())

        @block.sync
        def _(sp):
            sp.dma_start(x[:, :, :], x_dram).then_inc(loaded, 16)
            sp.wait_ge(loaded, 16)

        @block.gpsimd
        def _(pool):
            nc.gpsimd.memset(ident[:, :], 0.0).then_inc(zeroed, 1)
            pool.wait_ge(zeroed, 1)
            nc.gpsimd.affine_select(out=ident[:, :], in_=ident[:, :], compare_op=ALU.not_equal, fill=1.0,
                                    base=0, pattern=[[-1, P]], channel_multiplier=1).then_inc(zeroed, 1)
            pool.wait_ge(zeroed, 2)



HEADS0 = 16
HD0 = D // HEADS0
DEN_LEAST = 1e-6
KEY, VALUE, QUERY = range(3)


def linear_attention(nc, sh, w_qkv_dram, w_out_dram, decay_dram):
    x, xT, ident = sh.x, sh.xT, sh.ident
    with ExitStack() as ctx:
        sb, ps, sem = scope(nc, ctx, "a0_")
        ln = norm_buffers(sb, ps, sem)
        w_qkv, w_out = sb("w_qkv", [P, DC, 3 * D]), sb("w_out", [P, DC, D])
        decay = sb("decay", [P, DC])
        gain = sb("gain", [P, DC, N])
        same_head = sb("same_head", [P, P])
        exps, relus = sb("exps", [P, 4, HALF]), sb("relus", [P, 4, HALF])
        q, k, kv = sb("q", [P, DC, N]), sb("k", [P, DC, N]), sb("kv", [P, DC, N])
        run_k, run_kv = sb("run_k", [P, DC, N]), sb("run_kv", [P, DC, N])
        proj = ps("proj", [P, 4, HALF])
        sums = ps("sums", [P, 2, HALF])
        out = proj
        loaded, dve_steps, consts = sem("loaded"), sem("dve_steps"), sem("consts")
        decay_exp, projected = sem("decay_exp"), sem("projected")
        phi_parts, phi_done, kv_done = sem("phi_parts"), sem("phi_done"), sem("kv_done")
        scanned, qk_ready, sums_ready, sums_used = sem("scanned"), sem("qk_ready"), sem("sums_ready"), sem("sums_used")
        qkv_ready, heads_ready = sem("qkv_ready"), sem("heads_ready")
        out_ready, out_added = sem("out_ready"), sem("out_added")
        groups = [(c, kind, h) for c in range(DC) for kind in (KEY, VALUE, QUERY) for h in range(NH)]
        column = {KEY: D, VALUE: 2 * D, QUERY: 0}

        def phis(n):
            return sum(kind != VALUE for _, kind, _ in groups[:n])

        block = ctx.enter_context(nc.Block())

        @block.sync
        def _(sp):
            sp.dma_start(w_qkv[:, :, :], w_qkv_dram).then_inc(loaded, 16)
            sp.dma_start(decay[:, :], decay_dram).then_inc(loaded, 16)
            sp.dma_start(w_out[:, :, :], w_out_dram).then_inc(loaded, 16)

        @block.gpsimd
        def _(pool):
            norm_pool(nc, pool, ln)
            view = same_head[:, :].rearrange("p (h d) -> p h d", d=HD0)
            nc.gpsimd.memset(same_head[:, :], 1.0).then_inc(consts, 1)
            pool.wait_ge(consts, 1)
            nc.gpsimd.affine_select(out=view, in_=view, compare_op=ALU.is_ge, fill=0.0, base=0,
                                    pattern=[[-HD0, P // HD0], [0, HD0]], channel_multiplier=1).then_inc(consts, 1)
            pool.wait_ge(consts, 2)
            nc.gpsimd.affine_select(out=view, in_=view, compare_op=ALU.is_ge, fill=0.0, base=HD0 - 1,
                                    pattern=[[HD0, P // HD0], [0, HD0]], channel_multiplier=-1).then_inc(consts, 1)
            nc.gpsimd.memset(gain[:, :, :], 1.0).then_inc(consts, 1)
            pool.wait_ge(consts, 4)
            nc.gpsimd.memset(gain[:, :, :].rearrange("p c (b t) -> p (c b) t", t=T)[:, :, 0:1], 0.0).then_inc(consts, 1)
            for c in range(DC):
                pool.wait_ge(scanned, c + 1)
                nc.gpsimd.tensor_tensor(kv[:, c, :], q[:, c, :], run_kv[:, c, :], ALU.mult).then_inc(qkv_ready, 1)

        @block.tensor
        def _(pe):
            norm_tensor(nc, pe, ln, ident)
            pe.wait_ge(loaded, 48)
            pe.wait_ge(ln.copied, NT)
            for i, (c, kind, h) in enumerate(groups):
                if i >= 4:
                    pe.wait_ge(phi_parts, phis(i - 3))
                    if i - 3 > phis(i - 3):
                        pe.wait_ge(kv_done, i - 3 - phis(i - 3))
                for d in range(DC):
                    f = column[kind] + c * P
                    last = nc.tensor.matmul(proj[:, i % 4, :], w_qkv[:, d, f:f + P],
                                            xT[:, d, h * HALF:(h + 1) * HALF], start=(d == 0), stop=(d == DC - 1))
                last.then_inc(projected, 1)
            pe.wait_ge(consts, 3)
            for c in range(DC):
                pe.wait_ge(qk_ready, c + 1)
                for h in range(NH):
                    i = c * NH + h
                    if i >= 2:
                        pe.wait_ge(sums_used, i - 1)
                    nc.tensor.matmul(sums[:, i % 2, :], same_head[:, :], k[:, c, h * HALF:(h + 1) * HALF],
                                     start=True, stop=True).then_inc(sums_ready, 1)
            pe.wait_ge(heads_ready, DC)
            for t in range(NT):
                if t >= 2:
                    pe.wait_ge(out_added, t - 1)
                for c in range(DC):
                    last = nc.tensor.matmul(out[:, t % 2, 0:D], q[:, c, t * P:(t + 1) * P], w_out[:, c, :],
                                            start=(c == 0), stop=(c == DC - 1))
                last.then_inc(out_ready, 1)

        @block.scalar
        def _(act):
            norm_scalar(nc, act, ln, lambda t: xT[:, :, t * P:(t + 1) * P])
            act.wait_ge(loaded, 48)
            nc.scalar.activation(decay[:, :], decay[:, :], ACT.Exp, scale=-1.0).then_inc(decay_exp, 1)
            n = 0
            for i, (c, kind, h) in enumerate(groups):
                if kind == VALUE:
                    continue
                act.wait_ge(projected, i + 1)
                if n >= 4:
                    act.wait_ge(phi_done, n - 3)
                nc.scalar.activation(exps[:, n % 4, :], proj[:, i % 4, :], ACT.Exp)
                nc.scalar.activation(relus[:, n % 4, :], proj[:, i % 4, :], ACT.Relu).then_inc(phi_parts, 1)
                n += 1

        @block.vector
        def _(dve):
            chain = Chain(dve, dve_steps)
            norm_vector(nc, dve, ln, x, chain)
            dve.wait_ge(decay_exp, 1)
            chain.step(nc.vector.tensor_scalar(decay[:, :], decay[:, :], 1.0, None, ALU.add))
            chain.step(nc.vector.reciprocal(decay[:, :], decay[:, :]))
            dve.wait_ge(consts, 5)
            for c in range(DC):
                last = nc.vector.tensor_scalar(gain[:, c, :], gain[:, c, :], decay[:, c:c + 1], None, ALU.mult)
            chain.step(last)
            n = 0
            for i, (c, kind, h) in enumerate(groups):
                at = slice(h * HALF, (h + 1) * HALF)
                if kind == VALUE:
                    dve.wait_ge(projected, i + 1)
                    dve.wait_ge(phi_done, n)
                    nc.vector.tensor_tensor(kv[:, c, at], proj[:, i % 4, :], k[:, c, at], ALU.mult).then_inc(kv_done, 1)
                    continue
                dve.wait_ge(phi_parts, n + 1)
                nc.vector.scalar_tensor_tensor((k if kind == KEY else q)[:, c, at], exps[:, n % 4, :], 1.0,
                                               relus[:, n % 4, :], ALU.min, ALU.add).then_inc(phi_done, 1)
                n += 1
                if kind == QUERY and h == NH - 1:
                    dve.wait_ge(kv_done, NH * (c + 1))
                    dve.wait_ge(phi_done, n)
                    nc.vector.tensor_tensor_scan(run_k[:, c, :], gain[:, c, :], k[:, c, :], 0.0, ALU.mult, ALU.add)
                    chain.step(nc.vector.tensor_tensor_scan(run_kv[:, c, :], gain[:, c, :], kv[:, c, :], 0.0,
                                                            ALU.mult, ALU.add))
                    dve.sem_inc(scanned, 1)
                    nc.vector.tensor_tensor(k[:, c, :], q[:, c, :], run_k[:, c, :], ALU.mult).then_inc(qk_ready, 1)
            for c in range(DC):
                dve.wait_ge(qkv_ready, c + 1)
                dve.wait_ge(qk_ready, c + 1)
                for h in range(NH):
                    i = c * NH + h
                    at = slice(h * HALF, (h + 1) * HALF)
                    dve.wait_ge(sums_ready, i + 1)
                    nc.vector.tensor_scalar(run_k[:, c, at], sums[:, i % 2, :], DEN_LEAST, None, ALU.max).then_inc(sums_used, 1)
                    dve.wait_ge(sums_used, i + 1)
                    chain.step(nc.vector.reciprocal(run_k[:, c, at], run_k[:, c, at]))
                    last = nc.vector.tensor_tensor(q[:, c, at], kv[:, c, at], run_k[:, c, at], ALU.mult)
                last.then_inc(heads_ready, 1)
            for t in range(NT):
                dve.wait_ge(out_ready, t + 1)
                nc.vector.tensor_tensor(x[:, t, :], x[:, t, :], out[:, t % 2, 0:D], ALU.add).then_inc(out_added, 1)



EXPERTS_T = 4
PER_EXPERT = 12500 // EXPERTS_T


def token_experts(nc, sh, ids_dram, ctxT_dram):
    x, xT, ident, ctxT = sh.x, sh.xT, sh.ident, sh.ctxT
    with ExitStack() as ctx:
        sb, ps, sem = scope(nc, ctx, "m0_")
        ln = norm_buffers(sb, ps, sem)
        ids, idf = sb("ids", [P, N], I32), sb("idf", [P, N])
        mask = sb("mask", [P, EXPERTS_T, N])
        own = sb("own", [P, EXPERTS_T, DC, N])
        hid = sb("hid", [P, EXPERTS_T, DC, N])
        up = ps("up", [P, 4, HALF])
        out = ps("out", [P, 2, HALF])
        loaded, dve_steps, masks_ready, own_ready = sem("loaded"), sem("dve_steps"), sem("masks_ready"), sem("own_ready")
        up_ready, silu_ready, hid_ready, out_ready, out_added = (
            sem("up_ready"), sem("silu_ready"), sem("hid_ready"), sem("out_ready"), sem("out_added"))
        groups = [(e, f, h) for e in range(EXPERTS_T) for f in range(DC) for h in range(NH)]
        block = ctx.enter_context(nc.Block())

        @block.sync
        def _(sp):
            sp.dma_start(ids[:, :], ids_dram.broadcast_to([P, N])).then_inc(loaded, 16)
            sp.dma_start(ctxT[:, :, :], ctxT_dram).then_inc(loaded, 16)

        @block.gpsimd
        def _(pool):
            norm_pool(nc, pool, ln)
            for e in range(EXPERTS_T):
                pool.wait_ge(masks_ready, e + 1)
                pool.wait_ge(ln.copied, NT)
                for c in range(DC):
                    last = nc.gpsimd.tensor_tensor(own[:, e, c, :], xT[:, c, :], mask[:, e, :], ALU.mult)
                last.then_inc(own_ready, 1)

        @block.tensor
        def _(pe):
            norm_tensor(nc, pe, ln, ident)
            pe.wait_ge(loaded, 32)
            for i, (e, f, h) in enumerate(groups):
                pe.wait_ge(own_ready, e + 1)
                if i >= 4:
                    pe.wait_ge(hid_ready, i - 3)
                for d in range(DC):
                    last = nc.tensor.matmul(up[:, i % 4, :], ctxT[:, d, e * D + f * P:e * D + (f + 1) * P],
                                            own[:, e, d, h * HALF:(h + 1) * HALF], start=(d == 0), stop=(d == DC - 1))
                last.then_inc(up_ready, 1)
            pe.wait_ge(hid_ready, len(groups))
            for t in range(NT):
                if t >= 2:
                    pe.wait_ge(out_added, t - 1)
                for e in range(EXPERTS_T):
                    for f in range(DC):
                        last = nc.tensor.matmul(out[:, t % 2, 0:D], hid[:, e, f, t * P:(t + 1) * P],
                                                ctxT[:, f, e * D:(e + 1) * D], start=(e == f == 0),
                                                stop=(e == EXPERTS_T - 1 and f == DC - 1))
                last.then_inc(out_ready, 1)

        @block.scalar
        def _(act):
            norm_scalar(nc, act, ln, lambda t: xT[:, :, t * P:(t + 1) * P])
            for i, (e, f, h) in enumerate(groups):
                act.wait_ge(up_ready, i + 1)
                nc.scalar.activation(hid[:, e, f, h * HALF:(h + 1) * HALF], up[:, i % 4, :], ACT.Silu).then_inc(silu_ready, 1)

        @block.vector
        def _(dve):
            chain = Chain(dve, dve_steps)
            norm_vector(nc, dve, ln, x, chain)
            dve.wait_ge(loaded, 32)
            chain.step(nc.vector.tensor_copy(idf[:, :], ids[:, :]))
            for e in range(EXPERTS_T):
                if e == 0:
                    nc.vector.tensor_scalar(mask[:, e, :], idf[:, :], float(PER_EXPERT), None, ALU.is_lt).then_inc(masks_ready, 1)
                elif e == EXPERTS_T - 1:
                    nc.vector.tensor_scalar(mask[:, e, :], idf[:, :], float(e * PER_EXPERT), None, ALU.is_ge).then_inc(masks_ready, 1)
                else:
                    chain.step(nc.vector.tensor_scalar(mask[:, e, :], idf[:, :], float(e * PER_EXPERT), None, ALU.is_ge))
                    nc.vector.scalar_tensor_tensor(mask[:, e, :], idf[:, :], float((e + 1) * PER_EXPERT), mask[:, e, :],
                                                   ALU.is_lt, ALU.mult).then_inc(masks_ready, 1)
            for i, (e, f, h) in enumerate(groups):
                at = slice(h * HALF, (h + 1) * HALF)
                dve.wait_ge(silu_ready, i + 1)
                nc.vector.tensor_tensor(hid[:, e, f, at], up[:, i % 4, :], hid[:, e, f, at], ALU.mult).then_inc(hid_ready, 1)
            for t in range(NT):
                dve.wait_ge(out_ready, t + 1)
                nc.vector.tensor_tensor(x[:, t, :], x[:, t, :], out[:, t % 2, 0:D], ALU.add).then_inc(out_added, 1)


HEADS_R = 8
TOP = 8
RETR = 64
KEYS = 45
PAIRS = KEYS * KEYS
SIDE = HEADS_R * KEYS
UP = 1024
UC = UP // P
PB = (PAIRS + P - 1) // P
LAST = PAIRS - (PB - 1) * P
UNITS = NT * HEADS_R
BATCH = 4


def retrieval(nc, sh, i):
    with ExitStack() as ctx:
        sb, ps, sem = scope(nc, ctx, "r0_")
        r = Buffers()
        r.hT = sb("hT", [P, N])
        r.to_sims = sb("to_sims", [P, 2 * SIDE])
        r.down = sb("down", [P, PB * P])
        r.up = sb("up", [P, PB, D])
        r.loaded = sem("tables_loaded")
        private_state(nc, sh, r, i)
        weigh_experts(nc, sh, r)


def private_state(nc, sh, r, i):
    x, xT, ident = sh.x, sh.xT, sh.ident
    with ExitStack() as ctx:
        sb, ps, sem = scope(nc, ctx, "r1_")
        ln = norm_buffers(sb, ps, sem)
        w_up, b_up = sb("w_up", [P, DC, UP]), sb("b_up", [P, UC])
        w_down, b_down = sb("w_down", [P, UC, P]), sb("b_down", [P, 1])
        w_q, keys = sb("w_q", [P, UC, P]), sb("keys", [P, UC, 2, KEYS])
        wide = sb("wide", [P, UC, N])
        up = ps("up", [P, 4, HALF])
        low = ps("low", [P, 2, HALF])
        loaded, dve_steps, zeroed, keys_loaded = sem("loaded"), sem("dve_steps"), sem("zeroed"), sem("keys_loaded")
        sims_ready, up_ready, silu_ready, low_ready, done = (
            sem("sims_ready"), sem("up_ready"), sem("silu_ready"), sem("low_ready"), sem("done"))
        copied = sem("copied")
        groups = [(c, h) for c in range(UC) for h in range(NH)]
        block = ctx.enter_context(nc.Block())

        @block.sync
        def _(sp):
            for dst, src in ((w_q[:, :, :], "w_q"), (w_up[:, :, :], "w_up"), (b_up[:, :], "b_up"),
                             (w_down[:, :, :], "w_down"), (b_down[:, :], "b_down")):
                sp.dma_start(dst, i[src]).then_inc(loaded, 16)
            sp.wait_ge(zeroed, 1)
            for j in range(2):
                sp.dma_start(keys[j * RETR:(j + 1) * RETR, :, j, :], i["keys"][j]).then_inc(keys_loaded, 16)
            sp.dma_start(r.down[:, :], i["down"]).then_inc(r.loaded, 16)
            sp.dma_start(r.up[:, :, :], i["up"]).then_inc(r.loaded, 16)

        @block.gpsimd
        def _(pool):
            nc.gpsimd.memset(keys[:, :, :, :], 0.0).then_inc(zeroed, 1)
            norm_pool(nc, pool, ln)

        @block.tensor
        def _(pe):
            pe.wait_ge(loaded, 80)
            pe.wait_ge(keys_loaded, 32)
            for c in range(UC):
                last = nc.tensor.matmul(low[:, c // 4, (c % 4) * 2 * KEYS:(c % 4 + 1) * 2 * KEYS], w_q[:, c, :],
                                        keys[:, c, :, :].rearrange("p j k -> p (j k)"), start=True, stop=True)
            last.then_inc(sims_ready, 1)
            norm_tensor(nc, pe, ln, ident)
            pe.wait_ge(ln.copied, NT)
            for n, (c, h) in enumerate(groups):
                if n >= 4:
                    pe.wait_ge(silu_ready, n - 3)
                for d in range(DC):
                    last = nc.tensor.matmul(up[:, n % 4, :], w_up[:, d, c * P:(c + 1) * P],
                                            xT[:, d, h * HALF:(h + 1) * HALF], start=(d == 0), stop=(d == DC - 1))
                last.then_inc(up_ready, 1)
            pe.wait_ge(silu_ready, len(groups))
            pe.wait_ge(copied, 1)
            for h in range(NH):
                for c in range(UC):
                    last = nc.tensor.matmul(low[:, h, :], w_down[:, c, :], wide[:, c, h * HALF:(h + 1) * HALF],
                                            start=(c == 0), stop=(c == UC - 1))
                last.then_inc(low_ready, 1)

        @block.scalar
        def _(act):
            norm_scalar(nc, act, ln, lambda t: xT[:, :, t * P:(t + 1) * P])
            act.wait_ge(loaded, 80)
            for n, (c, h) in enumerate(groups):
                act.wait_ge(up_ready, n + 1)
                nc.scalar.activation(wide[:, c, h * HALF:(h + 1) * HALF], up[:, n % 4, :], ACT.Silu,
                                     bias=b_up[:, c:c + 1]).then_inc(silu_ready, 1)

        @block.vector
        def _(dve):
            chain = Chain(dve, dve_steps)
            norm_vector(nc, dve, ln, x, chain)
            dve.wait_ge(sims_ready, 1)
            nc.vector.tensor_copy(r.to_sims[:, :].rearrange("p (s n) -> p s n", s=2), low[:, :, 0:SIDE]).then_inc(copied, 1)
            dve.wait_ge(loaded, 80)
            for h in range(NH):
                dve.wait_ge(low_ready, h + 1)
                nc.vector.tensor_scalar(r.hT[:, h * HALF:(h + 1) * HALF], low[:, h, :], b_down[:, 0:1], None,
                                        ALU.add).then_inc(done, 1)


def weigh_experts(nc, sh, r):
    x, ident = sh.x, sh.ident
    with ExitStack() as ctx:
        sb, ps, sem = scope(nc, ctx, "r2_")
        RING = 10
        SUMS = 3
        sims = sb("sims", [P, NT, 2 * SIDE])
        pair_sum = sb("pair_sum", [P, SUMS, PAIRS])
        w = sb("w", [P, RING, PAIRS])
        wT = sb("wT", [P, PB, P])
        best = sb("best", [P, 2, HEADS_R, TOP])
        grid = sb("grid", [P, HEADS_R, TOP * TOP])
        kept = sb("kept", [P, 2, HEADS_R, TOP])
        neg_max = sb("neg_max", [P, 2, HEADS_R])
        below_max = sb("below_max", [P, HEADS_R, TOP])
        kept_exp = sb("kept_exp", [P, HEADS_R, TOP])
        scale = sb("scale", [P, 2, HEADS_R])
        head_sum = ps("head_sum", [P, 4, HALF])
        z = ps("z", [P, 4, HALF])
        dve_steps = sem("dve_steps")
        sims_ready, sims_copied, z_ready = sem("sims_ready"), sem("sims_copied"), sem("z_ready")
        best_ready, kept_ready, scale_ready = sem("best_ready"), sem("kept_ready"), sem("scale_ready")
        summed_pairs, exp_done, masked, weighted, silu_done, summed = (
            sem("summed_pairs"), sem("exp_done"), sem("masked"), sem("weighted"), sem("silu_done"), sem("summed"))
        wT_copied, out_ready, out_added = sem("wT_copied"), sem("out_ready"), sem("out_added")
        block = ctx.enter_context(nc.Block())

        @block.gpsimd
        def _(pool):
            for u in range(UNITS):
                t, h = divmod(u, HEADS_R)
                if h == 0:
                    pool.wait_ge(sims_copied, t + 1)
                if u >= SUMS:
                    pool.wait_ge(masked, u - SUMS + 1)
                a = sims[:, t, h * KEYS:(h + 1) * KEYS].rearrange("p (a o) -> p a o", o=1)
                b = sims[:, t, SIDE + h * KEYS:SIDE + (h + 1) * KEYS].rearrange("p (o b) -> p o b", o=1)
                nc.gpsimd.tensor_tensor(pair_sum[:, u % SUMS, :].rearrange("p (a b) -> p a b", b=KEYS),
                                        a.broadcast_to([P, KEYS, KEYS]), b.broadcast_to([P, KEYS, KEYS]),
                                        ALU.add).then_inc(summed_pairs, 1)

        @block.tensor
        def _(pe):
            pe.wait_ge(r.loaded, 32)

            def projections(t):
                pe.wait_ge(weighted, HEADS_R * t) if t >= 1 else pe.wait_ge(sims_copied, NT)
                for j in range(4):
                    lo, hi = j * HALF, min((j + 1) * HALF, PAIRS)
                    last = nc.tensor.matmul(z[:, j, 0:hi - lo], r.hT[:, t * P:(t + 1) * P], r.down[:, lo:hi],
                                            start=True, stop=True)
                last.then_inc(z_ready, 1)

            def output(t):
                pe.wait_ge(wT_copied, t + 1)
                for b in range(PB):
                    k = P if b < PB - 1 else LAST
                    last = nc.tensor.matmul(head_sum[:, 0, 0:D], wT[0:k, b, :], r.up[0:k, b, :],
                                            start=(b == 0), stop=(b == PB - 1))
                last.then_inc(out_ready, 1)

            for t in range(NT):
                if t >= 2:
                    pe.wait_ge(sims_copied, t - 1)
                for s in range(2):
                    last = nc.tensor.matmul(z[:, t % 2 * 2 + s, 0:SIDE], r.hT[:, t * P:(t + 1) * P],
                                            r.to_sims[:, s * SIDE:(s + 1) * SIDE], start=True, stop=True)
                last.then_inc(sims_ready, 1)
            projections(0)
            for u in range(UNITS):
                t, h = divmod(u, HEADS_R)
                if h == 2 and t + 1 < NT:
                    projections(t + 1)
                pe.wait_ge(silu_done, u + 1)
                if h == 0 and t >= 1:
                    pe.wait_ge(out_added, t)
                for b in range(PB):
                    m = P if b < PB - 1 else LAST
                    last = nc.tensor.matmul(head_sum[0:m, b // 4, (b % 4) * P:(b % 4 + 1) * P],
                                            w[:, u % RING, b * P:b * P + m], ident[:, :],
                                            start=(h == 0 and b % 4 == 0), stop=(h == HEADS_R - 1), skip_group_check=True)
                last.then_inc(summed, 1)
                if h == HEADS_R - 1:
                    output(t)

        @block.scalar
        def _(act):
            def exp_kept(t):
                act.wait_ge(best_ready, t + 1)
                if t >= 1:
                    act.wait_ge(scale_ready, t)
                nc.scalar.activation(kept_exp[:, :, :], below_max[:, :, :], ACT.Exp).then_inc(kept_ready, 1)

            def exps(g):
                for u in range(BATCH * g, BATCH * (g + 1)):
                    t, h = divmod(u, HEADS_R)
                    act.wait_ge(summed_pairs, u + 1)
                    if u >= RING:
                        act.wait_ge(summed, u - RING + 1)
                    nc.scalar.activation(w[:, u % RING, :], pair_sum[:, u % SUMS, :], ACT.Exp,
                                         bias=neg_max[:, t % 2, h:h + 1]).then_inc(exp_done, 1)

            def silus(g):
                for u in range(BATCH * g, BATCH * (g + 1)):
                    act.wait_ge(weighted, u + 1)
                    nc.scalar.activation(w[:, u % RING, :], w[:, u % RING, :], ACT.Silu).then_inc(silu_done, 1)

            for t in range(NT):
                act.wait_ge(sims_ready, t + 1)
                nc.scalar.copy(sims[:, t, :].rearrange("p (s n) -> p s n", s=2),
                               z[:, t % 2 * 2:t % 2 * 2 + 2, 0:SIDE]).then_inc(sims_copied, 1)
            exp_kept(0)
            exps(0)
            exps(1)
            for t in range(NT):
                silus(2 * t)
                if t + 1 < NT:
                    exp_kept(t + 1)
                    exps(2 * t + 2)
                silus(2 * t + 1)
                if t + 1 < NT:
                    exps(2 * t + 3)
                act.wait_ge(summed, HEADS_R * (t + 1))
                if t >= 1:
                    act.wait_ge(out_ready, t)
                nc.scalar.copy(wT[:, 0:PB - 1, :].rearrange("p b n -> p (b n)"),
                               head_sum[:, :, :].rearrange("p a b -> p (a b)")[:, 0:(PB - 1) * P])
                nc.scalar.copy(wT[0:LAST, PB - 1, :], head_sum[0:LAST, 3, 3 * P:4 * P]).then_inc(wT_copied, 1)

        @block.vector
        def _(dve):
            chain = Chain(dve, dve_steps)

            def choose(t):
                dve.wait_ge(sims_copied, t + 1)
                for s in range(2):
                    for h in range(HEADS_R):
                        at = s * SIDE + h * KEYS
                        last = nc.vector.max(best[:, s, h, :], sims[:, t, at:at + KEYS])
                chain.step(last)
                a = best[:, 0, :, :].rearrange("p h (a o) -> p h a o", o=1).broadcast_to([P, HEADS_R, TOP, TOP])
                b = best[:, 1, :, :].rearrange("p h (o b) -> p h o b", o=1).broadcast_to([P, HEADS_R, TOP, TOP])
                chain.step(nc.vector.tensor_tensor(grid[:, :, :].rearrange("p h (a b) -> p h a b", b=TOP), a, b, ALU.add))
                for h in range(HEADS_R):
                    last = nc.vector.max(kept[:, t % 2, h, :], grid[:, h, :])
                chain.step(last)
                if t >= 1:
                    dve.wait_ge(kept_ready, t)
                nc.vector.tensor_scalar(neg_max[:, t % 2, :], kept[:, t % 2, :, 0], -1.0, None, ALU.mult)
                top = kept[:, t % 2, :, 0:1].broadcast_to([P, HEADS_R, TOP])
                nc.vector.tensor_tensor(below_max[:, :, :], kept[:, t % 2, :, :], top, ALU.subtract).then_inc(best_ready, 1)

            def scales(t):
                dve.wait_ge(kept_ready, t + 1)
                chain.step(nc.vector.tensor_reduce(scale[:, t % 2, :], kept_exp[:, :, :], AX.X, ALU.add))
                chain.step(nc.vector.reciprocal(scale[:, t % 2, :], scale[:, t % 2, :]))
                dve.sem_inc(scale_ready, 1)

            def mask(u):
                t, h = divmod(u, HEADS_R)
                dve.wait_ge(exp_done, u + 1)
                nc.vector.scalar_tensor_tensor(w[:, u % RING, :], pair_sum[:, u % SUMS, :], kept[:, t % 2, h, TOP - 1:TOP],
                                               w[:, u % RING, :], ALU.is_ge, ALU.mult).then_inc(masked, 1)

            def weigh(u):
                t, h = divmod(u, HEADS_R)
                if h == 0:
                    scales(t)
                    dve.wait_ge(z_ready, t + 1)
                dve.wait_ge(masked, u + 1)
                nc.vector.scalar_tensor_tensor(w[:, u % RING, :], w[:, u % RING, :], scale[:, t % 2, h:h + 1],
                                               z[:, :, :].rearrange("p a b -> p (a b)")[:, 0:PAIRS],
                                               ALU.mult, ALU.mult).then_inc(weighted, 1)

            def residual(t):
                dve.wait_ge(out_ready, t + 1)
                nc.vector.tensor_tensor(x[:, t, :], x[:, t, :], head_sum[:, 0, 0:D], ALU.add).then_inc(out_added, 1)

            choose(0)
            for u in range(UNITS):
                t, h = divmod(u, HEADS_R)
                mask(u)
                if u >= 1:
                    weigh(u - 1)
                if h == 1 and t + 1 < NT:
                    choose(t + 1)
                if h == 6 and t >= 1:
                    residual(t - 1)
            weigh(UNITS - 1)
            residual(NT - 1)


TAPS = 3
WIDTH = 64
HEADS_B = 8
HD_B = 64
BLOCK = T // 16
WIDE_B = HEADS_B * HD_B
CB = WIDE_B // P
MASKED = -1e9


def block_attention(nc, sh, i):
    with ExitStack() as ctx:
        sb, ps, sem = scope(nc, ctx, "b0_")
        s = Buffers()
        s.qh = sb("qh", [P, CB, N])
        s.kh = sb("kh", [P, CB, N])
        s.vh = sb("vh", [P, NT, WIDE_B])
        s.w_o = sb("w_o", [P, CB, WIDTH])
        s.b_o = sb("b_o", [WIDTH, 1])
        s.proj = sb("proj", [WIDTH + 1, D])
        s.mask = sb("mask", [P, P])
        s.loaded = sem("out_loaded")
        convolve(nc, sh, s, i)
        attend_in_blocks(nc, sh, s)


def convolve(nc, sh, s, i):
    x, ident = sh.x, sh.ident
    with ExitStack() as ctx:
        sb, ps, sem = scope(nc, ctx, "b1_")
        ln = norm_buffers(sb, ps, sem)
        PADDED = T + TAPS - 1
        padded = sb("padded", [P, DC, B, PADDED])
        conv_w, conv_b = sb("conv_w", [P, TAPS, DC, 3 * WIDTH]), sb("conv_b", [P, 2])
        w_qk, b_q, b_k = sb("w_qk", [P, WIDE_B]), sb("b_q", [P, CB]), sb("b_k", [P, CB])
        w_v = sb("w_v", [WIDTH + 1, WIDE_B])
        qk, v = sb("qk", [P, N]), sb("v", [WIDTH + 1, N])
        acc = ps("acc", [P, 6, HALF])
        loaded, dve_steps, zeroed, mask_steps = sem("loaded"), sem("dve_steps"), sem("zeroed"), sem("mask_steps")
        conv_ready, conv_taken, heads_ready, heads_taken = (
            sem("conv_ready"), sem("conv_taken"), sem("heads_ready"), sem("heads_taken"))
        v_heads_ready, v_heads_taken = sem("v_heads_ready"), sem("v_heads_taken")
        loads = ((conv_w[:, :, :, :], "conv_w"), (conv_b[:, :], "conv_b"), (w_qk[:, :], "w_qk"), (b_q[:, :], "b_q"),
                 (b_k[:, :], "b_k"), (w_v[:, :], "w_v"))
        block = ctx.enter_context(nc.Block())

        @block.sync
        def _(sp):
            for dst, src in loads:
                sp.dma_start(dst, i[src]).then_inc(loaded, 16)
            for dst, src in ((s.w_o[:, :, :], "w_o"), (s.b_o[:, :], "b_o"), (s.proj[:, :], "proj")):
                sp.dma_start(dst, i[src]).then_inc(s.loaded, 16)

        @block.gpsimd
        def _(pool):
            nc.gpsimd.memset(padded[:, :, :, 0:TAPS - 1], 0.0).then_inc(zeroed, 1)
            pool.wait_ge(zeroed, 1)
            nc.gpsimd.memset(v[WIDTH:WIDTH + 1, :], 1.0).then_inc(zeroed, 1)
            pool.wait_ge(zeroed, 2)
            norm_pool(nc, pool, ln)
            nc.gpsimd.memset(s.mask[:, :], 0.0).then_inc(mask_steps, 1)
            pool.wait_ge(mask_steps, 1)
            nc.gpsimd.affine_select(out=s.mask[:, :], in_=s.mask[:, :], compare_op=ALU.is_ge, fill=MASKED, base=0,
                                    pattern=[[-1, P]], channel_multiplier=1).then_inc(mask_steps, 1)
            pool.wait_ge(mask_steps, 2)
            view = s.mask[:, :].rearrange("p (g k) -> p g k", k=BLOCK)
            nc.gpsimd.affine_select(out=view, in_=view, compare_op=ALU.is_ge, fill=MASKED, base=BLOCK - 1,
                                    pattern=[[BLOCK, P // BLOCK], [0, BLOCK]], channel_multiplier=-1).then_inc(mask_steps, 1)

        @block.tensor
        def _(pe):
            norm_tensor(nc, pe, ln, ident)
            pe.wait_ge(loaded, 16 * len(loads))
            pe.wait_ge(zeroed, 2)
            pe.wait_ge(ln.copied, NT)
            for part, m in ((0, 2 * WIDTH), (1, WIDTH)):
                for h in range(NH):
                    for n in range(TAPS * DC):
                        j, d = divmod(n, DC)
                        last = nc.tensor.matmul(
                            acc[0:m, 2 * part + h, :].rearrange("p (b t) -> p b t", t=T),
                            conv_w[:, j, d, part * 2 * WIDTH:part * 2 * WIDTH + m],
                            padded[:, d, 2 * h:2 * h + 2, j:j + T], start=(n == 0), stop=(n == TAPS * DC - 1))
                    last.then_inc(conv_ready, 1)
            n = 0
            for h in range(NH):
                pe.wait_ge(conv_taken, h + 1)
                for c in range(CB):
                    for which in range(2):
                        if n >= 2:
                            pe.wait_ge(heads_taken, n - 1)
                        at = slice(which * WIDTH, (which + 1) * WIDTH)
                        nc.tensor.matmul(acc[:, 4 + n % 2, :], w_qk[at, c * P:(c + 1) * P], qk[at, h * HALF:(h + 1) * HALF],
                                         start=True, stop=True).then_inc(heads_ready, 1)
                        n += 1
            pe.wait_ge(conv_taken, 2 * NH)
            for t in range(NT):
                if t >= 2:
                    pe.wait_ge(v_heads_taken, t - 1)
                nc.tensor.matmul(acc[:, t % 2, :], v[:, t * P:(t + 1) * P], w_v[:, :], start=True, stop=True).then_inc(v_heads_ready, 1)

        @block.scalar
        def _(act):
            norm_scalar(nc, act, ln, lambda t: padded[:, :, t * P // T, TAPS - 1 + t * P % T:TAPS - 1 + t * P % T + P])
            for t in range(NT):
                act.wait_ge(v_heads_ready, t + 1)
                nc.scalar.copy(s.vh[:, t, :], acc[:, t % 2, :]).then_inc(v_heads_taken, 1)

        @block.vector
        def _(dve):
            chain = Chain(dve, dve_steps)
            norm_vector(nc, dve, ln, x, chain)
            dve.wait_ge(loaded, 16 * len(loads))
            for h in range(NH):
                dve.wait_ge(conv_ready, h + 1)
                nc.vector.tensor_scalar(qk[:, h * HALF:(h + 1) * HALF], acc[:, h, :], conv_b[:, 0:1], None,
                                        ALU.add).then_inc(conv_taken, 1)
            for h in range(NH):
                dve.wait_ge(conv_ready, NH + h + 1)
                nc.vector.tensor_scalar(v[0:WIDTH, h * HALF:(h + 1) * HALF], acc[0:WIDTH, 2 + h, :], conv_b[0:WIDTH, 1:2],
                                        None, ALU.add).then_inc(conv_taken, 1)
            n = 0
            for h in range(NH):
                for c in range(CB):
                    for dst, bias, scale in ((s.qh, b_q, HD_B ** -0.5), (s.kh, b_k, 1.0)):
                        dve.wait_ge(heads_ready, n + 1)
                        nc.vector.tensor_scalar(dst[:, c, h * HALF:(h + 1) * HALF], acc[:, 4 + n % 2, :], bias[:, c:c + 1],
                                                scale, ALU.add, ALU.mult).then_inc(heads_taken, 1)
                        n += 1


def attend_in_blocks(nc, sh, s):
    x, ident = sh.x, sh.ident
    with ExitStack() as ctx:
        sb, ps, sem = scope(nc, ctx, "b2_")
        p = sb("p", [P, 2, HEADS_B, P])
        pT = sb("pT", [P, 2, HEADS_B, P])
        row_max, row_sum = sb("row_max", [P, 2, HEADS_B]), sb("row_sum", [P, 2, HEADS_B])
        heads_out, joined = sb("heads_out", [P, 2, WIDE_B]), sb("joined", [WIDTH + 1, 2, P])
        scores = ps("scores", [P, 2, 2, HALF])
        turned = ps("turned", [P, 2, HALF])
        mixed = ps("mixed", [P, 1, HALF])
        out = ps("out", [P, 1, HALF])
        dve_steps, ones_ready = sem("dve_steps"), sem("ones_ready")
        scored, masked, shifted, exp_done, sum_ready, probs_ready = (
            sem("scored"), sem("masked"), sem("shifted"), sem("exp_done"), sem("sum_ready"), sem("probs_ready"))
        turned_ready, turned_copied, mixed_ready, mixed_copied = (
            sem("turned_ready"), sem("turned_copied"), sem("mixed_ready"), sem("mixed_copied"))
        joined_ready, joined_copied, out_ready, out_added = (
            sem("joined_ready"), sem("joined_copied"), sem("out_ready"), sem("out_added"))
        block = ctx.enter_context(nc.Block())

        @block.gpsimd
        def _(pool):
            nc.gpsimd.memset(joined[WIDTH:WIDTH + 1, :, :], 1.0).then_inc(ones_ready, 1)
            pool.wait_ge(ones_ready, 1)
            for t in range(NT):
                pool.wait_ge(sum_ready, t + 1)
                nc.gpsimd.tensor_tensor(p[:, t % 2, :, :], p[:, t % 2, :, :],
                                        row_sum[:, t % 2, :].rearrange("p (h o) -> p h o", o=1).broadcast_to([P, HEADS_B, P]),
                                        ALU.mult).then_inc(probs_ready, 1)

        @block.tensor
        def _(pe):
            def score(t):
                if t >= 2:
                    pe.wait_ge(masked, t - 1)
                for h in range(HEADS_B):
                    c, j = divmod(h, 2)
                    at = slice(j * HD_B, (j + 1) * HD_B)
                    last = nc.tensor.matmul(scores[:, t % 2, j, c * P:(c + 1) * P], s.qh[at, c, t * P:(t + 1) * P],
                                            s.kh[at, c, t * P:(t + 1) * P], start=True, stop=True)
                last.then_inc(scored, 1)

            pe.wait_ge(s.loaded, 48)
            pe.wait_ge(ones_ready, 1)
            score(0)
            for t in range(NT):
                if t + 1 < NT:
                    score(t + 1)
                pe.wait_ge(probs_ready, t + 1)
                if t >= 1:
                    pe.wait_ge(turned_copied, t)
                for n in range(HEADS_B):
                    last = nc.tensor.transpose(turned[:, n // CB, (n % CB) * P:(n % CB + 1) * P], p[:, t % 2, n, :], ident[:, :])
                last.then_inc(turned_ready, 1)
                pe.wait_ge(turned_copied, t + 1)
                if t >= 1:
                    pe.wait_ge(mixed_copied, t)
                for h in range(HEADS_B):
                    c, j = divmod(h, 2)
                    last = nc.tensor.matmul(mixed[j * HD_B:(j + 1) * HD_B, 0, c * P:(c + 1) * P],
                                            s.vh[:, t, h * HD_B:(h + 1) * HD_B], pT[:, t % 2, j * CB + c, :],
                                            start=True, stop=True)
                last.then_inc(mixed_ready, 1)
                pe.wait_ge(mixed_copied, t + 1)
                if t >= 1:
                    pe.wait_ge(out_added, t)
                for c in range(CB):
                    last = nc.tensor.matmul(out[0:WIDTH, 0, 0:P], s.w_o[:, c, :], heads_out[:, t % 2, c * P:(c + 1) * P],
                                            start=(c == 0), stop=(c == CB - 1))
                last.then_inc(joined_ready, 1)
                pe.wait_ge(joined_copied, t + 1)
                nc.tensor.matmul(out[:, 0, 0:D], joined[:, t % 2, :], s.proj[:, :], start=True, stop=True).then_inc(out_ready, 1)

        @block.scalar
        def _(act):
            for t in range(NT):
                act.wait_ge(shifted, t + 1)
                nc.scalar.activation(p[:, t % 2, :, :], p[:, t % 2, :, :], ACT.Exp).then_inc(exp_done, 1)
                act.wait_ge(turned_ready, t + 1)
                nc.scalar.copy(pT[:, t % 2, :, :].rearrange("p h n -> p (h n)"),
                               turned[:, :, :].rearrange("p a b -> p (a b)")).then_inc(turned_copied, 1)
                act.wait_ge(mixed_ready, t + 1)
                nc.scalar.copy(heads_out[:, t % 2, :], mixed[:, 0, :]).then_inc(mixed_copied, 1)

        @block.vector
        def _(dve):
            chain = Chain(dve, dve_steps)

            def prepare(t):
                dve.wait_ge(scored, t + 1)
                if t >= 2:
                    dve.wait_ge(turned_ready, t - 1)
                nc.vector.tensor_tensor(p[:, t % 2, :, :], scores[:, t % 2, :, :].rearrange("p j (c n) -> p (j c) n", n=P),
                                        s.mask[:, :].rearrange("p (o n) -> p o n", o=1).broadcast_to([P, HEADS_B, P]),
                                        ALU.add).then_inc(masked, 1)
                dve.wait_ge(masked, t + 1)
                chain.step(nc.vector.tensor_reduce(row_max[:, t % 2, :], p[:, t % 2, :, :], AX.X, ALU.max))
                nc.vector.tensor_tensor(p[:, t % 2, :, :], p[:, t % 2, :, :],
                                        row_max[:, t % 2, :].rearrange("p (h o) -> p h o", o=1).broadcast_to([P, HEADS_B, P]),
                                        ALU.subtract).then_inc(shifted, 1)

            def sums(t):
                dve.wait_ge(exp_done, t + 1)
                chain.step(nc.vector.tensor_reduce(row_sum[:, t % 2, :], p[:, t % 2, :, :], AX.X, ALU.add))
                nc.vector.reciprocal(row_sum[:, t % 2, :], row_sum[:, t % 2, :]).then_inc(sum_ready, 1)

            dve.wait_ge(s.loaded, 48)
            prepare(0)
            for t in range(NT):
                sums(t)
                if t + 1 < NT:
                    prepare(t + 1)
                dve.wait_ge(joined_ready, t + 1)
                nc.vector.tensor_scalar(joined[0:WIDTH, t % 2, :], out[0:WIDTH, 0, 0:P], s.b_o[:, 0:1], None,
                                        ALU.add).then_inc(joined_copied, 1)
                dve.wait_ge(out_ready, t + 1)
                nc.vector.tensor_tensor(x[:, t, :], x[:, t, :], out[:, 0, 0:D], ALU.add).then_inc(out_added, 1)


HEADS_C = 16
HD_C = D // HEADS_C
PARTS = 4
LEVELS = 127.0
LEVELS_P = 255.0
SCALE_LEAST = 1e-8
WC = HEADS_C * PARTS * HD_C // P


def cross_attention(nc, sh, i):
    with ExitStack() as ctx:
        sb, ps, sem = scope(nc, ctx, "c0_")
        s = Buffers()
        s.qT = sb("qT", [P, WC, N], BF16)
        s.kT = sb("kT", [P, WC, N], BF16)
        s.v = sb("v", [P, NT, D], BF16)
        s.q_scale = sb("q_scale", [P, NT, HEADS_C])
        s.v_scale = sb("v_scale", [P, DC])
        s.identb = sb("identb", [P, P], BF16)
        s.w_p = sb("w_p", [P, DC, D])
        s.b_p = sb("b_p", [1, D])
        s.ones = sb("ones", [1, P])
        quantise(nc, sh, s, i)
        attend(nc, sh, s)


def quantise(nc, sh, s, i):
    x, xT, ident, ctxT = sh.x, sh.xT, sh.ident, sh.ctxT
    with ExitStack() as ctx:
        sb, ps, sem = scope(nc, ctx, "c1_")
        ln = norm_buffers(sb, ps, sem)
        w_q, w_kv = sb("w_q", [P, DC, D]), sb("w_kv", [P, DC, 2 * D])
        b_q, b_k, b_v = sb("b_q", [1, D]), sb("b_k", [1, D]), sb("b_v", [P, DC])
        k, q, vT = sb("k", [P, NT, D]), sb("q", [P, NT, D]), sb("vT", [P, DC, N])
        vTb = sb("vTb", [P, DC, N], BF16)
        scale, inverse = sb("scale", [P, NT, HEADS_C]), sb("inverse", [P, NT, HEADS_C])
        q_inverse = sb("q_inverse", [P, NT, HEADS_C])
        v_inverse = sb("v_inverse", [P, DC])
        k_parts = sb("k_parts", [P, NT, HEADS_C, PARTS, HD_C], BF16)
        q_parts = sb("q_parts", [P, NT, HEADS_C, PARTS, HD_C], BF16)
        rowb = ps("rowb", [P, 2, HALF])
        colb = ps("colb", [P, 2, HALF])
        turnedb = ps("turnedb", [P, 2, 2 * HALF], BF16)
        loaded, dve_steps, zeroed = sem("loaded"), sem("dve_steps"), sem("zeroed")
        rows_ready, rows_taken, cols_ready, cols_taken = sem("rows_ready"), sem("rows_taken"), sem("cols_ready"), sem("cols_taken")
        k_split, q_split, v_rounded, turned_ready, turned_copied = (
            sem("k_split"), sem("q_split"), sem("v_rounded"), sem("turned_ready"), sem("turned_copied"))
        loads = ((w_kv[:, :, :], "w_kv"), (b_k[:, :], "b_kc"), (b_v[:, :], "b_v"), (w_q[:, :, :], "w_qc"), (b_q[:, :], "b_qc"),
                 (s.w_p[:, :, :], "w_p"), (s.b_p[:, :], "b_p"))
        block = ctx.enter_context(nc.Block())

        @block.sync
        def _(sp):
            for dst, src in loads:
                sp.dma_start(dst, i[src]).then_inc(loaded, 16)

        @block.gpsimd
        def _(pool):
            nc.gpsimd.memset(k_parts[:, :, :, PARTS - 1, :], 0.0).then_inc(zeroed, 1)
            nc.gpsimd.memset(q_parts[:, :, :, PARTS - 1, :], 0.0).then_inc(zeroed, 1)
            nc.gpsimd.tensor_copy(s.identb[:, :], ident[:, :]).then_inc(zeroed, 1)
            pool.wait_ge(zeroed, 3)
            nc.gpsimd.memset(s.ones[:, :], 1.0).then_inc(zeroed, 1)
            pool.wait_ge(zeroed, 4)
            norm_pool(nc, pool, ln)

        @block.tensor
        def _(pe):
            pe.wait_ge(loaded, 16 * len(loads))
            pe.wait_ge(zeroed, 4)
            for n in range(2 * NT):
                t = n % NT
                if n == NT:
                    norm_tensor(nc, pe, ln, ident)
                    pe.wait_ge(ln.copied, NT)
                if n >= 2:
                    pe.wait_ge(rows_taken, n - 1)
                src, w, bias = (ctxT, w_kv, b_k) if n < NT else (xT, w_q, b_q)
                for c in range(DC):
                    nc.tensor.matmul(rowb[:, n % 2, 0:D], src[:, c, t * P:(t + 1) * P], w[:, c, 0:D], start=(c == 0), stop=False)
                nc.tensor.matmul(rowb[:, n % 2, 0:D], s.ones[:, :], bias[:, :], start=False, stop=True).then_inc(rows_ready, 1)
                if n < NT and n % 2 == 1:
                    g = n // 2
                    c, h = divmod(g, NH)
                    if g >= 2:
                        pe.wait_ge(cols_taken, g - 1)
                    for d in range(DC):
                        last = nc.tensor.matmul(colb[:, g % 2, :], w_kv[:, d, D + c * P:D + (c + 1) * P],
                                                ctxT[:, d, h * HALF:(h + 1) * HALF], start=(d == 0), stop=(d == DC - 1))
                    last.then_inc(cols_ready, 1)
            n = 0
            for split, src in ((k_split, k_parts), (v_rounded, vTb), (q_split, q_parts)):
                pe.wait_ge(split, 1)
                for t in range(NT) if src is not vTb else range(2):
                    if n >= 2:
                        pe.wait_ge(turned_copied, n - 1)
                    for c in range(WC):
                        if src is vTb:
                            m, d = divmod(4 * DC * t + c, DC)
                            block_in = vTb[:, d, m * P:(m + 1) * P]
                        else:
                            block_in = src[:, t, 2 * c:2 * c + 2, :, :].rearrange("p h r d -> p (h r d)")
                        last = nc.tensor.transpose(turnedb[:, n % 2, c * P:(c + 1) * P], block_in, s.identb[:, :])
                    last.then_inc(turned_ready, 1)
                    n += 1

        @block.scalar
        def _(act):
            act.wait_ge(loaded, 16 * len(loads))
            rows_done = 0

            def take_row(n):
                act.wait_ge(rows_ready, n + 1)
                if n < NT:
                    nc.scalar.copy(k[:, n, :], rowb[:, n % 2, 0:D]).then_inc(rows_taken, 1)
                else:
                    nc.scalar.activation(q[:, n - NT, :], rowb[:, n % 2, 0:D], ACT.Copy, scale=HD_C ** -0.5).then_inc(rows_taken, 1)

            for n in range(NT):
                take_row(n)
                if n % 2 == 1:
                    g = n // 2
                    c, h = divmod(g, NH)
                    act.wait_ge(cols_ready, g + 1)
                    nc.scalar.activation(vT[:, c, h * HALF:(h + 1) * HALF], colb[:, g % 2, :], ACT.Identity,
                                         bias=b_v[:, c:c + 1]).then_inc(cols_taken, 1)
            norm_scalar(nc, act, ln, lambda t: xT[:, :, t * P:(t + 1) * P])
            for n in range(NT, 2 * NT):
                take_row(n)
            n = 0
            for dst in (s.kT, s.v, s.qT):
                for t in range(NT) if dst is not s.v else range(2):
                    act.wait_ge(turned_ready, n + 1)
                    src = turnedb[:, n % 2, :]
                    if dst is s.v:
                        nc.scalar.copy(s.v[:, 4 * t:4 * t + 4, :].rearrange("p m n -> p (m n)"), src).then_inc(turned_copied, 1)
                    else:
                        nc.scalar.copy(dst[:, :, t * P:(t + 1) * P], src.rearrange("p (c n) -> p c n", n=P)).then_inc(turned_copied, 1)
                    n += 1

        @block.vector
        def _(dve):
            chain = Chain(dve, dve_steps)
            norm_vector(nc, dve, ln, x, chain)

            def heads(a):
                return a[:, :, :].rearrange("p t (h d) -> p (t h) d", d=HD_C)

            def spread(a):
                return a[:, :, :].rearrange("p t (h o) -> p (t h) o", o=1).broadcast_to([P, NT * HEADS_C, HD_C])

            def scales(a, scale_out, inverse_out):
                chain.step(nc.vector.tensor_reduce(scale_out[:, :, :].rearrange("p t h -> p (t h)"), heads(a), AX.X, ALU.max,
                                                   apply_absolute_value=True))
                chain.step(nc.vector.tensor_scalar(scale_out[:, :, :], scale_out[:, :, :], 1.0 / LEVELS, SCALE_LEAST,
                                                   ALU.mult, ALU.max))
                chain.step(nc.vector.reciprocal(inverse_out[:, :, :], scale_out[:, :, :]))

            def integers(a, inverse_out):
                chain.step(nc.vector.tensor_tensor(heads(a), heads(a), spread(inverse_out), ALU.mult))
                chain.step(nc.vector.tensor_scalar(a[:, :, :], a[:, :, :], ROUND, ROUND, ALU.add, ALU.subtract))
                chain.step(nc.vector.tensor_scalar(a[:, :, :], a[:, :, :], LEVELS, -LEVELS, ALU.min, ALU.max))

            def part(a, r):
                return a[:, :, :, r, :].rearrange("p t h d -> p (t h) d")

            dve.wait_ge(rows_taken, NT)
            scales(k, scale, inverse)
            integers(k, inverse)
            chain.step(nc.vector.tensor_tensor(heads(k), heads(k), spread(scale), ALU.mult))
            dve.wait_ge(zeroed, 2)
            chain.step(nc.vector.tensor_copy(part(k_parts, 0), heads(k)))
            chain.step(nc.vector.tensor_tensor(heads(k), heads(k), part(k_parts, 0), ALU.subtract))
            chain.step(nc.vector.tensor_copy(part(k_parts, 1), heads(k)))
            nc.vector.tensor_tensor(part(k_parts, 2), heads(k), part(k_parts, 1), ALU.subtract).then_inc(k_split, 1)
            dve.wait_ge(cols_taken, DC * NH)
            chain.step(nc.vector.tensor_reduce(s.v_scale[:, :], vT[:, :, :], AX.X, ALU.max, apply_absolute_value=True))
            chain.step(nc.vector.tensor_scalar(s.v_scale[:, :], s.v_scale[:, :], 1.0 / LEVELS, SCALE_LEAST, ALU.mult, ALU.max))
            chain.step(nc.vector.reciprocal(v_inverse[:, :], s.v_scale[:, :]))
            for c in range(DC):
                last = nc.vector.tensor_scalar(vT[:, c, :], vT[:, c, :], v_inverse[:, c:c + 1], ROUND, ALU.mult, ALU.add)
            chain.step(last)
            chain.step(nc.vector.tensor_scalar(vT[:, :, :], vT[:, :, :], ROUND, None, ALU.subtract))
            nc.vector.tensor_scalar(vTb[:, :, :], vT[:, :, :], LEVELS, -LEVELS, ALU.min, ALU.max).then_inc(v_rounded, 1)
            dve.wait_ge(rows_taken, 2 * NT)
            scales(q, s.q_scale, q_inverse)
            integers(q, q_inverse)
            for r in range(PARTS - 1):
                last = nc.vector.tensor_copy(part(q_parts, r), heads(q))
            last.then_inc(q_split, 1)


def attend(nc, sh, s):
    x, ident = sh.x, sh.ident
    with ExitStack() as ctx:
        sb, ps, sem = scope(nc, ctx, "c2_")
        RING = 6
        MIX_LAG = 5
        ON_ACT = 2
        LOG_LEVELS = float(np.log(LEVELS_P))
        UNITS_C = NT * HEADS_C
        probs = sb("probs", [P, RING, N], I16)
        bits = probs[:, :, :].bitcast(BF16)
        pT = sb("pT", [P, RING, NT, P], BF16)
        neg_max, bias = sb("neg_max", [P, NT, HEADS_C]), sb("bias", [P, NT, HEADS_C])
        row_sum = sb("row_sum", [P, NT, HEADS_C])
        o, oT = sb("o", [P, D]), sb("oT", [P, DC, P])
        scores = ps("scores", [P, 2, 2, HALF])
        turned = ps("turned", [P, 2, 2 * HALF], BF16)
        mixed = ps("mixed", [P, 1, HALF])
        tail = ps("tail", [P, 1, HALF])
        dve_steps = sem("dve_steps")
        scored, bias_ready, exp_done, turned_ready, turned_copied = (
            sem("scored"), sem("bias_ready"), sem("exp_done"), sem("turned_ready"), sem("turned_copied"))
        mixed_ready, o_ready, oT_ready, oT_copied, out_ready, out_added = (
            sem("mixed_ready"), sem("o_ready"), sem("oT_ready"), sem("oT_copied"), sem("out_ready"), sem("out_added"))
        turned_copied_act = sem("turned_copied_act")

        def on_act(u):
            return u % ON_ACT == ON_ACT - 1

        def wait_copied(eng, u):
            acts = sum(on_act(v) for v in range(u + 1))
            if acts:
                eng.wait_ge(turned_copied_act, acts)
            if u + 1 > acts:
                eng.wait_ge(turned_copied, u + 1 - acts)

        block = ctx.enter_context(nc.Block())

        @block.tensor
        def _(pe):
            def score(u):
                t, h = divmod(u, HEADS_C)
                if u >= 2:
                    pe.wait_ge(exp_done, u - 1)
                at = slice(h % 2 * P // 2, (h % 2 + 1) * P // 2)
                for n in range(2):
                    last = nc.tensor.matmul(scores[:, u % 2, n, :], s.qT[at, h // 2, t * P:(t + 1) * P],
                                            s.kT[at, h // 2, n * HALF:(n + 1) * HALF], start=True, stop=True)
                last.then_inc(scored, 1)

            def turn(u):
                pe.wait_ge(exp_done, u + 1)
                if u >= 2:
                    wait_copied(pe, u - 2)
                for n in range(NT):
                    last = nc.tensor.transpose(turned[:, u % 2, n * P:(n + 1) * P], bits[:, u % RING, n * P:(n + 1) * P],
                                               s.identb[:, :])
                last.then_inc(turned_ready, 1)

            def mix(u):
                t, h = divmod(u, HEADS_C)
                wait_copied(pe, u)
                if h == 0 and t >= 1:
                    pe.wait_ge(o_ready, t)
                for n in range(NT):
                    last = nc.tensor.matmul(mixed[:, 0, h * HD_C:(h + 1) * HD_C], pT[:, u % RING, n, :],
                                            s.v[:, n, h * HD_C:(h + 1) * HD_C], start=(n == 0), stop=(n == NT - 1))
                last.then_inc(mixed_ready, 1)

            def finish_a(t):
                pe.wait_ge(o_ready, t + 1)
                if t >= 1:
                    pe.wait_ge(out_added, t)
                for c in range(DC):
                    last = nc.tensor.transpose(tail[:, 0, c * P:(c + 1) * P], o[:, c * P:(c + 1) * P], ident[:, :])
                last.then_inc(oT_ready, 1)

            def finish_b(t):
                pe.wait_ge(oT_copied, t + 1)
                for c in range(DC):
                    nc.tensor.matmul(tail[:, 0, 0:D], oT[:, c, :], s.w_p[:, c, :], start=(c == 0), stop=False)
                nc.tensor.matmul(tail[:, 0, 0:D], s.ones[:, :], s.b_p[:, :], start=False, stop=True).then_inc(out_ready, 1)

            for u in range(UNITS_C + MIX_LAG):
                if u < UNITS_C:
                    score(u)
                if 2 <= u < UNITS_C + 2:
                    turn(u - 2)
                if u >= MIX_LAG:
                    mix(u - MIX_LAG)
                    t, h = divmod(u - MIX_LAG, HEADS_C)
                    if h == 3 and t >= 1:
                        finish_a(t - 1)
                    if h == 7 and t >= 1:
                        finish_b(t - 1)
            finish_a(NT - 1)
            finish_b(NT - 1)

        @block.scalar
        def _(act):
            def copy_turned(u):
                act.wait_ge(turned_ready, u + 1)
                if u >= RING:
                    act.wait_ge(mixed_ready, u - RING + 1)
                nc.scalar.copy(pT[:, u % RING, :, :].rearrange("p n q -> p (n q)"), turned[:, u % 2, :].bitcast(I16)).then_inc(turned_copied_act, 1)

            for u in range(UNITS_C + 2):
                if u < UNITS_C:
                    t, h = divmod(u, HEADS_C)
                    act.wait_ge(bias_ready, u + 1)
                    if u >= RING:
                        act.wait_ge(turned_ready, u - RING + 1)
                    nc.scalar.activation(probs[:, u % RING, :], scores[:, u % 2, :, :].rearrange("p a b -> p (a b)"), ACT.Exp,
                                         bias=bias[:, t, h:h + 1], scale=s.q_scale[:, t, h:h + 1],
                                         accum_out=row_sum[:, t, h:h + 1]).then_inc(exp_done, 1)
                if u >= 2 and on_act(u - 2):
                    copy_turned(u - 2)

        @block.vector
        def _(dve):
            chain = Chain(dve, dve_steps)

            def row_max(u):
                t, h = divmod(u, HEADS_C)
                dve.wait_ge(scored, u + 1)
                chain.step(nc.vector.tensor_reduce(neg_max[:, t, h:h + 1], scores[:, u % 2, :, :].rearrange("p a b -> p (a b)"),
                                                   AX.X, ALU.max, negate=True))
                nc.vector.tensor_scalar(bias[:, t, h:h + 1], neg_max[:, t, h:h + 1], s.q_scale[:, t, h:h + 1], LOG_LEVELS,
                                        ALU.mult, ALU.add).then_inc(bias_ready, 1)

            def copy_turned(u):
                dve.wait_ge(turned_ready, u + 1)
                if u >= RING:
                    dve.wait_ge(mixed_ready, u - RING + 1)
                nc.vector.tensor_copy(pT[:, u % RING, :, :].rearrange("p n q -> p (n q)"), turned[:, u % 2, :].bitcast(I16)).then_inc(turned_copied, 1)

            def normalise(t):
                dve.wait_ge(exp_done, HEADS_C * (t + 1))
                chain.step(nc.vector.reciprocal(row_sum[:, t, :], row_sum[:, t, :]))
                dve.wait_ge(mixed_ready, HEADS_C * (t + 1))
                if t >= 1:
                    dve.wait_ge(oT_ready, t)
                nc.vector.tensor_tensor(o[:, :].rearrange("p (h d) -> p h d", d=HD_C),
                                        mixed[:, 0, 0:D].rearrange("p (h d) -> p h d", d=HD_C),
                                        row_sum[:, t, :].rearrange("p (h o) -> p h o", o=1).broadcast_to([P, HEADS_C, HD_C]),
                                        ALU.mult).then_inc(o_ready, 1)

            def scale_values(t):
                dve.wait_ge(oT_ready, t + 1)
                if t >= 1:
                    dve.wait_ge(out_ready, t)
                for c in range(DC):
                    last = nc.vector.tensor_scalar(oT[:, c, :], tail[:, 0, c * P:(c + 1) * P], s.v_scale[:, c:c + 1], None, ALU.mult)
                last.then_inc(oT_copied, 1)

            def residual(t):
                dve.wait_ge(out_ready, t + 1)
                nc.vector.tensor_tensor(x[:, t, :], x[:, t, :], tail[:, 0, 0:D], ALU.add).then_inc(out_added, 1)

            for u in range(UNITS_C + 2):
                if u < UNITS_C:
                    row_max(u)
                if u >= 2 and not on_act(u - 2):
                    copy_turned(u - 2)
                if u >= HEADS_C + 2:
                    t, h = divmod(u - 2, HEADS_C)
                    if h == MIX_LAG - 2:
                        normalise(t - 1)
                    if h == 9:
                        scale_values(t - 1)
                    if h == 12:
                        residual(t - 1)
            normalise(NT - 1)
            scale_values(NT - 1)
            residual(NT - 1)


EXPERTS = 16
INNER = 176
RANKS = EXPERTS + 1
HIDDEN = RANKS * INNER
HC = (HIDDEN + P - 1) // P
PART_ROWS = 32
THREE = 3


def routed_experts(nc, sh, i):
    with ExitStack() as ctx:
        sb, ps, sem = scope(nc, ctx, "e0_")
        s = Buffers()
        s.w1 = sb("w1", [P, DC, HIDDEN])
        s.w3 = sb("w3", [P, DC, HIDDEN])
        s.w2 = sb("w2", [P, HC, D])
        s.weightsT = sb("weightsT", [THREE * PART_ROWS, N], BF16)
        s.spread = sb("spread", [THREE * PART_ROWS, HIDDEN], BF16)
        s.loaded = sem("weights_loaded")
        route(nc, sh, s, i)
        mix_experts(nc, sh, s)


def route(nc, sh, s, i):
    x, xT, ident = sh.x, sh.xT, sh.ident
    with ExitStack() as ctx:
        sb, ps, sem = scope(nc, ctx, "e1_")
        ln = norm_buffers(sb, ps, sem)
        gate, bias = sb("gate", [P, DC, EXPERTS]), sb("bias", [P, EXPERTS])
        number, number_i = sb("number", [P, EXPERTS]), sb("number_i", [P, EXPERTS], I32)
        score, chosen = sb("score", [P, NT, EXPERTS]), sb("chosen", [P, NT, EXPERTS])
        best, at, atf = sb("best", [P, NT, 8]), sb("at", [P, NT, 8], U32), sb("atf", [P, NT, 8])
        total = sb("total", [P, NT])
        parts = sb("parts", [P, NT, THREE, PART_ROWS], BF16)
        identb = sb("identb", [P, P], BF16)
        logits = ps("logits", [P, 1, HALF])
        turnedb = ps("turnedb", [P, 1, 2 * HALF], BF16)
        loaded, dve_steps, zeroed, spread_steps = sem("loaded"), sem("dve_steps"), sem("zeroed"), sem("spread_steps")
        logits_ready, score_ready, parts_ready, turned_ready, copied = (
            sem("logits_ready"), sem("score_ready"), sem("parts_ready"), sem("turned_ready"), sem("copied"))
        block = ctx.enter_context(nc.Block())

        @block.sync
        def _(sp):
            sp.dma_start(gate[:, :, :], i["gate"]).then_inc(loaded, 16)
            sp.dma_start(bias[:, :], i["bias"].broadcast_to([P, EXPERTS])).then_inc(loaded, 16)
            for dst, src in ((s.w1[:, :, :], "w1"), (s.w3[:, :, :], "w3"), (s.w2[:, :, :], "w2")):
                sp.dma_start(dst, i[src]).then_inc(s.loaded, 16)

        @block.gpsimd
        def _(pool):
            norm_pool(nc, pool, ln)
            nc.gpsimd.memset(parts[:, :, :, :], 0.0).then_inc(zeroed, 1)
            nc.gpsimd.iota(number_i[:, :], [[1, EXPERTS]], base=0, channel_multiplier=0).then_inc(zeroed, 1)
            nc.gpsimd.tensor_copy(identb[:, :], ident[:, :]).then_inc(zeroed, 1)
            view = s.spread[:, :].rearrange("p (e k) -> p e k", k=INNER)
            nc.gpsimd.memset(s.spread[:, :], 0.0).then_inc(spread_steps, 1)
            for r in range(THREE):
                pool.wait_ge(spread_steps, r + 1)
                nc.gpsimd.affine_select(out=view, in_=view, compare_op=ALU.not_equal, fill=1.0, base=-r * PART_ROWS,
                                        pattern=[[-1, RANKS], [0, INNER]], channel_multiplier=1).then_inc(spread_steps, 1)
            pool.wait_ge(spread_steps, THREE + 1)

        @block.tensor
        def _(pe):
            norm_tensor(nc, pe, ln, ident)
            pe.wait_ge(loaded, 32)
            pe.wait_ge(ln.copied, NT)
            for t in range(NT):
                for c in range(DC):
                    last = nc.tensor.matmul(logits[:, 0, t * EXPERTS:(t + 1) * EXPERTS], xT[:, c, t * P:(t + 1) * P],
                                            gate[:, c, :], start=(c == 0), stop=(c == DC - 1))
            last.then_inc(logits_ready, 1)
            pe.wait_ge(parts_ready, 1)
            for t in range(NT):
                last = nc.tensor.transpose(turnedb[0:THREE * PART_ROWS, 0, t * P:(t + 1) * P],
                                           parts[:, t, :, :].rearrange("p r e -> p (r e)"), identb[:, :])
            last.then_inc(turned_ready, 1)

        @block.scalar
        def _(act):
            norm_scalar(nc, act, ln, lambda t: xT[:, :, t * P:(t + 1) * P])
            act.wait_ge(logits_ready, 1)
            nc.scalar.activation(score[:, :, :].rearrange("p t e -> p (t e)"), logits[:, 0, 0:NT * EXPERTS],
                                 ACT.Sigmoid).then_inc(score_ready, 1)
            act.wait_ge(turned_ready, 1)
            nc.scalar.copy(s.weightsT[:, :], turnedb[0:THREE * PART_ROWS, 0, :]).then_inc(copied, 1)

        @block.vector
        def _(dve):
            chain = Chain(dve, dve_steps)
            norm_vector(nc, dve, ln, x, chain)
            dve.wait_ge(zeroed, 3)
            nc.vector.tensor_copy(number[:, :], number_i[:, :])
            dve.wait_ge(loaded, 32)
            dve.wait_ge(score_ready, 1)
            chain.step(nc.vector.tensor_tensor(chosen[:, :, :], score[:, :, :],
                                               bias[:, :].rearrange("p (o e) -> p o e", o=1).broadcast_to([P, NT, EXPERTS]), ALU.add))
            for t in range(NT):
                last = nc.vector.max(best[:, t, :], chosen[:, t, :])
            chain.step(last)
            for t in range(NT):
                last = nc.vector.max_index(at[:, t, :], best[:, t, :], chosen[:, t, :])
            chain.step(last)
            chain.step(nc.vector.tensor_copy(atf[:, :, :], at[:, :, :]))
            for t in range(NT):
                last = nc.vector.tensor_scalar(chosen[:, t, :], number[:, :], atf[:, t, 0:1], None, ALU.is_equal)
            chain.step(last)
            for t in range(NT):
                last = nc.vector.scalar_tensor_tensor(chosen[:, t, :], number[:, :], atf[:, t, 1:2], chosen[:, t, :],
                                                      ALU.is_equal, ALU.add)
            chain.step(last)
            chain.step(nc.vector.tensor_tensor(chosen[:, :, :], chosen[:, :, :], score[:, :, :], ALU.mult))
            chain.step(nc.vector.tensor_reduce(total[:, :], chosen[:, :, :], AX.X, ALU.add))
            chain.step(nc.vector.reciprocal(total[:, :], total[:, :]))
            chain.step(nc.vector.tensor_tensor(chosen[:, :, :], chosen[:, :, :],
                                               total[:, :].rearrange("p (t o) -> p t o", o=1).broadcast_to([P, NT, EXPERTS]), ALU.mult))
            for r in range(THREE):
                part = parts[:, :, r, 0:EXPERTS]
                chain.step(nc.vector.tensor_copy(part, chosen[:, :, :]))
                if r < THREE - 1:
                    chain.step(nc.vector.tensor_tensor(chosen[:, :, :], chosen[:, :, :], part, ALU.subtract))
            nc.vector.memset(parts[:, :, 0, EXPERTS:RANKS], 1.0).then_inc(parts_ready, 1)


def mix_experts(nc, sh, s):
    x, xT = sh.x, sh.xT
    with ExitStack() as ctx:
        sb, ps, sem = scope(nc, ctx, "e2_")
        RING = 4
        LAG = 2
        gated = sb("gated", [P, RING, HALF])
        a = ps("a", [P, 2, HALF])
        b = ps("b", [P, 2, HALF])
        weight = ps("weight", [P, 2, HALF])
        out = ps("out", [P, 2, HALF])
        TH = HALF // P
        a_ready, b_ready, silu_ready, product_ready, weighted, summed = (
            sem("a_ready"), sem("b_ready"), sem("silu_ready"), sem("product_ready"), sem("weighted"), sem("summed"))
        out_added = sem("out_added")
        units = [(h, c) for h in range(NH) for c in range(HC)]

        def size(c):
            return min(P, HIDDEN - c * P)

        block = ctx.enter_context(nc.Block())

        @block.tensor
        def _(pe):
            pe.wait_ge(s.loaded, 48)

            def hidden(u):
                h, c = units[u]
                m, at = size(c), slice(h * HALF, (h + 1) * HALF)
                if u >= 2:
                    pe.wait_ge(weighted, u - 1)
                for dst, w in ((a, s.w1), (b, s.w3)):
                    for d in range(DC):
                        last = nc.tensor.matmul(dst[0:m, u % 2, :], w[:, d, c * P:c * P + m], xT[:, d, at],
                                                start=(d == 0), stop=(d == DC - 1))
                    if dst is a:
                        last.then_inc(a_ready, 1)
                nc.tensor.matmul(weight[0:m, u % 2, :], s.spread[:, c * P:c * P + m], s.weightsT[:, at],
                                 start=True, stop=True).then_inc(b_ready, 1)

            def down(u):
                h, c = units[u]
                pe.wait_ge(weighted, u + 1)
                if c == 0 and h >= 1:
                    pe.wait_ge(out_added, h)
                for t in range(TH):
                    last = nc.tensor.matmul(out[:, t // 2, t % 2 * D:(t % 2 + 1) * D], gated[0:size(c), u % RING, t * P:(t + 1) * P],
                                            s.w2[0:size(c), c, :], start=(c == 0 and t % 2 == 0), stop=(c == HC - 1),
                                            skip_group_check=True)
                last.then_inc(summed, 1)

            for u in range(len(units) + LAG):
                if u < len(units):
                    hidden(u)
                if u >= LAG:
                    down(u - LAG)

        @block.scalar
        def _(act):
            for u, (h, c) in enumerate(units):
                act.wait_ge(a_ready, u + 1)
                if u >= RING:
                    act.wait_ge(summed, u - RING + 1)
                nc.scalar.activation(gated[0:size(c), u % RING, :], a[0:size(c), u % 2, :], ACT.Silu).then_inc(silu_ready, 1)

        @block.vector
        def _(dve):
            for u, (h, c) in enumerate(units):
                g = gated[0:size(c), u % RING, :]
                dve.wait_ge(silu_ready, u + 1)
                dve.wait_ge(b_ready, u + 1)
                nc.vector.tensor_tensor(g, b[0:size(c), u % 2, :], g, ALU.mult).then_inc(product_ready, 1)
                dve.wait_ge(product_ready, u + 1)
                nc.vector.tensor_tensor(g, weight[0:size(c), u % 2, :], g, ALU.mult).then_inc(weighted, 1)
                if c == HC - 1:
                    dve.wait_ge(summed, u + 1)
                    for j in range(TH // 2):
                        t = h * TH + 2 * j
                        last = nc.vector.tensor_tensor(x[:, t:t + 2, :].rearrange("p t d -> p (t d)"),
                                                       x[:, t:t + 2, :].rearrange("p t d -> p (t d)"), out[:, j, :], ALU.add)
                    last.then_inc(out_added, 1)


def finish_stage(nc, x, out_dram):
    with ExitStack() as ctx:
        sb, ps, sem = scope(nc, ctx, "end_")
        stored = sem("stored")
        block = ctx.enter_context(nc.Block())

        @block.sync
        def _(sp):
            sp.dma_start(out_dram, x[:, :, :]).then_inc(stored, 16)
            sp.wait_ge(stored, 16)


def decoder(nc, i, out):
    with ExitStack() as ctx:
        sb, ps, sem = scope(nc, ctx, "")
        sh = Buffers()
        sh.x = sb("x", [P, NT, D])
        sh.xT = sb("xT", [P, DC, N])
        sh.ident = sb("ident", [P, P])
        sh.ctxT = sb("ctxT", [P, DC, EXPERTS_T * D])
        start_stage(nc, sh.x, sh.ident, i["x"])
        linear_attention(nc, sh, i["w_qkv"], i["w_out"], i["decay"])
        token_experts(nc, sh, i["ids"], i["ctxT"])
        retrieval(nc, sh, i)
        block_attention(nc, sh, i)
        cross_attention(nc, sh, i)
        routed_experts(nc, sh, i)
        finish_stage(nc, sh.x, out)


def rows(a):
    a = np.asarray(a)
    return np.ascontiguousarray(a.reshape(-1, P, a.shape[-1]).transpose(1, 0, 2))


def column(a):
    return np.ascontiguousarray(np.asarray(a).reshape(-1, P).T)


def layouts(g):
    a = {}
    a["x"] = rows(np.asarray(g["x"]).reshape(N, D))
    a["w_qkv"] = rows(g["L0_attn_w_qkv"])
    a["w_out"] = rows(g["L0_attn_w_out"])
    a["decay"] = column(np.repeat(np.asarray(g["L0_attn_decay_param"]), HD0))
    a["ids"] = np.ascontiguousarray(np.asarray(g["itok_BxS_13_99985"]).reshape(1, N))
    a["ctxT"] = rows(np.asarray(g["ctx_2048"]).reshape(N, D).T)
    a["w_up"] = rows(np.asarray(g["L0_ffn_W_up"]).T)
    a["b_up"] = column(g["L0_ffn_b_up"])
    a["w_down"] = rows(np.asarray(g["L0_ffn_W_down"]).T)
    a["b_down"] = column(g["L0_ffn_b_down"])
    a["w_q"] = rows(g["L0_ffn_W_q"])
    k = np.asarray(g["L0_ffn_keys"]).reshape(HEADS_R // 2, 2, KEYS, 2, RETR)
    a["keys"] = np.ascontiguousarray(k.transpose(1, 4, 3, 0, 2).reshape(2, RETR, UC, KEYS))
    a["down"] = np.ascontiguousarray(np.asarray(g["L0_ffn_down_embed"]).T)
    a["up"] = rows(g["L0_ffn_up_embed"])
    w = np.asarray(g["L1_attn_conv_w"]).reshape(TAPS, DC, P, 3 * WIDTH)
    a["conv_w"] = np.ascontiguousarray(w.transpose(2, 0, 1, 3))
    b = np.asarray(g["L1_attn_conv_b"])
    a["conv_b"] = column(np.concatenate([b, np.zeros(P - WIDTH, b.dtype)]))
    a["w_qk"] = np.concatenate([np.asarray(g["L1_attn_" + n]).reshape(WIDTH, WIDE_B) for n in ("wq", "wk")])
    a["b_q"] = column(np.asarray(g["L1_attn_bq"]).reshape(-1))
    a["b_k"] = column(np.asarray(g["L1_attn_bk"]).reshape(-1))
    a["w_v"] = np.concatenate([np.asarray(g["L1_attn_wv"]).reshape(WIDTH, WIDE_B),
                               np.asarray(g["L1_attn_bv"]).reshape(1, WIDE_B)])
    a["w_o"] = rows(np.asarray(g["L1_attn_wo"]).reshape(WIDE_B, WIDTH))
    a["b_o"] = np.asarray(g["L1_attn_bo"]).reshape(WIDTH, 1)
    a["proj"] = np.concatenate([np.asarray(g["L1_attn_proj_w"]), np.asarray(g["L1_attn_proj_b"]).reshape(1, D)])
    a["w_kv"] = rows(g["L1_xattn_Wkv"])
    a["w_qc"] = rows(g["L1_xattn_Wq"])
    a["w_p"] = rows(g["L1_xattn_Wp"])
    b = np.asarray(g["L1_xattn_bkv"])
    a["b_kc"] = b[:D].reshape(1, D)
    a["b_v"] = column(b[D:])
    a["b_qc"] = np.asarray(g["L1_xattn_bq"]).reshape(1, D)
    a["b_p"] = np.asarray(g["L1_xattn_bp"]).reshape(1, D)
    a["gate"] = rows(np.asarray(g["L1_ffn_gate_w"]).T)
    a["bias"] = np.asarray(g["L1_ffn_bias"]).reshape(1, EXPERTS)
    for n in ("w1", "w3"):
        w = np.concatenate([np.asarray(g["L1_ffn_" + n]).reshape(EXPERTS * INNER, D), np.asarray(g["L1_ffn_shared_" + n])])
        a[n] = rows(w.T)
    w = np.concatenate([np.asarray(g["L1_ffn_w2"]).transpose(0, 2, 1).reshape(EXPERTS * INNER, D),
                        np.asarray(g["L1_ffn_shared_w2"]).T, np.zeros((HC * P - HIDDEN, D), np.float32)])
    a["w2"] = rows(w)
    return a


def kernel(**inputs):
    import concourse.bacc as bacc
    from concourse.bass_utils import run_bass_kernel_spmd

    nc = bacc.Bacc("TRN2", target_bir_lowering=False, num_devices=1)
    arrays, aps = {}, {}
    for name, a in layouts(inputs).items():
        arrays["in_" + name] = a
        aps[name] = nc.dram_tensor("in_" + name, a.shape, mybir.dt.from_np(a.dtype), kind="ExternalInput").ap()
    out = nc.dram_tensor("out", (P, NT, D), F32, kind="ExternalOutput").ap()
    decoder(nc, aps, out)
    r = run_bass_kernel_spmd(nc, [arrays], core_ids=[0])
    return np.asarray(r.results[0]["out"]).transpose(1, 0, 2).reshape(B, T, D)
```

```python
from contextlib import ExitStack

import numpy as np
import concourse.bass as bass
from concourse import mybir

F32 = mybir.dt.float32
BF16 = mybir.dt.bfloat16
I32 = mybir.dt.int32
I16 = mybir.dt.int16
U32 = mybir.dt.uint32
ALU = mybir.AluOpType
ACT = mybir.ActivationFunctionType
AX = mybir.AxisListType

P = 128
B, T, D = 4, 256, 256
N = B * T
NT = N // P
DC = D // P
HALF = 512
NH = N // HALF
LN_EPS = 1e-5
ROUND = 12582912.0


class Buffers:
    pass


class Chain:

    def __init__(self, engine, semaphore):
        self.engine, self.semaphore, self.count = engine, semaphore, 0

    def step(self, instruction):
        self.count += 1
        instruction.then_inc(self.semaphore, 1)
        self.engine.wait_ge(self.semaphore, self.count)


def scope(nc, ctx, prefix):
    def sb(name, shape, dt=F32):
        return ctx.enter_context(nc.sbuf_tensor(prefix + name, shape, dt))

    def ps(name, shape, dt=F32):
        return ctx.enter_context(nc.psum_tensor(prefix + name, shape, dt))

    def sem(name):
        return ctx.enter_context(nc.semaphore(prefix + name))
    return sb, ps, sem





def norm_semaphores(sem):
    ln = Buffers()
    ln.var_ready = sem("ln_var_ready")
    ln.rstd_ready = sem("ln_rstd_ready")
    ln.normed = sem("ln_normed")
    ln.turned_ready = sem("ln_turned_ready")
    ln.copied = sem("ln_copied")
    ln.norms = -1
    return ln


def norm_buffers(sb, ps, sh):
    ln = sh.ln
    ln.norms += 1
    ln.tiles = ln.norms * NT
    ln.stats = sb("ln_stats", [P, NT, 6])
    ln.mv = sb("ln_mv", [P, NT, 2])
    ln.rstd = sb("ln_rstd", [P, NT])
    ln.minus_half = sb("ln_minus_half", [P, NT])
    ln.xn = sb("ln_xn", [P, NT, D])
    ln.turned = ps("ln_turned", [P, 2, HALF])
    return ln


def norm_vector(nc, eng, ln, x, chain):
    for t in range(NT):
        last = nc.vector.bn_stats(ln.stats[:, t, :], x[:, t, :])
    chain.step(last)
    for t in range(NT):
        last = nc.vector.bn_aggr(ln.mv[:, t, :], ln.stats[:, t, :])
    chain.step(last)
    nc.vector.memset(ln.minus_half[:, :], -0.5)
    nc.vector.tensor_scalar(ln.rstd[:, :], ln.mv[:, :, 1], LN_EPS, None, ALU.add).then_inc(ln.var_ready, 1)
    eng.wait_ge(ln.rstd_ready, ln.norms + 1)
    for t in range(NT):
        nc.vector.tensor_scalar(ln.xn[:, t, :], x[:, t, :], ln.mv[:, t, 0:1], ln.rstd[:, t:t + 1],
                                ALU.subtract, ALU.mult).then_inc(ln.normed, 1)


def norm_pool(nc, pool, ln):
    pool.wait_ge(ln.var_ready, ln.norms + 1)
    nc.gpsimd.tensor_tensor(ln.rstd[:, :], ln.rstd[:, :], ln.minus_half[:, :], ALU.pow).then_inc(ln.rstd_ready, 1)


def norm_tensor(nc, pe, ln, ident):
    for t in range(NT):
        pe.wait_ge(ln.normed, ln.tiles + t + 1)
        if t >= 2:
            pe.wait_ge(ln.copied, ln.tiles + t - 1)
        for c in range(DC):
            last = nc.tensor.transpose(ln.turned[:, t % 2, c * P:(c + 1) * P], ln.xn[:, t, c * P:(c + 1) * P], ident[:, :])
        last.then_inc(ln.turned_ready, 1)


def norm_scalar(nc, act, ln, place):
    for t in range(NT):
        act.wait_ge(ln.turned_ready, ln.tiles + t + 1)
        nc.scalar.copy(place(t), ln.turned[:, t % 2, 0:D].rearrange("p (c n) -> p c n", c=DC)).then_inc(ln.copied, 1)



def start_stage(nc, x, ident, x_dram):
    with ExitStack() as ctx:
        sb, ps, sem = scope(nc, ctx, "st_")
        loaded, zeroed = sem("loaded"), sem("zeroed")
        block = ctx.enter_context(nc.Block())

        @block.sync
        def _(sp):
            sp.dma_start(x[:, :, :], x_dram).then_inc(loaded, 16)
            sp.wait_ge(loaded, 16)

        @block.gpsimd
        def _(pool):
            nc.gpsimd.memset(ident[:, :], 0.0).then_inc(zeroed, 1)
            pool.wait_ge(zeroed, 1)
            nc.gpsimd.affine_select(out=ident[:, :], in_=ident[:, :], compare_op=ALU.not_equal, fill=1.0,
                                    base=0, pattern=[[-1, P]], channel_multiplier=1).then_inc(zeroed, 1)
            pool.wait_ge(zeroed, 2)



HEADS0 = 16
HD0 = D // HEADS0
DEN_LEAST = 1e-6
KEY, VALUE, QUERY = range(3)


def linear_attention(nc, sh, w_qkv_dram, w_out_dram, decay_dram):
    x, xT, ident = sh.x, sh.xT, sh.ident
    with ExitStack() as ctx:
        sb, ps, sem = scope(nc, ctx, "a0_")
        ln = norm_buffers(sb, ps, sh)
        w_qkv, w_out = sb("w_qkv", [P, DC, 3 * D]), sb("w_out", [P, DC, D])
        decay = sb("decay", [P, DC])
        gain = sb("gain", [P, DC, N])
        same_head = sb("same_head", [P, P])
        exps, relus = sb("exps", [P, 4, HALF]), sb("relus", [P, 4, HALF])
        q, k, kv = sb("q", [P, DC, N]), sb("k", [P, DC, N]), sb("kv", [P, DC, N])
        run_k, run_kv = sb("run_k", [P, DC, N]), sb("run_kv", [P, DC, N])
        proj = ps("proj", [P, 4, HALF])
        sums = ps("sums", [P, 2, HALF])
        out = proj
        loaded, dve_steps, consts = sem("loaded"), sem("dve_steps"), sem("consts")
        decay_exp, projected = sem("decay_exp"), sem("projected")
        phi_parts, phi_done, kv_done = sem("phi_parts"), sem("phi_done"), sem("kv_done")
        scanned, qk_ready, sums_ready, sums_used = sem("scanned"), sem("qk_ready"), sem("sums_ready"), sem("sums_used")
        qkv_ready, heads_ready = sem("qkv_ready"), sem("heads_ready")
        out_ready, out_added = sem("out_ready"), sem("out_added")
        groups = [(c, kind, h) for c in range(DC) for kind in (KEY, VALUE, QUERY) for h in range(NH)]
        column = {KEY: D, VALUE: 2 * D, QUERY: 0}

        def phis(n):
            return sum(kind != VALUE for _, kind, _ in groups[:n])

        block = ctx.enter_context(nc.Block())

        @block.sync
        def _(sp):
            sp.dma_start(w_qkv[:, :, :], w_qkv_dram).then_inc(loaded, 16)
            sp.dma_start(decay[:, :], decay_dram).then_inc(loaded, 16)
            sp.dma_start(w_out[:, :, :], w_out_dram).then_inc(loaded, 16)

        @block.gpsimd
        def _(pool):
            norm_pool(nc, pool, ln)
            view = same_head[:, :].rearrange("p (h d) -> p h d", d=HD0)
            nc.gpsimd.memset(same_head[:, :], 1.0).then_inc(consts, 1)
            pool.wait_ge(consts, 1)
            nc.gpsimd.affine_select(out=view, in_=view, compare_op=ALU.is_ge, fill=0.0, base=0,
                                    pattern=[[-HD0, P // HD0], [0, HD0]], channel_multiplier=1).then_inc(consts, 1)
            pool.wait_ge(consts, 2)
            nc.gpsimd.affine_select(out=view, in_=view, compare_op=ALU.is_ge, fill=0.0, base=HD0 - 1,
                                    pattern=[[HD0, P // HD0], [0, HD0]], channel_multiplier=-1).then_inc(consts, 1)
            nc.gpsimd.memset(gain[:, :, :], 1.0).then_inc(consts, 1)
            pool.wait_ge(consts, 4)
            nc.gpsimd.memset(gain[:, :, :].rearrange("p c (b t) -> p (c b) t", t=T)[:, :, 0:1], 0.0).then_inc(consts, 1)
            for c in range(DC):
                pool.wait_ge(scanned, c + 1)
                nc.gpsimd.tensor_tensor(kv[:, c, :], q[:, c, :], run_kv[:, c, :], ALU.mult).then_inc(qkv_ready, 1)

        @block.tensor
        def _(pe):
            norm_tensor(nc, pe, ln, ident)
            pe.wait_ge(loaded, 48)
            pe.wait_ge(ln.copied, ln.tiles + NT)
            for i, (c, kind, h) in enumerate(groups):
                if i >= 4:
                    pe.wait_ge(phi_parts, phis(i - 3))
                    if i - 3 > phis(i - 3):
                        pe.wait_ge(kv_done, i - 3 - phis(i - 3))
                for d in range(DC):
                    f = column[kind] + c * P
                    last = nc.tensor.matmul(proj[:, i % 4, :], w_qkv[:, d, f:f + P],
                                            xT[:, d, h * HALF:(h + 1) * HALF], start=(d == 0), stop=(d == DC - 1))
                last.then_inc(projected, 1)
            pe.wait_ge(consts, 3)
            for c in range(DC):
                pe.wait_ge(qk_ready, c + 1)
                for h in range(NH):
                    i = c * NH + h
                    if i >= 2:
                        pe.wait_ge(sums_used, i - 1)
                    nc.tensor.matmul(sums[:, i % 2, :], same_head[:, :], k[:, c, h * HALF:(h + 1) * HALF],
                                     start=True, stop=True).then_inc(sums_ready, 1)
            pe.wait_ge(heads_ready, DC)
            for t in range(NT):
                if t >= 2:
                    pe.wait_ge(out_added, t - 1)
                for c in range(DC):
                    last = nc.tensor.matmul(out[:, t % 2, 0:D], q[:, c, t * P:(t + 1) * P], w_out[:, c, :],
                                            start=(c == 0), stop=(c == DC - 1))
                last.then_inc(out_ready, 1)

        @block.scalar
        def _(act):
            norm_scalar(nc, act, ln, lambda t: xT[:, :, t * P:(t + 1) * P])
            act.wait_ge(loaded, 48)
            nc.scalar.activation(decay[:, :], decay[:, :], ACT.Exp, scale=-1.0).then_inc(decay_exp, 1)
            n = 0
            for i, (c, kind, h) in enumerate(groups):
                if kind == VALUE:
                    continue
                act.wait_ge(projected, i + 1)
                if n >= 4:
                    act.wait_ge(phi_done, n - 3)
                nc.scalar.activation(exps[:, n % 4, :], proj[:, i % 4, :], ACT.Exp)
                nc.scalar.activation(relus[:, n % 4, :], proj[:, i % 4, :], ACT.Relu).then_inc(phi_parts, 1)
                n += 1

        @block.vector
        def _(dve):
            chain = Chain(dve, dve_steps)
            norm_vector(nc, dve, ln, x, chain)
            dve.wait_ge(decay_exp, 1)
            chain.step(nc.vector.tensor_scalar(decay[:, :], decay[:, :], 1.0, None, ALU.add))
            chain.step(nc.vector.reciprocal(decay[:, :], decay[:, :]))
            dve.wait_ge(consts, 5)
            for c in range(DC):
                last = nc.vector.tensor_scalar(gain[:, c, :], gain[:, c, :], decay[:, c:c + 1], None, ALU.mult)
            chain.step(last)
            n = 0
            for i, (c, kind, h) in enumerate(groups):
                at = slice(h * HALF, (h + 1) * HALF)
                if kind == VALUE:
                    dve.wait_ge(projected, i + 1)
                    dve.wait_ge(phi_done, n)
                    nc.vector.tensor_tensor(kv[:, c, at], proj[:, i % 4, :], k[:, c, at], ALU.mult).then_inc(kv_done, 1)
                    continue
                dve.wait_ge(phi_parts, n + 1)
                nc.vector.scalar_tensor_tensor((k if kind == KEY else q)[:, c, at], exps[:, n % 4, :], 1.0,
                                               relus[:, n % 4, :], ALU.min, ALU.add).then_inc(phi_done, 1)
                n += 1
                if kind == QUERY and h == NH - 1:
                    dve.wait_ge(kv_done, NH * (c + 1))
                    dve.wait_ge(phi_done, n)
                    nc.vector.tensor_tensor_scan(run_k[:, c, :], gain[:, c, :], k[:, c, :], 0.0, ALU.mult, ALU.add)
                    chain.step(nc.vector.tensor_tensor_scan(run_kv[:, c, :], gain[:, c, :], kv[:, c, :], 0.0,
                                                            ALU.mult, ALU.add))
                    dve.sem_inc(scanned, 1)
                    nc.vector.tensor_tensor(k[:, c, :], q[:, c, :], run_k[:, c, :], ALU.mult).then_inc(qk_ready, 1)
            for c in range(DC):
                dve.wait_ge(qkv_ready, c + 1)
                dve.wait_ge(qk_ready, c + 1)
                for h in range(NH):
                    i = c * NH + h
                    at = slice(h * HALF, (h + 1) * HALF)
                    dve.wait_ge(sums_ready, i + 1)
                    nc.vector.tensor_scalar(run_k[:, c, at], sums[:, i % 2, :], DEN_LEAST, None, ALU.max).then_inc(sums_used, 1)
                    dve.wait_ge(sums_used, i + 1)
                    chain.step(nc.vector.reciprocal(run_k[:, c, at], run_k[:, c, at]))
                    last = nc.vector.tensor_tensor(q[:, c, at], kv[:, c, at], run_k[:, c, at], ALU.mult)
                last.then_inc(heads_ready, 1)
            for t in range(NT):
                dve.wait_ge(out_ready, t + 1)
                nc.vector.tensor_tensor(x[:, t, :], x[:, t, :], out[:, t % 2, 0:D], ALU.add).then_inc(out_added, 1)



EXPERTS_T = 4
PER_EXPERT = 12500 // EXPERTS_T


def token_experts(nc, sh, ids_dram, ctxT_dram):
    x, xT, ident, ctxT = sh.x, sh.xT, sh.ident, sh.ctxT
    with ExitStack() as ctx:
        sb, ps, sem = scope(nc, ctx, "m0_")
        ln = norm_buffers(sb, ps, sh)
        ids, idf = sb("ids", [P, N], I32), sb("idf", [P, N])
        mask = sb("mask", [P, EXPERTS_T, N])
        own = sb("own", [P, EXPERTS_T, DC, N])
        hid = sb("hid", [P, EXPERTS_T, DC, N])
        up = ps("up", [P, 4, HALF])
        out = ps("out", [P, 2, HALF])
        loaded, dve_steps, masks_ready, own_ready = sem("loaded"), sem("dve_steps"), sem("masks_ready"), sem("own_ready")
        up_ready, silu_ready, hid_ready, out_ready, out_added = (
            sem("up_ready"), sem("silu_ready"), sem("hid_ready"), sem("out_ready"), sem("out_added"))
        groups = [(e, f, h) for e in range(EXPERTS_T) for f in range(DC) for h in range(NH)]
        block = ctx.enter_context(nc.Block())

        @block.sync
        def _(sp):
            sp.dma_start(ids[:, :], ids_dram.broadcast_to([P, N])).then_inc(loaded, 16)
            sp.dma_start(ctxT[:, :, :], ctxT_dram).then_inc(loaded, 16)

        @block.gpsimd
        def _(pool):
            norm_pool(nc, pool, ln)
            for e in range(EXPERTS_T):
                pool.wait_ge(masks_ready, e + 1)
                pool.wait_ge(ln.copied, ln.tiles + NT)
                for c in range(DC):
                    last = nc.gpsimd.tensor_tensor(own[:, e, c, :], xT[:, c, :], mask[:, e, :], ALU.mult)
                last.then_inc(own_ready, 1)

        @block.tensor
        def _(pe):
            norm_tensor(nc, pe, ln, ident)
            pe.wait_ge(loaded, 32)
            for i, (e, f, h) in enumerate(groups):
                pe.wait_ge(own_ready, e + 1)
                if i >= 4:
                    pe.wait_ge(hid_ready, i - 3)
                for d in range(DC):
                    last = nc.tensor.matmul(up[:, i % 4, :], ctxT[:, d, e * D + f * P:e * D + (f + 1) * P],
                                            own[:, e, d, h * HALF:(h + 1) * HALF], start=(d == 0), stop=(d == DC - 1))
                last.then_inc(up_ready, 1)
            pe.wait_ge(hid_ready, len(groups))
            for t in range(NT):
                if t >= 2:
                    pe.wait_ge(out_added, t - 1)
                for e in range(EXPERTS_T):
                    for f in range(DC):
                        last = nc.tensor.matmul(out[:, t % 2, 0:D], hid[:, e, f, t * P:(t + 1) * P],
                                                ctxT[:, f, e * D:(e + 1) * D], start=(e == f == 0),
                                                stop=(e == EXPERTS_T - 1 and f == DC - 1))
                last.then_inc(out_ready, 1)

        @block.scalar
        def _(act):
            norm_scalar(nc, act, ln, lambda t: xT[:, :, t * P:(t + 1) * P])
            for i, (e, f, h) in enumerate(groups):
                act.wait_ge(up_ready, i + 1)
                nc.scalar.activation(hid[:, e, f, h * HALF:(h + 1) * HALF], up[:, i % 4, :], ACT.Silu).then_inc(silu_ready, 1)

        @block.vector
        def _(dve):
            chain = Chain(dve, dve_steps)
            norm_vector(nc, dve, ln, x, chain)
            dve.wait_ge(loaded, 32)
            chain.step(nc.vector.tensor_copy(idf[:, :], ids[:, :]))
            for e in range(EXPERTS_T):
                if e == 0:
                    nc.vector.tensor_scalar(mask[:, e, :], idf[:, :], float(PER_EXPERT), None, ALU.is_lt).then_inc(masks_ready, 1)
                elif e == EXPERTS_T - 1:
                    nc.vector.tensor_scalar(mask[:, e, :], idf[:, :], float(e * PER_EXPERT), None, ALU.is_ge).then_inc(masks_ready, 1)
                else:
                    chain.step(nc.vector.tensor_scalar(mask[:, e, :], idf[:, :], float(e * PER_EXPERT), None, ALU.is_ge))
                    nc.vector.scalar_tensor_tensor(mask[:, e, :], idf[:, :], float((e + 1) * PER_EXPERT), mask[:, e, :],
                                                   ALU.is_lt, ALU.mult).then_inc(masks_ready, 1)
            for i, (e, f, h) in enumerate(groups):
                at = slice(h * HALF, (h + 1) * HALF)
                dve.wait_ge(silu_ready, i + 1)
                nc.vector.tensor_tensor(hid[:, e, f, at], up[:, i % 4, :], hid[:, e, f, at], ALU.mult).then_inc(hid_ready, 1)
            for t in range(NT):
                dve.wait_ge(out_ready, t + 1)
                nc.vector.tensor_tensor(x[:, t, :], x[:, t, :], out[:, t % 2, 0:D], ALU.add).then_inc(out_added, 1)


HEADS_R = 8
TOP = 8
RETR = 64
KEYS = 45
PAIRS = KEYS * KEYS
SIDE = HEADS_R * KEYS
UP = 1024
UC = UP // P
PB = (PAIRS + P - 1) // P
LAST = PAIRS - (PB - 1) * P
UNITS = NT * HEADS_R
BATCH = 4


def retrieval(nc, sh, i):
    with ExitStack() as ctx:
        sb, ps, sem = scope(nc, ctx, "r0_")
        r = Buffers()
        r.hT = sb("hT", [P, N])
        r.to_sims = sb("to_sims", [P, 2 * SIDE])
        r.down = sb("down", [P, PB * P])
        r.up = sb("up", [P, PB, D])
        r.loaded = sem("tables_loaded")
        private_state(nc, sh, r, i)
        weigh_experts(nc, sh, r)


def private_state(nc, sh, r, i):
    x, xT, ident = sh.x, sh.xT, sh.ident
    with ExitStack() as ctx:
        sb, ps, sem = scope(nc, ctx, "r1_")
        ln = norm_buffers(sb, ps, sh)
        w_up, b_up = sb("w_up", [P, DC, UP]), sb("b_up", [P, UC])
        w_down, b_down = sb("w_down", [P, UC, P]), sb("b_down", [P, 1])
        w_q, keys = sb("w_q", [P, UC, P]), sb("keys", [P, UC, 2, KEYS])
        wide = sb("wide", [P, UC, N])
        up = ps("up", [P, 4, HALF])
        low = ps("low", [P, 2, HALF])
        loaded, dve_steps, zeroed, keys_loaded = sem("loaded"), sem("dve_steps"), sem("zeroed"), sem("keys_loaded")
        sims_ready, up_ready, silu_ready, low_ready, done = (
            sem("sims_ready"), sem("up_ready"), sem("silu_ready"), sem("low_ready"), sem("done"))
        copied = sem("copied")
        groups = [(c, h) for c in range(UC) for h in range(NH)]
        block = ctx.enter_context(nc.Block())

        @block.sync
        def _(sp):
            for dst, src in ((w_up[:, :, :], "w_up"), (b_up[:, :], "b_up"), (w_q[:, :, :], "w_q"),
                             (w_down[:, :, :], "w_down"), (b_down[:, :], "b_down")):
                sp.dma_start(dst, i[src]).then_inc(loaded, 16)
            sp.wait_ge(zeroed, 1)
            for j in range(2):
                sp.dma_start(keys[j * RETR:(j + 1) * RETR, :, j, :], i["keys"][j]).then_inc(keys_loaded, 16)
            sp.dma_start(r.down[:, :], i["down"]).then_inc(r.loaded, 16)
            sp.dma_start(r.up[:, :, :], i["up"]).then_inc(r.loaded, 16)

        @block.gpsimd
        def _(pool):
            nc.gpsimd.memset(keys[:, :, :, :], 0.0).then_inc(zeroed, 1)
            norm_pool(nc, pool, ln)

        @block.tensor
        def _(pe):
            norm_tensor(nc, pe, ln, ident)
            pe.wait_ge(loaded, 80)
            pe.wait_ge(keys_loaded, 32)
            pe.wait_ge(ln.copied, ln.tiles + NT)
            for n, (c, h) in enumerate(groups):
                if n == len(groups) - 2:
                    for c in range(UC):
                        last = nc.tensor.matmul(low[:, c // 4, (c % 4) * 2 * KEYS:(c % 4 + 1) * 2 * KEYS], w_q[:, c, :],
                                                keys[:, c, :, :].rearrange("p j k -> p (j k)"), start=True, stop=True)
                    last.then_inc(sims_ready, 1)
                if n >= 4:
                    pe.wait_ge(silu_ready, n - 3)
                for d in range(DC):
                    last = nc.tensor.matmul(up[:, n % 4, :], w_up[:, d, c * P:(c + 1) * P],
                                            xT[:, d, h * HALF:(h + 1) * HALF], start=(d == 0), stop=(d == DC - 1))
                last.then_inc(up_ready, 1)
            pe.wait_ge(silu_ready, len(groups))
            pe.wait_ge(copied, 1)
            for h in range(NH):
                for c in range(UC):
                    last = nc.tensor.matmul(low[:, h, :], w_down[:, c, :], wide[:, c, h * HALF:(h + 1) * HALF],
                                            start=(c == 0), stop=(c == UC - 1))
                last.then_inc(low_ready, 1)

        @block.scalar
        def _(act):
            norm_scalar(nc, act, ln, lambda t: xT[:, :, t * P:(t + 1) * P])
            act.wait_ge(loaded, 80)
            for n, (c, h) in enumerate(groups):
                act.wait_ge(up_ready, n + 1)
                nc.scalar.activation(wide[:, c, h * HALF:(h + 1) * HALF], up[:, n % 4, :], ACT.Silu,
                                     bias=b_up[:, c:c + 1]).then_inc(silu_ready, 1)

        @block.vector
        def _(dve):
            chain = Chain(dve, dve_steps)
            norm_vector(nc, dve, ln, x, chain)
            dve.wait_ge(sims_ready, 1)
            nc.vector.tensor_copy(r.to_sims[:, :].rearrange("p (s n) -> p s n", s=2), low[:, :, 0:SIDE]).then_inc(copied, 1)
            dve.wait_ge(loaded, 80)
            for h in range(NH):
                dve.wait_ge(low_ready, h + 1)
                nc.vector.tensor_scalar(r.hT[:, h * HALF:(h + 1) * HALF], low[:, h, :], b_down[:, 0:1], None,
                                        ALU.add).then_inc(done, 1)


def weigh_experts(nc, sh, r):
    x, ident = sh.x, sh.ident
    with ExitStack() as ctx:
        sb, ps, sem = scope(nc, ctx, "r2_")
        RING = 10
        sims = sb("sims", [P, NT, 2 * SIDE])
        pair_sum = sb("pair_sum", [P, 3, PAIRS])
        sums = [pair_sum[:, k, :] for k in range(3)] + [a[:, :, :].rearrange("p c n -> p (c n)")[:, 0:PAIRS] for a in (sh.xT, sh.ctxT)]
        SUMS = len(sums)
        w = sb("w", [P, RING, PAIRS])
        wT = sb("wT", [P, PB, P])
        best = sb("best", [P, 2, HEADS_R, TOP])
        grid = sb("grid", [P, HEADS_R, TOP * TOP])
        kept = sb("kept", [P, 2, HEADS_R, TOP])
        neg_max = sb("neg_max", [P, 2, HEADS_R])
        below_max = sb("below_max", [P, HEADS_R, TOP])
        kept_exp = sb("kept_exp", [P, HEADS_R, TOP])
        scale = sb("scale", [P, 2, HEADS_R])
        head_sum = ps("head_sum", [P, 4, HALF])
        z = ps("z", [P, 4, HALF])
        dve_steps = sem("dve_steps")
        sims_ready, sims_copied, z_ready = sem("sims_ready"), sem("sims_copied"), sem("z_ready")
        best_ready, kept_ready, scale_ready = sem("best_ready"), sem("kept_ready"), sem("scale_ready")
        summed_pairs, exp_done, masked, weighted, silu_done, summed = (
            sem("summed_pairs"), sem("exp_done"), sem("masked"), sem("weighted"), sem("silu_done"), sem("summed"))
        wT_copied, out_ready, out_added = sem("wT_copied"), sem("out_ready"), sem("out_added")
        block = ctx.enter_context(nc.Block())

        @block.gpsimd
        def _(pool):
            for u in range(UNITS):
                t, h = divmod(u, HEADS_R)
                if h == 0:
                    pool.wait_ge(sims_copied, t + 1)
                if u >= SUMS:
                    pool.wait_ge(masked, u - SUMS + 1)
                a = sims[:, t, h * KEYS:(h + 1) * KEYS].rearrange("p (a o) -> p a o", o=1)
                b = sims[:, t, SIDE + h * KEYS:SIDE + (h + 1) * KEYS].rearrange("p (o b) -> p o b", o=1)
                nc.gpsimd.tensor_tensor(sums[u % SUMS].rearrange("p (a b) -> p a b", b=KEYS),
                                        a.broadcast_to([P, KEYS, KEYS]), b.broadcast_to([P, KEYS, KEYS]),
                                        ALU.add).then_inc(summed_pairs, 1)

        @block.tensor
        def _(pe):
            pe.wait_ge(r.loaded, 32)

            def projections(t):
                pe.wait_ge(weighted, HEADS_R * t) if t >= 1 else pe.wait_ge(sims_copied, NT)
                for j in range(4):
                    lo, hi = j * HALF, min((j + 1) * HALF, PAIRS)
                    last = nc.tensor.matmul(z[:, j, 0:hi - lo], r.hT[:, t * P:(t + 1) * P], r.down[:, lo:hi],
                                            start=True, stop=True)
                last.then_inc(z_ready, 1)

            def output(t):
                pe.wait_ge(wT_copied, t + 1)
                for b in range(PB):
                    k = P if b < PB - 1 else LAST
                    last = nc.tensor.matmul(head_sum[:, 0, 0:D], wT[0:k, b, :], r.up[0:k, b, :],
                                            start=(b == 0), stop=(b == PB - 1))
                last.then_inc(out_ready, 1)

            for t in range(NT):
                if t >= 2:
                    pe.wait_ge(sims_copied, t - 1)
                for s in range(2):
                    last = nc.tensor.matmul(z[:, t % 2 * 2 + s, 0:SIDE], r.hT[:, t * P:(t + 1) * P],
                                            r.to_sims[:, s * SIDE:(s + 1) * SIDE], start=True, stop=True)
                last.then_inc(sims_ready, 1)
            projections(0)
            for u in range(UNITS):
                t, h = divmod(u, HEADS_R)
                if h == 2 and t + 1 < NT:
                    projections(t + 1)
                pe.wait_ge(silu_done, u + 1)
                if h == 0 and t >= 1:
                    pe.wait_ge(out_added, t)
                for b in range(PB):
                    m = P if b < PB - 1 else LAST
                    last = nc.tensor.matmul(head_sum[0:m, b // 4, (b % 4) * P:(b % 4 + 1) * P],
                                            w[:, u % RING, b * P:b * P + m], ident[:, :],
                                            start=(h == 0 and b % 4 == 0), stop=(h == HEADS_R - 1), skip_group_check=True)
                last.then_inc(summed, 1)
                if h == HEADS_R - 1:
                    output(t)

        @block.scalar
        def _(act):
            def exp_kept(t):
                act.wait_ge(best_ready, t + 1)
                if t >= 1:
                    act.wait_ge(scale_ready, t)
                nc.scalar.activation(kept_exp[:, :, :], below_max[:, :, :], ACT.Exp).then_inc(kept_ready, 1)

            def exps(g):
                for u in range(BATCH * g, BATCH * (g + 1)):
                    t, h = divmod(u, HEADS_R)
                    act.wait_ge(summed_pairs, u + 1)
                    if u >= RING:
                        act.wait_ge(summed, u - RING + 1)
                    nc.scalar.activation(w[:, u % RING, :], sums[u % SUMS], ACT.Exp,
                                         bias=neg_max[:, t % 2, h:h + 1]).then_inc(exp_done, 1)

            def silus(g):
                for u in range(BATCH * g, BATCH * (g + 1)):
                    act.wait_ge(weighted, u + 1)
                    nc.scalar.activation(w[:, u % RING, :], w[:, u % RING, :], ACT.Silu).then_inc(silu_done, 1)

            for t in range(NT):
                act.wait_ge(sims_ready, t + 1)
                nc.scalar.copy(sims[:, t, :].rearrange("p (s n) -> p s n", s=2),
                               z[:, t % 2 * 2:t % 2 * 2 + 2, 0:SIDE]).then_inc(sims_copied, 1)
            exp_kept(0)
            exps(0)
            exps(1)
            for t in range(NT):
                silus(2 * t)
                if t + 1 < NT:
                    exp_kept(t + 1)
                    exps(2 * t + 2)
                silus(2 * t + 1)
                if t + 1 < NT:
                    exps(2 * t + 3)
                act.wait_ge(summed, HEADS_R * (t + 1))
                if t >= 1:
                    act.wait_ge(out_ready, t)
                nc.scalar.copy(wT[:, 0:PB - 1, :].rearrange("p b n -> p (b n)"),
                               head_sum[:, :, :].rearrange("p a b -> p (a b)")[:, 0:(PB - 1) * P])
                nc.scalar.copy(wT[0:LAST, PB - 1, :], head_sum[0:LAST, 3, 3 * P:4 * P]).then_inc(wT_copied, 1)

        @block.vector
        def _(dve):
            chain = Chain(dve, dve_steps)

            def choose(t):
                dve.wait_ge(sims_copied, t + 1)
                for s in range(2):
                    for h in range(HEADS_R):
                        at = s * SIDE + h * KEYS
                        last = nc.vector.max(best[:, s, h, :], sims[:, t, at:at + KEYS])
                chain.step(last)
                a = best[:, 0, :, :].rearrange("p h (a o) -> p h a o", o=1).broadcast_to([P, HEADS_R, TOP, TOP])
                b = best[:, 1, :, :].rearrange("p h (o b) -> p h o b", o=1).broadcast_to([P, HEADS_R, TOP, TOP])
                chain.step(nc.vector.tensor_tensor(grid[:, :, :].rearrange("p h (a b) -> p h a b", b=TOP), a, b, ALU.add))
                for h in range(HEADS_R):
                    last = nc.vector.max(kept[:, t % 2, h, :], grid[:, h, :])
                chain.step(last)
                if t >= 1:
                    dve.wait_ge(kept_ready, t)
                nc.vector.tensor_scalar(neg_max[:, t % 2, :], kept[:, t % 2, :, 0], -1.0, None, ALU.mult)
                top = kept[:, t % 2, :, 0:1].broadcast_to([P, HEADS_R, TOP])
                nc.vector.tensor_tensor(below_max[:, :, :], kept[:, t % 2, :, :], top, ALU.subtract).then_inc(best_ready, 1)

            def scales(t):
                dve.wait_ge(kept_ready, t + 1)
                chain.step(nc.vector.tensor_reduce(scale[:, t % 2, :], kept_exp[:, :, :], AX.X, ALU.add))
                chain.step(nc.vector.reciprocal(scale[:, t % 2, :], scale[:, t % 2, :]))
                dve.sem_inc(scale_ready, 1)

            def mask(u):
                t, h = divmod(u, HEADS_R)
                dve.wait_ge(exp_done, u + 1)
                nc.vector.scalar_tensor_tensor(w[:, u % RING, :], sums[u % SUMS], kept[:, t % 2, h, TOP - 1:TOP],
                                               w[:, u % RING, :], ALU.is_ge, ALU.mult).then_inc(masked, 1)

            def weigh(u):
                t, h = divmod(u, HEADS_R)
                if h == 0:
                    scales(t)
                    dve.wait_ge(z_ready, t + 1)
                dve.wait_ge(masked, u + 1)
                nc.vector.scalar_tensor_tensor(w[:, u % RING, :], w[:, u % RING, :], scale[:, t % 2, h:h + 1],
                                               z[:, :, :].rearrange("p a b -> p (a b)")[:, 0:PAIRS],
                                               ALU.mult, ALU.mult).then_inc(weighted, 1)

            def residual(t):
                dve.wait_ge(out_ready, t + 1)
                nc.vector.tensor_tensor(x[:, t, :], x[:, t, :], head_sum[:, 0, 0:D], ALU.add).then_inc(out_added, 1)

            choose(0)
            for u in range(UNITS):
                t, h = divmod(u, HEADS_R)
                mask(u)
                if u >= 1:
                    weigh(u - 1)
                if h == 1 and t + 1 < NT:
                    choose(t + 1)
                if h == 6 and t >= 1:
                    residual(t - 1)
            weigh(UNITS - 1)
            residual(NT - 1)


TAPS = 3
WIDTH = 64
HEADS_B = 8
HD_B = 64
BLOCK = T // 16
WIDE_B = HEADS_B * HD_B
CB = WIDE_B // P
MASKED = -1e9


def block_attention(nc, sh, i):
    with ExitStack() as ctx:
        sb, ps, sem = scope(nc, ctx, "b0_")
        s = Buffers()
        s.qh = sb("qh", [P, CB, N])
        s.kh = sb("kh", [P, CB, N])
        s.vh = sb("vh", [P, NT, WIDE_B])
        s.w_o = sb("w_o", [P, CB, WIDTH])
        s.b_o = sb("b_o", [WIDTH, 1])
        s.proj = sb("proj", [WIDTH + 1, D])
        s.mask = sb("mask", [P, P])
        s.loaded = sem("out_loaded")
        convolve(nc, sh, s, i)
        attend_in_blocks(nc, sh, s)


def convolve(nc, sh, s, i):
    x, ident = sh.x, sh.ident
    with ExitStack() as ctx:
        sb, ps, sem = scope(nc, ctx, "b1_")
        ln = norm_buffers(sb, ps, sh)
        PADDED = T + TAPS - 1
        padded = sb("padded", [P, DC, B, PADDED])
        conv_w, conv_b = sb("conv_w", [P, TAPS, DC, 3 * WIDTH]), sb("conv_b", [P, 2])
        w_qk, b_q, b_k = sb("w_qk", [P, WIDE_B]), sb("b_q", [P, CB]), sb("b_k", [P, CB])
        w_v = sb("w_v", [WIDTH + 1, WIDE_B])
        qk, v = sb("qk", [P, N]), sb("v", [WIDTH + 1, N])
        acc = ps("acc", [P, 6, HALF])
        loaded, dve_steps, zeroed, mask_steps = sem("loaded"), sem("dve_steps"), sem("zeroed"), sem("mask_steps")
        conv_ready, conv_taken, heads_ready, heads_taken = (
            sem("conv_ready"), sem("conv_taken"), sem("heads_ready"), sem("heads_taken"))
        v_heads_ready, v_heads_taken = sem("v_heads_ready"), sem("v_heads_taken")
        loads = ((conv_w[:, :, :, :], "conv_w"), (conv_b[:, :], "conv_b"), (w_qk[:, :], "w_qk"), (b_q[:, :], "b_q"),
                 (b_k[:, :], "b_k"), (w_v[:, :], "w_v"))
        block = ctx.enter_context(nc.Block())

        @block.sync
        def _(sp):
            for dst, src in loads:
                sp.dma_start(dst, i[src]).then_inc(loaded, 16)
            for dst, src in ((s.w_o[:, :, :], "w_o"), (s.b_o[:, :], "b_o"), (s.proj[:, :], "proj")):
                sp.dma_start(dst, i[src]).then_inc(s.loaded, 16)

        @block.gpsimd
        def _(pool):
            nc.gpsimd.memset(padded[:, :, :, 0:TAPS - 1], 0.0).then_inc(zeroed, 1)
            pool.wait_ge(zeroed, 1)
            nc.gpsimd.memset(v[WIDTH:WIDTH + 1, :], 1.0).then_inc(zeroed, 1)
            pool.wait_ge(zeroed, 2)
            norm_pool(nc, pool, ln)
            nc.gpsimd.memset(s.mask[:, :], 0.0).then_inc(mask_steps, 1)
            pool.wait_ge(mask_steps, 1)
            nc.gpsimd.affine_select(out=s.mask[:, :], in_=s.mask[:, :], compare_op=ALU.is_ge, fill=MASKED, base=0,
                                    pattern=[[-1, P]], channel_multiplier=1).then_inc(mask_steps, 1)
            pool.wait_ge(mask_steps, 2)
            view = s.mask[:, :].rearrange("p (g k) -> p g k", k=BLOCK)
            nc.gpsimd.affine_select(out=view, in_=view, compare_op=ALU.is_ge, fill=MASKED, base=BLOCK - 1,
                                    pattern=[[BLOCK, P // BLOCK], [0, BLOCK]], channel_multiplier=-1).then_inc(mask_steps, 1)

        @block.tensor
        def _(pe):
            norm_tensor(nc, pe, ln, ident)
            pe.wait_ge(loaded, 16 * len(loads))
            pe.wait_ge(zeroed, 2)
            pe.wait_ge(ln.copied, ln.tiles + NT)
            for part, m in ((0, 2 * WIDTH), (1, WIDTH)):
                for h in range(NH):
                    for n in range(TAPS * DC):
                        j, d = divmod(n, DC)
                        last = nc.tensor.matmul(
                            acc[0:m, 2 * part + h, :].rearrange("p (b t) -> p b t", t=T),
                            conv_w[:, j, d, part * 2 * WIDTH:part * 2 * WIDTH + m],
                            padded[:, d, 2 * h:2 * h + 2, j:j + T], start=(n == 0), stop=(n == TAPS * DC - 1))
                    last.then_inc(conv_ready, 1)
            n = 0
            for h in range(NH):
                pe.wait_ge(conv_taken, h + 1)
                for c in range(CB):
                    for which in range(2):
                        if n >= 2:
                            pe.wait_ge(heads_taken, n - 1)
                        at = slice(which * WIDTH, (which + 1) * WIDTH)
                        nc.tensor.matmul(acc[:, 4 + n % 2, :], w_qk[at, c * P:(c + 1) * P], qk[at, h * HALF:(h + 1) * HALF],
                                         start=True, stop=True).then_inc(heads_ready, 1)
                        n += 1
            pe.wait_ge(conv_taken, 2 * NH)
            for t in range(NT):
                if t >= 2:
                    pe.wait_ge(v_heads_taken, t - 1)
                nc.tensor.matmul(acc[:, t % 2, :], v[:, t * P:(t + 1) * P], w_v[:, :], start=True, stop=True).then_inc(v_heads_ready, 1)

        @block.scalar
        def _(act):
            norm_scalar(nc, act, ln, lambda t: padded[:, :, t * P // T, TAPS - 1 + t * P % T:TAPS - 1 + t * P % T + P])
            for t in range(NT):
                act.wait_ge(v_heads_ready, t + 1)
                nc.scalar.copy(s.vh[:, t, :], acc[:, t % 2, :]).then_inc(v_heads_taken, 1)

        @block.vector
        def _(dve):
            chain = Chain(dve, dve_steps)
            norm_vector(nc, dve, ln, x, chain)
            dve.wait_ge(loaded, 16 * len(loads))
            for h in range(NH):
                dve.wait_ge(conv_ready, h + 1)
                nc.vector.tensor_scalar(qk[:, h * HALF:(h + 1) * HALF], acc[:, h, :], conv_b[:, 0:1], None,
                                        ALU.add).then_inc(conv_taken, 1)
            for h in range(NH):
                dve.wait_ge(conv_ready, NH + h + 1)
                nc.vector.tensor_scalar(v[0:WIDTH, h * HALF:(h + 1) * HALF], acc[0:WIDTH, 2 + h, :], conv_b[0:WIDTH, 1:2],
                                        None, ALU.add).then_inc(conv_taken, 1)
            n = 0
            for h in range(NH):
                for c in range(CB):
                    for dst, bias, scale in ((s.qh, b_q, HD_B ** -0.5), (s.kh, b_k, 1.0)):
                        dve.wait_ge(heads_ready, n + 1)
                        nc.vector.tensor_scalar(dst[:, c, h * HALF:(h + 1) * HALF], acc[:, 4 + n % 2, :], bias[:, c:c + 1],
                                                scale, ALU.add, ALU.mult).then_inc(heads_taken, 1)
                        n += 1


def attend_in_blocks(nc, sh, s):
    x, ident = sh.x, sh.ident
    with ExitStack() as ctx:
        sb, ps, sem = scope(nc, ctx, "b2_")
        p = sb("p", [P, 2, HEADS_B, P])
        pT = sb("pT", [P, 2, HEADS_B, P])
        row_max, row_sum = sb("row_max", [P, 2, HEADS_B]), sb("row_sum", [P, 2, HEADS_B])
        heads_out, joined = sb("heads_out", [P, 2, WIDE_B]), sb("joined", [WIDTH + 1, 2, P])
        scores = ps("scores", [P, 2, 2, HALF])
        turned = ps("turned", [P, 2, HALF])
        mixed = ps("mixed", [P, 1, HALF])
        out = ps("out", [P, 1, HALF])
        dve_steps, ones_ready = sem("dve_steps"), sem("ones_ready")
        scored, masked, shifted, exp_done, sum_ready, probs_ready = (
            sem("scored"), sem("masked"), sem("shifted"), sem("exp_done"), sem("sum_ready"), sem("probs_ready"))
        turned_ready, turned_copied, mixed_ready, mixed_copied = (
            sem("turned_ready"), sem("turned_copied"), sem("mixed_ready"), sem("mixed_copied"))
        joined_ready, joined_copied, out_ready, out_added = (
            sem("joined_ready"), sem("joined_copied"), sem("out_ready"), sem("out_added"))
        block = ctx.enter_context(nc.Block())

        @block.gpsimd
        def _(pool):
            nc.gpsimd.memset(joined[WIDTH:WIDTH + 1, :, :], 1.0).then_inc(ones_ready, 1)
            pool.wait_ge(ones_ready, 1)
            for t in range(NT):
                pool.wait_ge(sum_ready, t + 1)
                nc.gpsimd.tensor_tensor(p[:, t % 2, :, :], p[:, t % 2, :, :],
                                        row_sum[:, t % 2, :].rearrange("p (h o) -> p h o", o=1).broadcast_to([P, HEADS_B, P]),
                                        ALU.mult).then_inc(probs_ready, 1)

        @block.tensor
        def _(pe):
            def score(t):
                if t >= 2:
                    pe.wait_ge(masked, t - 1)
                for h in range(HEADS_B):
                    c, j = divmod(h, 2)
                    at = slice(j * HD_B, (j + 1) * HD_B)
                    last = nc.tensor.matmul(scores[:, t % 2, j, c * P:(c + 1) * P], s.qh[at, c, t * P:(t + 1) * P],
                                            s.kh[at, c, t * P:(t + 1) * P], start=True, stop=True)
                last.then_inc(scored, 1)

            pe.wait_ge(s.loaded, 48)
            pe.wait_ge(ones_ready, 1)
            score(0)
            for t in range(NT):
                if t + 1 < NT:
                    score(t + 1)
                pe.wait_ge(probs_ready, t + 1)
                if t >= 1:
                    pe.wait_ge(turned_copied, t)
                for n in range(HEADS_B):
                    last = nc.tensor.transpose(turned[:, n // CB, (n % CB) * P:(n % CB + 1) * P], p[:, t % 2, n, :], ident[:, :])
                last.then_inc(turned_ready, 1)
                pe.wait_ge(turned_copied, t + 1)
                if t >= 1:
                    pe.wait_ge(mixed_copied, t)
                for h in range(HEADS_B):
                    c, j = divmod(h, 2)
                    last = nc.tensor.matmul(mixed[j * HD_B:(j + 1) * HD_B, 0, c * P:(c + 1) * P],
                                            s.vh[:, t, h * HD_B:(h + 1) * HD_B], pT[:, t % 2, j * CB + c, :],
                                            start=True, stop=True)
                last.then_inc(mixed_ready, 1)
                pe.wait_ge(mixed_copied, t + 1)
                if t >= 1:
                    pe.wait_ge(out_added, t)
                for c in range(CB):
                    last = nc.tensor.matmul(out[0:WIDTH, 0, 0:P], s.w_o[:, c, :], heads_out[:, t % 2, c * P:(c + 1) * P],
                                            start=(c == 0), stop=(c == CB - 1))
                last.then_inc(joined_ready, 1)
                pe.wait_ge(joined_copied, t + 1)
                nc.tensor.matmul(out[:, 0, 0:D], joined[:, t % 2, :], s.proj[:, :], start=True, stop=True).then_inc(out_ready, 1)

        @block.scalar
        def _(act):
            for t in range(NT):
                act.wait_ge(shifted, t + 1)
                nc.scalar.activation(p[:, t % 2, :, :], p[:, t % 2, :, :], ACT.Exp).then_inc(exp_done, 1)
                act.wait_ge(turned_ready, t + 1)
                nc.scalar.copy(pT[:, t % 2, :, :].rearrange("p h n -> p (h n)"),
                               turned[:, :, :].rearrange("p a b -> p (a b)")).then_inc(turned_copied, 1)
                act.wait_ge(mixed_ready, t + 1)
                nc.scalar.copy(heads_out[:, t % 2, :], mixed[:, 0, :]).then_inc(mixed_copied, 1)

        @block.vector
        def _(dve):
            chain = Chain(dve, dve_steps)

            def prepare(t):
                dve.wait_ge(scored, t + 1)
                if t >= 2:
                    dve.wait_ge(turned_ready, t - 1)
                nc.vector.tensor_tensor(p[:, t % 2, :, :], scores[:, t % 2, :, :].rearrange("p j (c n) -> p (j c) n", n=P),
                                        s.mask[:, :].rearrange("p (o n) -> p o n", o=1).broadcast_to([P, HEADS_B, P]),
                                        ALU.add).then_inc(masked, 1)
                dve.wait_ge(masked, t + 1)
                chain.step(nc.vector.tensor_reduce(row_max[:, t % 2, :], p[:, t % 2, :, :], AX.X, ALU.max))
                nc.vector.tensor_tensor(p[:, t % 2, :, :], p[:, t % 2, :, :],
                                        row_max[:, t % 2, :].rearrange("p (h o) -> p h o", o=1).broadcast_to([P, HEADS_B, P]),
                                        ALU.subtract).then_inc(shifted, 1)

            def sums(t):
                dve.wait_ge(exp_done, t + 1)
                chain.step(nc.vector.tensor_reduce(row_sum[:, t % 2, :], p[:, t % 2, :, :], AX.X, ALU.add))
                nc.vector.reciprocal(row_sum[:, t % 2, :], row_sum[:, t % 2, :]).then_inc(sum_ready, 1)

            dve.wait_ge(s.loaded, 48)
            prepare(0)
            for t in range(NT):
                sums(t)
                if t + 1 < NT:
                    prepare(t + 1)
                dve.wait_ge(joined_ready, t + 1)
                nc.vector.tensor_scalar(joined[0:WIDTH, t % 2, :], out[0:WIDTH, 0, 0:P], s.b_o[:, 0:1], None,
                                        ALU.add).then_inc(joined_copied, 1)
                dve.wait_ge(out_ready, t + 1)
                nc.vector.tensor_tensor(x[:, t, :], x[:, t, :], out[:, 0, 0:D], ALU.add).then_inc(out_added, 1)


HEADS_C = 16
HD_C = D // HEADS_C
PARTS = 4
LEVELS = 127.0
LEVELS_P = 255.0
SCALE_LEAST = 1e-8
WC = HEADS_C * PARTS * HD_C // P


def cross_attention(nc, sh, i):
    with ExitStack() as ctx:
        sb, ps, sem = scope(nc, ctx, "c0_")
        s = Buffers()
        s.qT = sb("qT", [P, WC, N], BF16)
        s.kT = sb("kT", [P, WC, N], BF16)
        s.v = sb("v", [P, NT, D], BF16)
        s.q_scale = sb("q_scale", [P, NT, HEADS_C])
        s.v_scale = sb("v_scale", [P, DC])
        s.identb = sb("identb", [P, P], BF16)
        s.w_p = sb("w_p", [P, DC, D])
        s.b_p = sb("b_p", [1, D])
        s.ones = sb("ones", [1, P])
        quantise(nc, sh, s, i)
        load_experts(nc, sh.ew, i)
        attend(nc, sh, s)


def quantise(nc, sh, s, i):
    x, xT, ident, ctxT = sh.x, sh.xT, sh.ident, sh.ctxT
    with ExitStack() as ctx:
        sb, ps, sem = scope(nc, ctx, "c1_")
        ln = norm_buffers(sb, ps, sh)
        w_q, w_kv = sb("w_q", [P, DC, D]), sb("w_kv", [P, DC, 2 * D])
        b_q, b_k, b_v = sb("b_q", [1, D]), sb("b_k", [1, D]), sb("b_v", [P, DC])
        k, q, vT = sb("k", [P, NT, D]), sb("q", [P, NT, D]), sb("vT", [P, DC, N])
        vTb = sb("vTb", [P, DC, N], BF16)
        scale, inverse = sb("scale", [P, NT, HEADS_C]), sb("inverse", [P, NT, HEADS_C])
        q_inverse = sb("q_inverse", [P, NT, HEADS_C])
        v_inverse = sb("v_inverse", [P, DC])
        parts = sb("parts", [P, NT, HEADS_C, PARTS, HD_C], BF16)
        rowb = ps("rowb", [P, 2, HALF])
        colb = ps("colb", [P, 2, HALF])
        turnedb = ps("turnedb", [P, 2, 2 * HALF], BF16)
        loaded, dve_steps, zeroed = sem("loaded"), sem("dve_steps"), sem("zeroed")
        rows_ready, rows_taken, cols_ready, cols_taken = sem("rows_ready"), sem("rows_taken"), sem("cols_ready"), sem("cols_taken")
        k_split, q_split, v_rounded, turned_ready, turned_copied = (
            sem("k_split"), sem("q_split"), sem("v_rounded"), sem("turned_ready"), sem("turned_copied"))
        loads = ((w_kv[:, :, :], "w_kv"), (b_k[:, :], "b_kc"), (b_v[:, :], "b_v"), (w_q[:, :, :], "w_qc"), (b_q[:, :], "b_qc"),
                 (s.w_p[:, :, :], "w_p"), (s.b_p[:, :], "b_p"),
                 (ctxT[:, :, :], "ctxT"))
        block = ctx.enter_context(nc.Block())

        @block.sync
        def _(sp):
            for dst, src in loads:
                sp.dma_start(dst, i[src]).then_inc(loaded, 16)

        @block.gpsimd
        def _(pool):
            nc.gpsimd.memset(parts[:, :, :, PARTS - 1, :], 0.0).then_inc(zeroed, 1)
            nc.gpsimd.tensor_copy(s.identb[:, :], ident[:, :]).then_inc(zeroed, 1)
            pool.wait_ge(zeroed, 2)
            nc.gpsimd.memset(s.ones[:, :], 1.0).then_inc(zeroed, 1)
            pool.wait_ge(zeroed, 3)
            norm_pool(nc, pool, ln)

        @block.tensor
        def _(pe):
            pe.wait_ge(loaded, 16 * len(loads))
            pe.wait_ge(zeroed, 3)
            for n in range(2 * NT):
                t = n % NT
                if n == NT:
                    norm_tensor(nc, pe, ln, ident)
                    pe.wait_ge(ln.copied, ln.tiles + NT)
                if n >= 2:
                    pe.wait_ge(rows_taken, n - 1)
                src, w, bias = (ctxT, w_kv, b_k) if n < NT else (xT, w_q, b_q)
                for c in range(DC):
                    nc.tensor.matmul(rowb[:, n % 2, 0:D], src[:, c, t * P:(t + 1) * P], w[:, c, 0:D], start=(c == 0), stop=False)
                nc.tensor.matmul(rowb[:, n % 2, 0:D], s.ones[:, :], bias[:, :], start=False, stop=True).then_inc(rows_ready, 1)
                if n < NT and n % 2 == 1:
                    g = n // 2
                    c, h = divmod(g, NH)
                    if g >= 2:
                        pe.wait_ge(cols_taken, g - 1)
                    for d in range(DC):
                        last = nc.tensor.matmul(colb[:, g % 2, :], w_kv[:, d, D + c * P:D + (c + 1) * P],
                                                ctxT[:, d, h * HALF:(h + 1) * HALF], start=(d == 0), stop=(d == DC - 1))
                    last.then_inc(cols_ready, 1)
            n = 0
            for split, src in ((k_split, parts), (v_rounded, vTb), (q_split, parts)):
                pe.wait_ge(split, 1)
                for t in range(NT) if src is not vTb else range(2):
                    if n >= 2:
                        pe.wait_ge(turned_copied, n - 1)
                    for c in range(WC):
                        if src is vTb:
                            m, d = divmod(4 * DC * t + c, DC)
                            block_in = vTb[:, d, m * P:(m + 1) * P]
                        else:
                            block_in = src[:, t, 2 * c:2 * c + 2, :, :].rearrange("p h r d -> p (h r d)")
                        last = nc.tensor.transpose(turnedb[:, n % 2, c * P:(c + 1) * P], block_in, s.identb[:, :])
                    last.then_inc(turned_ready, 1)
                    n += 1

        @block.scalar
        def _(act):
            act.wait_ge(loaded, 16 * len(loads))
            rows_done = 0

            def take_row(n):
                act.wait_ge(rows_ready, n + 1)
                if n < NT:
                    nc.scalar.copy(k[:, n, :], rowb[:, n % 2, 0:D]).then_inc(rows_taken, 1)
                else:
                    nc.scalar.activation(q[:, n - NT, :], rowb[:, n % 2, 0:D], ACT.Copy, scale=HD_C ** -0.5).then_inc(rows_taken, 1)

            for n in range(NT):
                take_row(n)
                if n % 2 == 1:
                    g = n // 2
                    c, h = divmod(g, NH)
                    act.wait_ge(cols_ready, g + 1)
                    nc.scalar.activation(vT[:, c, h * HALF:(h + 1) * HALF], colb[:, g % 2, :], ACT.Identity,
                                         bias=b_v[:, c:c + 1]).then_inc(cols_taken, 1)
            norm_scalar(nc, act, ln, lambda t: xT[:, :, t * P:(t + 1) * P])
            for n in range(NT, 2 * NT):
                take_row(n)
            n = 0
            for dst in (s.kT, s.v, s.qT):
                for t in range(NT) if dst is not s.v else range(2):
                    act.wait_ge(turned_ready, n + 1)
                    src = turnedb[:, n % 2, :]
                    if dst is s.v:
                        nc.scalar.copy(s.v[:, 4 * t:4 * t + 4, :].rearrange("p m n -> p (m n)"), src).then_inc(turned_copied, 1)
                    else:
                        nc.scalar.copy(dst[:, :, t * P:(t + 1) * P], src.rearrange("p (c n) -> p c n", n=P)).then_inc(turned_copied, 1)
                    n += 1

        @block.vector
        def _(dve):
            chain = Chain(dve, dve_steps)
            norm_vector(nc, dve, ln, x, chain)

            def heads(a):
                return a[:, :, :].rearrange("p t (h d) -> p (t h) d", d=HD_C)

            def spread(a):
                return a[:, :, :].rearrange("p t (h o) -> p (t h) o", o=1).broadcast_to([P, NT * HEADS_C, HD_C])

            def scales(a, scale_out, inverse_out):
                chain.step(nc.vector.tensor_reduce(scale_out[:, :, :].rearrange("p t h -> p (t h)"), heads(a), AX.X, ALU.max,
                                                   apply_absolute_value=True))
                chain.step(nc.vector.tensor_scalar(scale_out[:, :, :], scale_out[:, :, :], 1.0 / LEVELS, SCALE_LEAST,
                                                   ALU.mult, ALU.max))
                chain.step(nc.vector.reciprocal(inverse_out[:, :, :], scale_out[:, :, :]))

            def integers(a, inverse_out):
                chain.step(nc.vector.tensor_tensor(heads(a), heads(a), spread(inverse_out), ALU.mult))
                chain.step(nc.vector.tensor_scalar(a[:, :, :], a[:, :, :], ROUND, ROUND, ALU.add, ALU.subtract))
                chain.step(nc.vector.tensor_scalar(a[:, :, :], a[:, :, :], LEVELS, -LEVELS, ALU.min, ALU.max))

            def part(a, r):
                return a[:, :, :, r, :].rearrange("p t h d -> p (t h) d")

            dve.wait_ge(rows_taken, NT)
            scales(k, scale, inverse)
            integers(k, inverse)
            chain.step(nc.vector.tensor_tensor(heads(k), heads(k), spread(scale), ALU.mult))
            dve.wait_ge(zeroed, 1)
            chain.step(nc.vector.tensor_copy(part(parts, 0), heads(k)))
            chain.step(nc.vector.tensor_tensor(heads(k), heads(k), part(parts, 0), ALU.subtract))
            chain.step(nc.vector.tensor_copy(part(parts, 1), heads(k)))
            nc.vector.tensor_tensor(part(parts, 2), heads(k), part(parts, 1), ALU.subtract).then_inc(k_split, 1)
            dve.wait_ge(cols_taken, DC * NH)
            chain.step(nc.vector.tensor_reduce(s.v_scale[:, :], vT[:, :, :], AX.X, ALU.max, apply_absolute_value=True))
            chain.step(nc.vector.tensor_scalar(s.v_scale[:, :], s.v_scale[:, :], 1.0 / LEVELS, SCALE_LEAST, ALU.mult, ALU.max))
            chain.step(nc.vector.reciprocal(v_inverse[:, :], s.v_scale[:, :]))
            for c in range(DC):
                last = nc.vector.tensor_scalar(vT[:, c, :], vT[:, c, :], v_inverse[:, c:c + 1], ROUND, ALU.mult, ALU.add)
            chain.step(last)
            chain.step(nc.vector.tensor_scalar(vT[:, :, :], vT[:, :, :], ROUND, None, ALU.subtract))
            nc.vector.tensor_scalar(vTb[:, :, :], vT[:, :, :], LEVELS, -LEVELS, ALU.min, ALU.max).then_inc(v_rounded, 1)
            dve.wait_ge(rows_taken, 2 * NT)
            scales(q, s.q_scale, q_inverse)
            integers(q, q_inverse)
            dve.wait_ge(turned_ready, NT)
            for r in range(PARTS - 1):
                last = nc.vector.tensor_copy(part(parts, r), heads(q))
            last.then_inc(q_split, 1)


def attend(nc, sh, s):
    x, ident = sh.x, sh.ident
    with ExitStack() as ctx:
        sb, ps, sem = scope(nc, ctx, "c2_")
        RING = 6
        MIX_LAG = 5
        ON_ACT = 2
        LOG_LEVELS = float(np.log(LEVELS_P))
        UNITS_C = NT * HEADS_C
        probs = sb("probs", [P, RING, N], I16)
        bits = probs[:, :, :].bitcast(BF16)
        pT = sb("pT", [P, RING, NT, P], BF16)
        neg_max, bias = sb("neg_max", [P, NT, HEADS_C]), sb("bias", [P, NT, HEADS_C])
        row_sum = sb("row_sum", [P, NT, HEADS_C])
        o, oT = sb("o", [P, D]), sb("oT", [P, DC, P])
        scores = ps("scores", [P, 2, 2, HALF])
        turned = ps("turned", [P, 2, 2 * HALF], BF16)
        mixed = ps("mixed", [P, 1, HALF])
        tail = ps("tail", [P, 1, HALF])
        dve_steps = sem("dve_steps")
        scored, bias_ready, exp_done, turned_ready, turned_copied = (
            sem("scored"), sem("bias_ready"), sem("exp_done"), sem("turned_ready"), sem("turned_copied"))
        mixed_ready, o_ready, oT_ready, oT_copied, out_ready, out_added = (
            sem("mixed_ready"), sem("o_ready"), sem("oT_ready"), sem("oT_copied"), sem("out_ready"), sem("out_added"))
        turned_copied_act = sem("turned_copied_act")

        def on_act(u):
            return u % ON_ACT == ON_ACT - 1

        def wait_copied(eng, u):
            acts = sum(on_act(v) for v in range(u + 1))
            if acts:
                eng.wait_ge(turned_copied_act, acts)
            if u + 1 > acts:
                eng.wait_ge(turned_copied, u + 1 - acts)

        block = ctx.enter_context(nc.Block())

        @block.tensor
        def _(pe):
            def score(u):
                t, h = divmod(u, HEADS_C)
                if u >= 2:
                    pe.wait_ge(exp_done, u - 1)
                at = slice(h % 2 * P // 2, (h % 2 + 1) * P // 2)
                for n in range(2):
                    last = nc.tensor.matmul(scores[:, u % 2, n, :], s.qT[at, h // 2, t * P:(t + 1) * P],
                                            s.kT[at, h // 2, n * HALF:(n + 1) * HALF], start=True, stop=True)
                last.then_inc(scored, 1)

            def turn(u):
                pe.wait_ge(exp_done, u + 1)
                if u >= 2:
                    wait_copied(pe, u - 2)
                for n in range(NT):
                    last = nc.tensor.transpose(turned[:, u % 2, n * P:(n + 1) * P], bits[:, u % RING, n * P:(n + 1) * P],
                                               s.identb[:, :])
                last.then_inc(turned_ready, 1)

            def mix(u):
                t, h = divmod(u, HEADS_C)
                wait_copied(pe, u)
                if h == 0 and t >= 1:
                    pe.wait_ge(o_ready, t)
                for n in range(NT):
                    last = nc.tensor.matmul(mixed[:, 0, h * HD_C:(h + 1) * HD_C], pT[:, u % RING, n, :],
                                            s.v[:, n, h * HD_C:(h + 1) * HD_C], start=(n == 0), stop=(n == NT - 1))
                last.then_inc(mixed_ready, 1)

            def finish_a(t):
                pe.wait_ge(o_ready, t + 1)
                if t >= 1:
                    pe.wait_ge(out_added, t)
                for c in range(DC):
                    last = nc.tensor.transpose(tail[:, 0, c * P:(c + 1) * P], o[:, c * P:(c + 1) * P], ident[:, :])
                last.then_inc(oT_ready, 1)

            def finish_b(t):
                pe.wait_ge(oT_copied, t + 1)
                for c in range(DC):
                    nc.tensor.matmul(tail[:, 0, 0:D], oT[:, c, :], s.w_p[:, c, :], start=(c == 0), stop=False)
                nc.tensor.matmul(tail[:, 0, 0:D], s.ones[:, :], s.b_p[:, :], start=False, stop=True).then_inc(out_ready, 1)

            for u in range(UNITS_C + MIX_LAG):
                if u < UNITS_C:
                    score(u)
                if 2 <= u < UNITS_C + 2:
                    turn(u - 2)
                if u >= MIX_LAG:
                    mix(u - MIX_LAG)
                    t, h = divmod(u - MIX_LAG, HEADS_C)
                    if h == 3 and t >= 1:
                        finish_a(t - 1)
                    if h == 7 and t >= 1:
                        finish_b(t - 1)
            finish_a(NT - 1)
            finish_b(NT - 1)

        @block.scalar
        def _(act):
            def copy_turned(u):
                act.wait_ge(turned_ready, u + 1)
                if u >= RING:
                    act.wait_ge(mixed_ready, u - RING + 1)
                nc.scalar.copy(pT[:, u % RING, :, :].rearrange("p n q -> p (n q)"), turned[:, u % 2, :].bitcast(I16)).then_inc(turned_copied_act, 1)

            for u in range(UNITS_C + 2):
                if u < UNITS_C:
                    t, h = divmod(u, HEADS_C)
                    act.wait_ge(bias_ready, u + 1)
                    if u >= RING:
                        act.wait_ge(turned_ready, u - RING + 1)
                    nc.scalar.activation(probs[:, u % RING, :], scores[:, u % 2, :, :].rearrange("p a b -> p (a b)"), ACT.Exp,
                                         bias=bias[:, t, h:h + 1], scale=s.q_scale[:, t, h:h + 1],
                                         accum_out=row_sum[:, t, h:h + 1]).then_inc(exp_done, 1)
                if u >= 2 and on_act(u - 2):
                    copy_turned(u - 2)

        @block.vector
        def _(dve):
            chain = Chain(dve, dve_steps)

            def row_max(u):
                t, h = divmod(u, HEADS_C)
                dve.wait_ge(scored, u + 1)
                chain.step(nc.vector.tensor_reduce(neg_max[:, t, h:h + 1], scores[:, u % 2, :, :].rearrange("p a b -> p (a b)"),
                                                   AX.X, ALU.max, negate=True))
                nc.vector.tensor_scalar(bias[:, t, h:h + 1], neg_max[:, t, h:h + 1], s.q_scale[:, t, h:h + 1], LOG_LEVELS,
                                        ALU.mult, ALU.add).then_inc(bias_ready, 1)

            def copy_turned(u):
                dve.wait_ge(turned_ready, u + 1)
                if u >= RING:
                    dve.wait_ge(mixed_ready, u - RING + 1)
                nc.vector.tensor_copy(pT[:, u % RING, :, :].rearrange("p n q -> p (n q)"), turned[:, u % 2, :].bitcast(I16)).then_inc(turned_copied, 1)

            def normalise(t):
                dve.wait_ge(exp_done, HEADS_C * (t + 1))
                chain.step(nc.vector.reciprocal(row_sum[:, t, :], row_sum[:, t, :]))
                dve.wait_ge(mixed_ready, HEADS_C * (t + 1))
                if t >= 1:
                    dve.wait_ge(oT_ready, t)
                nc.vector.tensor_tensor(o[:, :].rearrange("p (h d) -> p h d", d=HD_C),
                                        mixed[:, 0, 0:D].rearrange("p (h d) -> p h d", d=HD_C),
                                        row_sum[:, t, :].rearrange("p (h o) -> p h o", o=1).broadcast_to([P, HEADS_C, HD_C]),
                                        ALU.mult).then_inc(o_ready, 1)

            def scale_values(t):
                dve.wait_ge(oT_ready, t + 1)
                if t >= 1:
                    dve.wait_ge(out_ready, t)
                for c in range(DC):
                    last = nc.vector.tensor_scalar(oT[:, c, :], tail[:, 0, c * P:(c + 1) * P], s.v_scale[:, c:c + 1], None, ALU.mult)
                last.then_inc(oT_copied, 1)

            def residual(t):
                dve.wait_ge(out_ready, t + 1)
                nc.vector.tensor_tensor(x[:, t, :], x[:, t, :], tail[:, 0, 0:D], ALU.add).then_inc(out_added, 1)

            for u in range(UNITS_C + 2):
                if u < UNITS_C:
                    row_max(u)
                if u >= 2 and not on_act(u - 2):
                    copy_turned(u - 2)
                if u >= HEADS_C + 2:
                    t, h = divmod(u - 2, HEADS_C)
                    if h == MIX_LAG - 2:
                        normalise(t - 1)
                    if h == 9:
                        scale_values(t - 1)
                    if h == 12:
                        residual(t - 1)
            normalise(NT - 1)
            scale_values(NT - 1)
            residual(NT - 1)


EXPERTS = 16
KEPT = 2
INNER = 176
RANKS = EXPERTS + 1
PICKS = KEPT * NT
SORTED = KEPT * NT + EXPERTS
GROUP = 4
FAR = INNER - P


EW_LOADS = 16 * (DC + 2)


def expert_weights(nc, ctx, sh):
    sb, ps, sem = scope(nc, ctx, "ew_")
    ew = sh.ew = Buffers()
    ew.w13 = sb("w13", [P, DC, RANKS * 2 * INNER])
    ew.w2 = sb("w2", [P, 2, RANKS, D])
    ew.rows_in = nc.dram_tensor("sorted_rows", (SORTED * P, D), F32).ap()
    ew.rows_out = nc.dram_tensor("expert_rows", (SORTED * P, D), F32).ap()
    ew.loaded, ew.zeroed = sem("loaded"), sem("zeroed")
    ew.padded = sem("padded")


def load_experts(nc, ew, i):
    with nc.Block() as block:

        @block.vector
        def _(dve):
            nc.vector.memset(ew.w2[:, 1, :, :], 0.0).then_inc(ew.padded, 1)

        @block.sync
        def _(sp):
            for c in range(DC):
                sp.dma_start(ew.w13[:, c, :], i["w13"][c]).then_inc(ew.loaded, 16)
            sp.dma_start(ew.w2[:, 0, :, :], i["w2_near"]).then_inc(ew.loaded, 16)
            sp.wait_ge(ew.padded, 1)
            sp.dma_start(ew.w2[0:FAR, 1, :, :], i["w2_far"]).then_inc(ew.loaded, 16)
            zeros = ew.w2[P // 2:, 1, 0:1, :].broadcast_to([P // 2, 2 * SORTED, D])
            sp.dma_start(ew.rows_in.rearrange("(j p) d -> p j d", p=P // 2), zeros).then_inc(ew.zeroed, 16)


def routed_experts(nc, sh, i):
    with ExitStack() as ctx:
        sb, ps, sem = scope(nc, ctx, "e0_")
        s = Buffers()
        s.xn = sb("xn", [P, NT, D])
        s.place = sb("place", [P, PICKS], U32)
        s.weight = sb("weight", [P, KEPT, NT])
        s.tile_expert = sb("tile_expert", [P, SORTED], I32)
        s.gated = sb("gated", [P, 2, 2 * P])
        s.ready = sem("ready")
        route(nc, sh, s, i)
        mix_experts(nc, sh, s)


def route(nc, sh, s, i):
    x, xT, ident = sh.x, sh.xT, sh.ident
    with ExitStack() as ctx:
        sb, ps, sem = scope(nc, ctx, "e1_")
        ln = norm_buffers(sb, ps, sh)
        ln.xn = s.xn
        gate, bias = sb("gate", [P, DC, EXPERTS]), sb("bias", [P, EXPERTS])
        number, number_i = sb("number", [P, SORTED]), sb("number_i", [P, SORTED], I32)
        score, chosen = sb("score", [P, NT, EXPERTS]), sb("chosen", [P, NT, EXPERTS])
        best, at, atf = sb("best", [P, NT, 8]), sb("at", [P, NT, 8], U32), sb("atf", [P, NT, 8])
        picked = sb("picked", [P, PICKS, EXPERTS])
        pickedb = sb("pickedb", [P, PICKS, EXPERTS], BF16)
        ranked = sb("ranked", [P, PICKS, EXPERTS])
        total, placef = sb("total", [P, NT]), sb("placef", [P, PICKS])
        earlier, onesb = sb("earlier", [P, P], BF16), sb("onesb", [P, P], BF16)
        tiles, end, start = sb("tiles", [P, EXPERTS]), sb("end", [P, EXPERTS]), sb("start", [P, EXPERTS])
        before, ones = sb("before", [P, SORTED, EXPERTS]), sb("ones", [P, EXPERTS])
        expert = sb("expert", [P, SORTED])
        logits = ps("logits", [P, 1, HALF])
        rank = ps("rank", [P, 1, HALF])
        ranks = rank[:, 0, 0:(PICKS + 1) * EXPERTS].rearrange("p (j e) -> p j e", e=EXPERTS)
        loaded, dve_steps, consts = sem("loaded"), sem("dve_steps"), sem("consts")
        logits_ready, score_ready, picked_ready, rank_ready = (
            sem("logits_ready"), sem("score_ready"), sem("picked_ready"), sem("rank_ready"))
        block = ctx.enter_context(nc.Block())

        @block.sync
        def _(sp):
            sp.dma_start(gate[:, :, :], i["gate"]).then_inc(loaded, 16)
            sp.dma_start(bias[:, :], i["bias"].broadcast_to([P, EXPERTS])).then_inc(loaded, 16)

        @block.gpsimd
        def _(pool):
            norm_pool(nc, pool, ln)
            nc.gpsimd.iota(number_i[:, :], [[1, SORTED]], base=0, channel_multiplier=0).then_inc(consts, 1)
            nc.gpsimd.memset(onesb[:, :], 1.0).then_inc(consts, 1)
            nc.gpsimd.memset(earlier[:, :], 1.0).then_inc(consts, 1)
            nc.gpsimd.memset(ones[:, :], 1.0).then_inc(consts, 1)
            nc.gpsimd.memset(s.gated[:, :, :], 0.0).then_inc(consts, 1)
            pool.wait_ge(consts, 5)
            nc.gpsimd.affine_select(out=earlier[:, :], in_=earlier[:, :], compare_op=ALU.is_gt, fill=0.0, base=0,
                                    pattern=[[1, P]], channel_multiplier=-1).then_inc(consts, 1)
            pool.wait_ge(consts, 6)

        @block.tensor
        def _(pe):
            norm_tensor(nc, pe, ln, ident)
            pe.wait_ge(loaded, 32)
            pe.wait_ge(ln.copied, ln.tiles + NT)
            for t in range(NT):
                for c in range(DC):
                    last = nc.tensor.matmul(logits[:, 0, t * EXPERTS:(t + 1) * EXPERTS], xT[:, c, t * P:(t + 1) * P],
                                            gate[:, c, :], start=(c == 0), stop=(c == DC - 1))
            last.then_inc(logits_ready, 1)
            pe.wait_ge(consts, 6)
            pe.wait_ge(picked_ready, 1)
            nc.tensor.matmul(ranks[:, 0:PICKS, :], earlier[:, :], pickedb[:, :, :], start=True, stop=False,
                             skip_group_check=True)
            for j in range(PICKS):
                last = nc.tensor.matmul(ranks[:, j + 1:, :], onesb[:, :],
                                        pickedb[:, j:j + 1, :].broadcast_to([P, PICKS - j, EXPERTS]),
                                        start=False, stop=(j == PICKS - 1), skip_group_check=True)
            last.then_inc(rank_ready, 1)

        @block.scalar
        def _(act):
            norm_scalar(nc, act, ln, lambda t: xT[:, :, t * P:(t + 1) * P])
            act.wait_ge(logits_ready, 1)
            nc.scalar.activation(score[:, :, :].rearrange("p t e -> p (t e)"), logits[:, 0, 0:NT * EXPERTS],
                                 ACT.Sigmoid).then_inc(score_ready, 1)

        @block.vector
        def _(dve):
            chain = Chain(dve, dve_steps)
            norm_vector(nc, dve, ln, x, chain)
            dve.wait_ge(consts, 4)
            nc.vector.tensor_copy(number[:, :], number_i[:, :])
            dve.wait_ge(loaded, 32)
            dve.wait_ge(score_ready, 1)
            chain.step(nc.vector.tensor_tensor(chosen[:, :, :], score[:, :, :],
                                               bias[:, :].rearrange("p (o e) -> p o e", o=1).broadcast_to([P, NT, EXPERTS]), ALU.add))
            for t in range(NT):
                last = nc.vector.max(best[:, t, :], chosen[:, t, :])
            chain.step(last)
            for t in range(NT):
                last = nc.vector.max_index(at[:, t, :], best[:, t, :], chosen[:, t, :])
            chain.step(last)
            chain.step(nc.vector.tensor_copy(atf[:, :, :], at[:, :, :]))
            numbers = number[:, 0:EXPERTS].rearrange("p (o e) -> p o e", o=1)
            for k in range(KEPT):
                last = nc.vector.tensor_tensor(picked[:, k * NT:(k + 1) * NT, :], atf[:, :, k:k + 1].broadcast_to([P, NT, EXPERTS]),
                                               numbers.broadcast_to([P, NT, EXPERTS]), ALU.is_equal)
            chain.step(last)
            nc.vector.tensor_copy(pickedb[:, :, :], picked[:, :, :]).then_inc(picked_ready, 1)
            for k in range(KEPT):
                last = nc.vector.tensor_tensor(ranked[:, k * NT:(k + 1) * NT, :], picked[:, k * NT:(k + 1) * NT, :],
                                               score[:, :, :], ALU.mult)
            chain.step(last)
            chain.step(nc.vector.tensor_reduce(s.weight[:, :, :].rearrange("p k t -> p (k t)"), ranked[:, :, :], AX.X, ALU.add))
            chain.step(nc.vector.tensor_tensor(total[:, :], s.weight[:, 0, :], s.weight[:, 1, :], ALU.add))
            chain.step(nc.vector.reciprocal(total[:, :], total[:, :]))
            for k in range(KEPT):
                nc.vector.tensor_tensor(s.weight[:, k, :], s.weight[:, k, :], total[:, :], ALU.mult)
            dve.wait_ge(rank_ready, 1)
            chain.step(nc.vector.tensor_scalar(tiles[:, :], ranks[:, PICKS, :], 1.0 / P, (P - 1.0) / P - 0.5 + 0.25 / P,
                                               ALU.mult, ALU.add))
            chain.step(nc.vector.tensor_scalar(tiles[:, :], tiles[:, :], ROUND, ROUND, ALU.add, ALU.subtract))
            chain.step(nc.vector.tensor_tensor_scan(end[:, :], ones[:, :], tiles[:, :], 0.0, ALU.mult, ALU.add))
            nc.vector.tensor_tensor(before[:, :, :], end[:, :].rearrange("p (o e) -> p o e", o=1).broadcast_to([P, SORTED, EXPERTS]),
                                    number[:, :].rearrange("p (j o) -> p j o", o=1).broadcast_to([P, SORTED, EXPERTS]), ALU.is_le)
            chain.step(nc.vector.tensor_tensor(start[:, :], end[:, :], tiles[:, :], ALU.subtract))
            chain.step(nc.vector.scalar_tensor_tensor(ranked[:, :, :], start[:, :].rearrange("p (o e) -> p o e", o=1).broadcast_to([P, PICKS, EXPERTS]),
                                                      float(P), ranks[:, 0:PICKS, :], ALU.mult, ALU.add))
            chain.step(nc.vector.tensor_tensor(ranked[:, :, :], ranked[:, :, :], picked[:, :, :], ALU.mult))
            chain.step(nc.vector.tensor_reduce(placef[:, :], ranked[:, :, :], AX.X, ALU.add))
            nc.vector.tensor_copy(s.place[:, :], placef[:, :]).then_inc(s.ready, 1)
            chain.step(nc.vector.tensor_reduce(expert[:, :], before[:, :, :], AX.X, ALU.add))
            nc.vector.tensor_scalar(s.tile_expert[:, :], expert[:, :], EXPERTS - 1.0, None, ALU.min).then_inc(s.ready, 1)


def mix_experts(nc, sh, s):
    x, xT, ident, ew = sh.x, sh.xT, sh.ident, sh.ew
    with ExitStack() as ctx:
        sb, ps, sem = scope(nc, ctx, "e2_")
        units = NT + SORTED
        row = sb("row", [P, SORTED, D])
        rowT = sb("rowT", [P, 2, DC, P])
        gatedT = sb("gatedT", [P, 2, 2, P])
        made = sb("made", [P, SORTED, D])
        turned = ps("turned", [P, 2, HALF])
        hidden = ps("hidden", [P, 2, HALF])
        gated_turned = ps("gated_turned", [P, 2, HALF])
        y = ps("y", [P, 2, HALF])
        scattered, stored, fetched = sem("scattered"), sem("stored"), sem("fetched")
        row_loaded = [sem("row_loaded%d" % j) for j in range(SORTED // GROUP)]
        turned_ready, turned_copied, hidden_ready, silu_ready, gated_ready = (
            sem("turned_ready"), sem("turned_copied"), sem("hidden_ready"), sem("silu_ready"), sem("gated_ready"))
        gated_turned_ready, gated_copied, y_ready, y_taken, added = (
            sem("gated_turned_ready"), sem("gated_copied"), sem("y_ready"), sem("y_taken"), sem("added"))
        block = ctx.enter_context(nc.Block())

        @block.gpsimd
        def _(pool):
            pool.wait_ge(s.ready, 1)
            pool.wait_ge(ew.zeroed, 16)
            for j in range(PICKS):
                nc.gpsimd.indirect_dma_start(ew.rows_in, bass.IndirectOffsetOnAxis(s.place[:, j:j + 1], 0),
                                             s.xn[:, j % NT, :], None).then_inc(scattered, 16)
            pool.wait_ge(stored, 16 * (SORTED // GROUP))
            for t in range(NT):
                for k in range(KEPT):
                    j = k * NT + t
                    nc.gpsimd.indirect_dma_start(row[:, j, :], None, ew.rows_out,
                                                 bass.IndirectOffsetOnAxis(s.place[:, j:j + 1], 0)).then_inc(fetched, 16)

        @block.sync
        def _(sp):
            sp.wait_ge(scattered, 16 * PICKS)
            for g in range(SORTED // GROUP):
                sp.dma_start(row[:, g * GROUP:(g + 1) * GROUP, :],
                             ew.rows_in[g * GROUP * P:(g + 1) * GROUP * P, :].rearrange("(j p) d -> p j d", p=P)
                             ).then_inc(row_loaded[g], 16)
            for g in range(SORTED // GROUP):
                sp.wait_ge(y_taken, NT + (g + 1) * GROUP)
                sp.dma_start(ew.rows_out[g * GROUP * P:(g + 1) * GROUP * P, :].rearrange("(j p) d -> p j d", p=P),
                             made[:, g * GROUP:(g + 1) * GROUP, :]).then_inc(stored, 16)
            sp.wait_ge(stored, 16 * (SORTED // GROUP))

        @block.tensor
        def _(pe):
            expert = {}

            def turn(j):
                if j % GROUP == 0:
                    pe.wait_ge(row_loaded[j // GROUP], 16)
                if j >= 2:
                    pe.wait_ge(turned_copied, j - 1)
                for c in range(DC):
                    last = nc.tensor.transpose(turned[:, j % 2, c * P:(c + 1) * P], row[:, j, c * P:(c + 1) * P], ident[:, :])
                last.then_inc(turned_ready, 1)

            def up(u):
                j = u - NT
                if j >= 0:
                    pe.wait_ge(turned_copied, j + 1)
                    expert[j] = pe.value_load(s.tile_expert[0:1, j:j + 1], min_val=0, max_val=EXPERTS - 1)
                if u >= 2:
                    pe.wait_ge(gated_ready, u - 1)
                for c in range(DC):
                    if j < 0:
                        left = xT[:, c, u * P:(u + 1) * P]
                        right = ew.w13[:, c, EXPERTS * 2 * INNER:]
                    else:
                        left = rowT[:, j % 2, c, :]
                        right = ew.w13[:, c, bass.ds(expert[j] * (2 * INNER), 2 * INNER)]
                    last = nc.tensor.matmul(hidden[:, u % 2, 0:2 * INNER], left, right, start=(c == 0), stop=(c == DC - 1))
                last.then_inc(hidden_ready, 1)

            def turn_gated(u):
                pe.wait_ge(gated_ready, u + 1)
                if u >= 2:
                    pe.wait_ge(gated_copied, u - 1)
                for c in range(2):
                    last = nc.tensor.transpose(gated_turned[:, u % 2, c * P:(c + 1) * P], s.gated[:, u % 2, c * P:(c + 1) * P], ident[:, :])
                last.then_inc(gated_turned_ready, 1)

            def down(u):
                j = u - NT
                pe.wait_ge(gated_copied, u + 1)
                if u >= 2:
                    pe.wait_ge(y_taken, u - 1)
                for c in range(2):
                    right = ew.w2[:, c, EXPERTS, :] if j < 0 else ew.w2[:, c, bass.ds(expert[j], 1), :]
                    last = nc.tensor.matmul(y[:, u % 2, 0:D], gatedT[:, u % 2, c, :], right, start=(c == 0), stop=(c == 1))
                last.then_inc(y_ready, 1)

            pe.wait_ge(ew.loaded, EW_LOADS)
            pe.wait_ge(s.ready, 2)
            for n in range(units + 3):
                if NT <= n < units:
                    turn(n - NT)
                if 1 <= n <= units:
                    up(n - 1)
                if 2 <= n <= units + 1:
                    turn_gated(n - 2)
                if n >= 3:
                    down(n - 3)

        @block.scalar
        def _(act):
            def copy_turned(j):
                act.wait_ge(turned_ready, j + 1)
                if j >= 2:
                    act.wait_ge(hidden_ready, NT + j - 1)
                nc.scalar.copy(rowT[:, j % 2, :, :].rearrange("p c n -> p (c n)"), turned[:, j % 2, 0:D]).then_inc(turned_copied, 1)

            for n in range(units + 1):
                if NT <= n < units:
                    copy_turned(n - NT)
                if n >= 1:
                    u = n - 1
                    act.wait_ge(hidden_ready, u + 1)
                    if u >= 2:
                        act.wait_ge(gated_turned_ready, u - 1)
                    nc.scalar.activation(s.gated[:, u % 2, 0:INNER], hidden[:, u % 2, 0:INNER], ACT.Silu).then_inc(silu_ready, 1)

        @block.vector
        def _(dve):
            def gate(u):
                dve.wait_ge(silu_ready, u + 1)
                nc.vector.tensor_tensor(s.gated[:, u % 2, 0:INNER], hidden[:, u % 2, INNER:2 * INNER],
                                        s.gated[:, u % 2, 0:INNER], ALU.mult).then_inc(gated_ready, 1)

            def copy_gated(u):
                dve.wait_ge(gated_turned_ready, u + 1)
                if u >= 2:
                    dve.wait_ge(y_ready, u - 1)
                nc.vector.tensor_copy(gatedT[:, u % 2, :, :].rearrange("p c n -> p (c n)"),
                                      gated_turned[:, u % 2, 0:2 * P]).then_inc(gated_copied, 1)

            def take(u):
                dve.wait_ge(y_ready, u + 1)
                if u < NT:
                    nc.vector.tensor_tensor(x[:, u, :], x[:, u, :], y[:, u % 2, 0:D], ALU.add).then_inc(y_taken, 1)
                else:
                    nc.vector.tensor_copy(made[:, u - NT, :], y[:, u % 2, 0:D]).then_inc(y_taken, 1)

            for n in range(units + 2):
                if n < units:
                    gate(n)
                if 1 <= n <= units:
                    copy_gated(n - 1)
                if n >= 2:
                    take(n - 2)
            dve.wait_ge(y_taken, NT)
            for t in range(NT):
                for k in range(KEPT):
                    dve.wait_ge(fetched, 16 * PICKS)
                    if k >= 1:
                        dve.wait_ge(added, t * KEPT + k)
                    nc.vector.scalar_tensor_tensor(x[:, t, :], row[:, k * NT + t, :], s.weight[:, k, t:t + 1], x[:, t, :],
                                                   ALU.mult, ALU.add).then_inc(added, 1)

def finish_stage(nc, x, out_dram, stored):
    with nc.Block() as block:
        @block.sync
        def _(sp):
            sp.dma_start(out_dram, x[:, :, :]).then_inc(stored, 16)
            sp.wait_ge(stored, 16)


def decoder(nc, i, out):
    with ExitStack() as ctx:
        sb, ps, sem = scope(nc, ctx, "")
        stored = sem("stored")
        sh = Buffers()
        sh.ln = norm_semaphores(sem)
        sh.x = sb("x", [P, NT, D])
        sh.xT = sb("xT", [P, DC, N])
        sh.ident = sb("ident", [P, P])
        sh.ctxT = sb("ctxT", [P, DC, EXPERTS_T * D])
        start_stage(nc, sh.x, sh.ident, i["x"])
        linear_attention(nc, sh, i["w_qkv"], i["w_out"], i["decay"])
        token_experts(nc, sh, i["ids"], i["ctxT"])
        retrieval(nc, sh, i)
        block_attention(nc, sh, i)
        expert_weights(nc, ctx, sh)
        cross_attention(nc, sh, i)
        routed_experts(nc, sh, i)
        finish_stage(nc, sh.x, out, stored)


def rows(a):
    a = np.asarray(a)
    return np.ascontiguousarray(a.reshape(-1, P, a.shape[-1]).transpose(1, 0, 2))


def column(a):
    return np.ascontiguousarray(np.asarray(a).reshape(-1, P).T)


def layouts(g):
    a = {}
    a["x"] = rows(np.asarray(g["x"]).reshape(N, D))
    a["w_qkv"] = rows(g["L0_attn_w_qkv"])
    a["w_out"] = rows(g["L0_attn_w_out"])
    a["decay"] = column(np.repeat(np.asarray(g["L0_attn_decay_param"]), HD0))
    a["ids"] = np.ascontiguousarray(np.asarray(g["itok_BxS_13_99985"]).reshape(1, N))
    a["ctxT"] = rows(np.asarray(g["ctx_2048"]).reshape(N, D).T)
    a["w_up"] = rows(np.asarray(g["L0_ffn_W_up"]).T)
    a["b_up"] = column(g["L0_ffn_b_up"])
    a["w_down"] = rows(np.asarray(g["L0_ffn_W_down"]).T)
    a["b_down"] = column(g["L0_ffn_b_down"])
    a["w_q"] = rows(g["L0_ffn_W_q"])
    k = np.asarray(g["L0_ffn_keys"]).reshape(HEADS_R // 2, 2, KEYS, 2, RETR)
    a["keys"] = np.ascontiguousarray(k.transpose(1, 4, 3, 0, 2).reshape(2, RETR, UC, KEYS))
    a["down"] = np.ascontiguousarray(np.asarray(g["L0_ffn_down_embed"]).T)
    a["up"] = rows(g["L0_ffn_up_embed"])
    w = np.asarray(g["L1_attn_conv_w"]).reshape(TAPS, DC, P, 3 * WIDTH)
    a["conv_w"] = np.ascontiguousarray(w.transpose(2, 0, 1, 3))
    b = np.asarray(g["L1_attn_conv_b"])
    a["conv_b"] = column(np.concatenate([b, np.zeros(P - WIDTH, b.dtype)]))
    a["w_qk"] = np.concatenate([np.asarray(g["L1_attn_" + n]).reshape(WIDTH, WIDE_B) for n in ("wq", "wk")])
    a["b_q"] = column(np.asarray(g["L1_attn_bq"]).reshape(-1))
    a["b_k"] = column(np.asarray(g["L1_attn_bk"]).reshape(-1))
    a["w_v"] = np.concatenate([np.asarray(g["L1_attn_wv"]).reshape(WIDTH, WIDE_B),
                               np.asarray(g["L1_attn_bv"]).reshape(1, WIDE_B)])
    a["w_o"] = rows(np.asarray(g["L1_attn_wo"]).reshape(WIDE_B, WIDTH))
    a["b_o"] = np.asarray(g["L1_attn_bo"]).reshape(WIDTH, 1)
    a["proj"] = np.concatenate([np.asarray(g["L1_attn_proj_w"]), np.asarray(g["L1_attn_proj_b"]).reshape(1, D)])
    a["w_kv"] = rows(g["L1_xattn_Wkv"])
    a["w_qc"] = rows(g["L1_xattn_Wq"])
    a["w_p"] = rows(g["L1_xattn_Wp"])
    b = np.asarray(g["L1_xattn_bkv"])
    a["b_kc"] = b[:D].reshape(1, D)
    a["b_v"] = column(b[D:])
    a["b_qc"] = np.asarray(g["L1_xattn_bq"]).reshape(1, D)
    a["b_p"] = np.asarray(g["L1_xattn_bp"]).reshape(1, D)
    a["gate"] = rows(np.asarray(g["L1_ffn_gate_w"]).T)
    a["bias"] = np.asarray(g["L1_ffn_bias"]).reshape(1, EXPERTS)
    w1 = np.concatenate([np.asarray(g["L1_ffn_w1"]), np.asarray(g["L1_ffn_shared_w1"])[None]])
    w3 = np.concatenate([np.asarray(g["L1_ffn_w3"]), np.asarray(g["L1_ffn_shared_w3"])[None]])
    w = np.concatenate([w1, w3], axis=1).reshape(RANKS * 2 * INNER, D)
    a["w13"] = np.ascontiguousarray(w.T.reshape(DC, P, RANKS * 2 * INNER))
    w2 = np.concatenate([np.asarray(g["L1_ffn_w2"]), np.asarray(g["L1_ffn_shared_w2"])[None]]).transpose(2, 0, 1)
    a["w2_near"], a["w2_far"] = np.ascontiguousarray(w2[:P]), np.ascontiguousarray(w2[P:])
    return a


def kernel(**inputs):
    import concourse.bacc as bacc
    from concourse.bass_utils import run_bass_kernel_spmd

    nc = bacc.Bacc("TRN2", target_bir_lowering=False, num_devices=1)
    arrays, aps = {}, {}
    for name, a in layouts(inputs).items():
        arrays["in_" + name] = a
        aps[name] = nc.dram_tensor("in_" + name, a.shape, mybir.dt.from_np(a.dtype), kind="ExternalInput").ap()
    out = nc.dram_tensor("out", (P, NT, D), F32, kind="ExternalOutput").ap()
    decoder(nc, aps, out)
    r = run_bass_kernel_spmd(nc, [arrays], core_ids=[0])
    return np.asarray(r.results[0]["out"]).transpose(1, 0, 2).reshape(B, T, D)
```

```python
from contextlib import ExitStack

import numpy as np
import concourse.bass as bass
from concourse import mybir

F32 = mybir.dt.float32
BF16 = mybir.dt.bfloat16
I32 = mybir.dt.int32
I16 = mybir.dt.int16
U32 = mybir.dt.uint32
ALU = mybir.AluOpType
ACT = mybir.ActivationFunctionType
AX = mybir.AxisListType

P = 128
B, T, D = 4, 256, 256
N = B * T
NT = N // P
DC = D // P
HALF = 512
NH = N // HALF
LN_EPS = 1e-5
ROUND = 12582912.0


class Buffers:
    pass


class Chain:

    def __init__(self, engine, semaphore):
        self.engine, self.semaphore, self.count = engine, semaphore, 0

    def step(self, instruction):
        self.count += 1
        instruction.then_inc(self.semaphore, 1)
        self.engine.wait_ge(self.semaphore, self.count)


def scope(nc, ctx, prefix):
    def sb(name, shape, dt=F32):
        return ctx.enter_context(nc.sbuf_tensor(prefix + name, shape, dt))

    def ps(name, shape, dt=F32):
        return ctx.enter_context(nc.psum_tensor(prefix + name, shape, dt))

    def sem(name):
        return ctx.enter_context(nc.semaphore(prefix + name))
    return sb, ps, sem





def norm_shared(sb, sem):
    ln = Buffers()
    ln.var_ready = sem("ln_var_ready")
    ln.rstd_ready = sem("ln_rstd_ready")
    ln.normed = sem("ln_normed")
    ln.turned_ready = sem("ln_turned_ready")
    ln.copied = sem("ln_copied")
    ln.steps = sem("ln_steps")
    ln.stats = sb("ln_stats", [P, NT, 6])
    ln.mv = sb("ln_mv", [P, NT, 2])
    ln.rstd = sb("ln_rstd", [P, NT])
    ln.minus_half = sb("ln_minus_half", [P, NT])
    ln.norms, ln.step_count = -1, 0
    return ln


def norm_buffers(sb, ps, sh):
    ln = sh.ln
    ln.norms += 1
    ln.tiles = ln.norms * NT
    ln.xn = sb("ln_xn", [P, NT, D])
    ln.turned = ps("ln_turned", [P, 2, HALF])
    return ln


def norm_statistics(nc, eng, sh, t):
    ln = sh.ln
    nc.vector.bn_stats(ln.stats[:, t, :], sh.x[:, t, :]).then_inc(ln.steps, 1)
    if t >= 1:
        nc.vector.bn_aggr(ln.mv[:, t - 1, :], ln.stats[:, t - 1, :]).then_inc(ln.steps, 1)
        ln.step_count += 1
    ln.step_count += 1
    eng.wait_ge(ln.steps, ln.step_count)
    if t == NT - 1:
        nc.vector.bn_aggr(ln.mv[:, t, :], ln.stats[:, t, :]).then_inc(ln.steps, 1)
        ln.step_count += 1
        eng.wait_ge(ln.steps, ln.step_count)
        nc.vector.tensor_scalar(ln.rstd[:, :], ln.mv[:, :, 1], LN_EPS, None, ALU.add).then_inc(ln.var_ready, 1)


def norm_vector(nc, eng, ln, x, chain):
    eng.wait_ge(ln.rstd_ready, ln.norms + 1)
    for t in range(NT):
        nc.vector.tensor_scalar(ln.xn[:, t, :], x[:, t, :], ln.mv[:, t, 0:1], ln.rstd[:, t:t + 1],
                                ALU.subtract, ALU.mult).then_inc(ln.normed, 1)


def norm_pool(nc, pool, ln, norm):
    pool.wait_ge(ln.var_ready, norm + 1)
    nc.gpsimd.tensor_tensor(ln.rstd[:, :], ln.rstd[:, :], ln.minus_half[:, :], ALU.pow).then_inc(ln.rstd_ready, 1)


def norm_tensor(nc, pe, ln, ident):
    for t in range(NT):
        pe.wait_ge(ln.normed, ln.tiles + t + 1)
        if t >= 2:
            pe.wait_ge(ln.copied, ln.tiles + t - 1)
        for c in range(DC):
            last = nc.tensor.transpose(ln.turned[:, t % 2, c * P:(c + 1) * P], ln.xn[:, t, c * P:(c + 1) * P], ident[:, :])
        last.then_inc(ln.turned_ready, 1)


def norm_scalar(nc, act, ln, place):
    for t in range(NT):
        act.wait_ge(ln.turned_ready, ln.tiles + t + 1)
        nc.scalar.copy(place(t), ln.turned[:, t % 2, 0:D].rearrange("p (c n) -> p c n", c=DC)).then_inc(ln.copied, 1)



def start_stage(nc, x, ident, x_dram):
    with ExitStack() as ctx:
        sb, ps, sem = scope(nc, ctx, "st_")
        loaded, zeroed = sem("loaded"), sem("zeroed")
        block = ctx.enter_context(nc.Block())

        @block.sync
        def _(sp):
            sp.dma_start(x[:, :, :], x_dram).then_inc(loaded, 16)
            sp.wait_ge(loaded, 16)

        @block.gpsimd
        def _(pool):
            nc.gpsimd.memset(ident[:, :], 0.0).then_inc(zeroed, 1)
            pool.wait_ge(zeroed, 1)
            nc.gpsimd.affine_select(out=ident[:, :], in_=ident[:, :], compare_op=ALU.not_equal, fill=1.0,
                                    base=0, pattern=[[-1, P]], channel_multiplier=1).then_inc(zeroed, 1)
            pool.wait_ge(zeroed, 2)



HEADS0 = 16
HD0 = D // HEADS0
DEN_LEAST = 1e-6
KEY, VALUE, QUERY = range(3)


def linear_attention(nc, sh, i):
    x, xT, ident = sh.x, sh.xT, sh.ident
    with ExitStack() as ctx:
        sb, ps, sem = scope(nc, ctx, "a0_")
        ln = norm_buffers(sb, ps, sh)
        w_qkv, w_out = sb("w_qkv", [P, DC, 3 * D]), sb("w_out", [P, DC, D])
        decay = sb("decay", [P, DC])
        gain = sb("gain", [P, DC, N])
        head_of = sb("head_of", [P, P // HD0])
        spread = sb("spread", [HEADS0, D])
        inverse, inverseT = sb("inverse", [P, NT, DC, P // HD0]), sb("inverseT", [HEADS0, N])
        exps, relus = sb("exps", [P, 4, HALF]), sb("relus", [P, 4, HALF])
        q, k, kv = sb("q", [P, DC, N]), sb("k", [P, DC, N]), sb("kv", [P, DC, N])
        run_k, run_kv = sb("run_k", [P, DC, N]), sb("run_kv", [P, DC, N])
        proj = ps("proj", [P, 4, HALF])
        sums = ps("sums", [P, 1, HALF])
        out = proj
        loaded, dve_steps, consts = sem("loaded"), sem("dve_steps"), sem("consts")
        decay_exp, projected = sem("decay_exp"), sem("projected")
        phi_parts, phi_done, kv_done = sem("phi_parts"), sem("phi_done"), sem("kv_done")
        scanned, qk_ready, sums_ready, inverse_ready = sem("scanned"), sem("qk_ready"), sem("sums_ready"), sem("inverse_ready")
        inverse_turned, inverse_copied, spread_ready = sem("inverse_turned"), sem("inverse_copied"), sem("spread_ready")
        qkv_ready, heads_ready = sem("qkv_ready"), sem("heads_ready")
        out_ready, out_added = sem("out_ready"), sem("out_added")
        groups = [(c, kind, h) for c in range(DC) for kind in (KEY, VALUE, QUERY) for h in range(NH)]
        column = {KEY: D, VALUE: 2 * D, QUERY: 0}

        def phis(n):
            return sum(kind != VALUE for _, kind, _ in groups[:n])

        block = ctx.enter_context(nc.Block())

        @block.sync
        def _(sp):
            sp.dma_start(w_qkv[:, :, :], i["w_qkv"]).then_inc(loaded, 16)
            sp.dma_start(decay[:, :], i["decay"]).then_inc(loaded, 16)
            sp.dma_start(w_out[:, :, :], i["w_out"]).then_inc(loaded, 16)
            load_tokens(sp, sh, i)

        @block.gpsimd
        def _(pool):
            norm_pool(nc, pool, ln, 0)
            nc.gpsimd.memset(head_of[:, :], 1.0).then_inc(consts, 1)
            pool.wait_ge(consts, 1)
            nc.gpsimd.affine_select(out=head_of[:, :], in_=head_of[:, :], compare_op=ALU.is_ge, fill=0.0, base=0,
                                    pattern=[[-HD0, P // HD0]], channel_multiplier=1).then_inc(consts, 1)
            pool.wait_ge(consts, 2)
            nc.gpsimd.affine_select(out=head_of[:, :], in_=head_of[:, :], compare_op=ALU.is_ge, fill=0.0, base=HD0 - 1,
                                    pattern=[[HD0, P // HD0]], channel_multiplier=-1).then_inc(consts, 1)
            nc.gpsimd.memset(gain[:, :, :], 1.0).then_inc(consts, 1)
            pool.wait_ge(consts, 4)
            nc.gpsimd.memset(gain[:, :, :].rearrange("p c (b t) -> p (c b) t", t=T)[:, :, 0:1], 0.0).then_inc(consts, 1)
            pool.wait_ge(consts, 5)
            nc.gpsimd.memset(spread[:, :], 0.0).then_inc(consts, 1)
            pool.wait_ge(consts, 6)
            heads = spread[:, :].rearrange("p (h d) -> p h d", d=HD0)
            nc.gpsimd.affine_select(out=heads, in_=heads, compare_op=ALU.not_equal, fill=1.0, base=0,
                                    pattern=[[-1, HEADS0], [0, HD0]], channel_multiplier=1).then_inc(consts, 1)
            for c in range(DC):
                pool.wait_ge(scanned, c + 1)
                nc.gpsimd.tensor_tensor(kv[:, c, :], q[:, c, :], run_kv[:, c, :], ALU.mult).then_inc(qkv_ready, 1)
            norm_pool(nc, pool, ln, ln.norms + 1)

        @block.tensor
        def _(pe):
            norm_tensor(nc, pe, ln, ident)
            pe.wait_ge(loaded, 48)
            pe.wait_ge(ln.copied, ln.tiles + NT)
            for i, (c, kind, h) in enumerate(groups):
                if i >= 4:
                    pe.wait_ge(phi_parts, phis(i - 3))
                    if i - 3 > phis(i - 3):
                        pe.wait_ge(kv_done, i - 3 - phis(i - 3))
                for d in range(DC):
                    f = column[kind] + c * P
                    last = nc.tensor.matmul(proj[:, i % 4, :], w_qkv[:, d, f:f + P],
                                            xT[:, d, h * HALF:(h + 1) * HALF], start=(d == 0), stop=(d == DC - 1))
                last.then_inc(projected, 1)
            pe.wait_ge(consts, 7)
            for c in range(DC):
                pe.wait_ge(qk_ready, c + 1)
                for t in range(NT):
                    at = (t * DC + c) * (P // HD0)
                    last = nc.tensor.matmul(sums[:, 0, at:at + P // HD0], k[:, c, t * P:(t + 1) * P], head_of[:, :],
                                            start=True, stop=True)
            last.then_inc(sums_ready, 1)
            pe.wait_ge(inverse_ready, 1)
            for t in range(NT):
                h, n = divmod(t, HALF // P)
                last = nc.tensor.transpose(ln.turned[0:HEADS0, h, n * P:(n + 1) * P],
                                           inverse[:, t, :, :].rearrange("p c h -> p (c h)"), ident[:, :])
                if n == HALF // P - 1:
                    last.then_inc(inverse_turned, 1)
            for h in range(NH):
                pe.wait_ge(inverse_copied, h + 1)
                for c in range(DC):
                    nc.tensor.matmul(proj[:, h * DC + c, :], spread[:, c * P:(c + 1) * P], inverseT[:, h * HALF:(h + 1) * HALF],
                                     start=True, stop=True).then_inc(spread_ready, 1)
            for t in range(NT):
                pe.wait_ge(heads_ready, DC * (t * P // HALF + 1))
                if t >= 2:
                    pe.wait_ge(out_added, t - 1)
                for c in range(DC):
                    last = nc.tensor.matmul(out[:, t % 2, 0:D], q[:, c, t * P:(t + 1) * P], w_out[:, c, :],
                                            start=(c == 0), stop=(c == DC - 1))
                last.then_inc(out_ready, 1)

        @block.scalar
        def _(act):
            norm_scalar(nc, act, ln, lambda t: xT[:, :, t * P:(t + 1) * P])
            act.wait_ge(loaded, 48)
            nc.scalar.activation(decay[:, :], decay[:, :], ACT.Exp, scale=-1.0).then_inc(decay_exp, 1)
            n = 0
            for i, (c, kind, h) in enumerate(groups):
                if kind == VALUE:
                    continue
                act.wait_ge(projected, i + 1)
                if n >= 4:
                    act.wait_ge(phi_done, n - 3)
                nc.scalar.activation(exps[:, n % 4, :], proj[:, i % 4, :], ACT.Exp)
                nc.scalar.activation(relus[:, n % 4, :], proj[:, i % 4, :], ACT.Relu).then_inc(phi_parts, 1)
                n += 1
            for h in range(NH):
                act.wait_ge(inverse_turned, h + 1)
                nc.scalar.copy(inverseT[:, h * HALF:(h + 1) * HALF], ln.turned[0:HEADS0, h, :]).then_inc(inverse_copied, 1)

        @block.vector
        def _(dve):
            chain = Chain(dve, dve_steps)
            for t in range(NT):
                last = nc.vector.bn_stats(ln.stats[:, t, :], x[:, t, :])
            chain.step(last)
            for t in range(NT):
                last = nc.vector.bn_aggr(ln.mv[:, t, :], ln.stats[:, t, :])
            chain.step(last)
            nc.vector.memset(ln.minus_half[:, :], -0.5)
            nc.vector.tensor_scalar(ln.rstd[:, :], ln.mv[:, :, 1], LN_EPS, None, ALU.add).then_inc(ln.var_ready, 1)
            norm_vector(nc, dve, ln, x, chain)
            dve.wait_ge(decay_exp, 1)
            chain.step(nc.vector.tensor_scalar(decay[:, :], decay[:, :], 1.0, None, ALU.add))
            chain.step(nc.vector.reciprocal(decay[:, :], decay[:, :]))
            dve.wait_ge(consts, 5)
            for c in range(DC):
                last = nc.vector.tensor_scalar(gain[:, c, :], gain[:, c, :], decay[:, c:c + 1], None, ALU.mult)
            chain.step(last)
            n = 0
            for i, (c, kind, h) in enumerate(groups):
                at = slice(h * HALF, (h + 1) * HALF)
                if kind == VALUE:
                    dve.wait_ge(projected, i + 1)
                    dve.wait_ge(phi_done, n)
                    nc.vector.tensor_tensor(kv[:, c, at], proj[:, i % 4, :], k[:, c, at], ALU.mult).then_inc(kv_done, 1)
                    continue
                dve.wait_ge(phi_parts, n + 1)
                nc.vector.scalar_tensor_tensor((k if kind == KEY else q)[:, c, at], exps[:, n % 4, :], 1.0,
                                               relus[:, n % 4, :], ALU.min, ALU.add).then_inc(phi_done, 1)
                n += 1
                if kind == QUERY and h == NH - 1:
                    dve.wait_ge(kv_done, NH * (c + 1))
                    dve.wait_ge(phi_done, n)
                    nc.vector.tensor_tensor_scan(run_k[:, c, :], gain[:, c, :], k[:, c, :], 0.0, ALU.mult, ALU.add)
                    chain.step(nc.vector.tensor_tensor_scan(run_kv[:, c, :], gain[:, c, :], kv[:, c, :], 0.0,
                                                            ALU.mult, ALU.add))
                    dve.sem_inc(scanned, 1)
                    nc.vector.tensor_tensor(k[:, c, :], q[:, c, :], run_k[:, c, :], ALU.mult).then_inc(qk_ready, 1)
            dve.wait_ge(sums_ready, 1)
            flat = inverse[:, :, :, :].rearrange("p t c h -> p (t c h)")
            chain.step(nc.vector.tensor_scalar(flat, sums[:, 0, 0:NT * HEADS0], DEN_LEAST, None, ALU.max))
            nc.vector.reciprocal(flat, flat).then_inc(inverse_ready, 1)
            dve.wait_ge(qkv_ready, DC)
            for h in range(NH):
                for c in range(DC):
                    at = slice(h * HALF, (h + 1) * HALF)
                    dve.wait_ge(spread_ready, h * DC + c + 1)
                    nc.vector.tensor_tensor(q[:, c, at], proj[:, h * DC + c, :], kv[:, c, at], ALU.mult).then_inc(heads_ready, 1)
            for t in range(NT):
                dve.wait_ge(out_ready, t + 1)
                nc.vector.tensor_tensor(x[:, t, :], x[:, t, :], out[:, t % 2, 0:D], ALU.add).then_inc(out_added, 1)
                dve.wait_ge(out_added, t + 1)
                norm_statistics(nc, dve, sh, t)



EXPERTS_T = 4
PER_EXPERT = 12500 // EXPERTS_T


def load_tokens(sp, sh, i):
    sp.dma_start(sh.ids[:, :], i["ids"].broadcast_to([P, N])).then_inc(sh.tokens_loaded, 16)
    sp.dma_start(sh.ctxT[:, :, :], i["ctxT"]).then_inc(sh.tokens_loaded, 16)


def token_experts(nc, sh, i):
    x, xT, ident, ctxT = sh.x, sh.xT, sh.ident, sh.ctxT
    with ExitStack() as ctx:
        sb, ps, sem = scope(nc, ctx, "m0_")
        ln = norm_buffers(sb, ps, sh)
        ids, idf = sh.ids, sb("idf", [P, N])
        mask = sb("mask", [P, EXPERTS_T, N])
        own = sb("own", [P, EXPERTS_T, DC, N])
        hid = sb("hid", [P, EXPERTS_T, DC, N])
        up = ps("up", [P, 4, HALF])
        out = ps("out", [P, 2, HALF])
        loaded = sh.tokens_loaded
        dve_steps, masks_ready, own_ready = sem("dve_steps"), sem("masks_ready"), sem("own_ready")
        up_ready, silu_ready, hid_ready, out_ready, out_added = (
            sem("up_ready"), sem("silu_ready"), sem("hid_ready"), sem("out_ready"), sem("out_added"))
        groups = [(e, f, h) for e in range(EXPERTS_T) for f in range(DC) for h in range(NH)]
        block = ctx.enter_context(nc.Block())

        @block.sync
        def _(sp):
            load_private(sp, sh, i)

        @block.gpsimd
        def _(pool):
            for e in range(EXPERTS_T):
                pool.wait_ge(masks_ready, e + 1)
                pool.wait_ge(ln.copied, ln.tiles + NT)
                for c in range(DC):
                    last = nc.gpsimd.tensor_tensor(own[:, e, c, :], xT[:, c, :], mask[:, e, :], ALU.mult)
                last.then_inc(own_ready, 1)
            norm_pool(nc, pool, ln, ln.norms + 1)

        @block.tensor
        def _(pe):
            norm_tensor(nc, pe, ln, ident)
            pe.wait_ge(loaded, 32)
            for i, (e, f, h) in enumerate(groups):
                pe.wait_ge(own_ready, e + 1)
                if i >= 4:
                    pe.wait_ge(hid_ready, i - 3)
                for d in range(DC):
                    last = nc.tensor.matmul(up[:, i % 4, :], ctxT[:, d, e * D + f * P:e * D + (f + 1) * P],
                                            own[:, e, d, h * HALF:(h + 1) * HALF], start=(d == 0), stop=(d == DC - 1))
                last.then_inc(up_ready, 1)
            pe.wait_ge(hid_ready, len(groups))
            for t in range(NT):
                if t >= 2:
                    pe.wait_ge(out_added, t - 1)
                for e in range(EXPERTS_T):
                    for f in range(DC):
                        last = nc.tensor.matmul(out[:, t % 2, 0:D], hid[:, e, f, t * P:(t + 1) * P],
                                                ctxT[:, f, e * D:(e + 1) * D], start=(e == f == 0),
                                                stop=(e == EXPERTS_T - 1 and f == DC - 1))
                last.then_inc(out_ready, 1)

        @block.scalar
        def _(act):
            norm_scalar(nc, act, ln, lambda t: xT[:, :, t * P:(t + 1) * P])
            for i, (e, f, h) in enumerate(groups):
                act.wait_ge(up_ready, i + 1)
                nc.scalar.activation(hid[:, e, f, h * HALF:(h + 1) * HALF], up[:, i % 4, :], ACT.Silu).then_inc(silu_ready, 1)

        @block.vector
        def _(dve):
            chain = Chain(dve, dve_steps)
            norm_vector(nc, dve, ln, x, chain)
            dve.wait_ge(loaded, 32)
            chain.step(nc.vector.tensor_copy(idf[:, :], ids[:, :]))
            for e in range(EXPERTS_T):
                if e == 0:
                    nc.vector.tensor_scalar(mask[:, e, :], idf[:, :], float(PER_EXPERT), None, ALU.is_lt).then_inc(masks_ready, 1)
                elif e == EXPERTS_T - 1:
                    nc.vector.tensor_scalar(mask[:, e, :], idf[:, :], float(e * PER_EXPERT), None, ALU.is_ge).then_inc(masks_ready, 1)
                else:
                    chain.step(nc.vector.tensor_scalar(mask[:, e, :], idf[:, :], float(e * PER_EXPERT), None, ALU.is_ge))
                    nc.vector.scalar_tensor_tensor(mask[:, e, :], idf[:, :], float((e + 1) * PER_EXPERT), mask[:, e, :],
                                                   ALU.is_lt, ALU.mult).then_inc(masks_ready, 1)
            for i, (e, f, h) in enumerate(groups):
                at = slice(h * HALF, (h + 1) * HALF)
                dve.wait_ge(silu_ready, i + 1)
                nc.vector.tensor_tensor(hid[:, e, f, at], up[:, i % 4, :], hid[:, e, f, at], ALU.mult).then_inc(hid_ready, 1)
            for t in range(NT):
                dve.wait_ge(out_ready, t + 1)
                nc.vector.tensor_tensor(x[:, t, :], x[:, t, :], out[:, t % 2, 0:D], ALU.add).then_inc(out_added, 1)
                dve.wait_ge(out_added, t + 1)
                norm_statistics(nc, dve, sh, t)


HEADS_R = 8
TOP = 8
RETR = 64
KEYS = 45
PAIRS = KEYS * KEYS
SIDE = HEADS_R * KEYS
UP = 1024
UC = UP // P
PB = (PAIRS + P - 1) // P
LAST = PAIRS - (PB - 1) * P
UNITS = NT * HEADS_R
BATCH = 4


def retrieval_tables(nc, ctx, sh):
    sb, ps, sem = scope(nc, ctx, "r0_")
    r = sh.r = Buffers()
    r.hT = sb("hT", [P, N])
    r.to_sims = sb("to_sims", [P, 2 * SIDE])
    r.down = sb("down", [P, PB * P])
    r.up = sb("up", [P, PB, D])
    r.loaded = sem("tables_loaded")


def early_weights(nc, ctx, sh):
    sb, ps, sem = scope(nc, ctx, "p0_")
    sh.ids = sb("ids", [P, N], I32)
    pw = sh.pw = Buffers()
    pw.w_up, pw.b_up = sb("w_up", [P, DC, UP]), sb("b_up", [P, UC])
    pw.w_down, pw.b_down = sb("w_down", [P, UC, P]), sb("b_down", [P, 1])
    pw.w_q = sb("w_q", [P, UC, P])
    pw.loaded = sem("loaded")


PRIVATE_LOADS = 5 * 16


def load_private(sp, sh, i):
    pw = sh.pw
    for dst, src in ((pw.w_up[:, :, :], "w_up"), (pw.b_up[:, :], "b_up"), (pw.w_q[:, :, :], "w_q"),
                     (pw.w_down[:, :, :], "w_down"), (pw.b_down[:, :], "b_down")):
        sp.dma_start(dst, i[src]).then_inc(pw.loaded, 16)


def private_state(nc, sh, r, i):
    x, xT, ident = sh.x, sh.xT, sh.ident
    with ExitStack() as ctx:
        sb, ps, sem = scope(nc, ctx, "r1_")
        ln = norm_buffers(sb, ps, sh)
        pw = sh.pw
        w_up, b_up, w_down, b_down, w_q = pw.w_up, pw.b_up, pw.w_down, pw.b_down, pw.w_q
        keys = sb("keys", [P, UC, 2, KEYS])
        wide = sb("wide", [P, UC, N])
        up = ps("up", [P, 4, HALF])
        low = ps("low", [P, 2, HALF])
        loaded = pw.loaded
        dve_steps, zeroed, keys_loaded = sem("dve_steps"), sem("zeroed"), sem("keys_loaded")
        sims_ready, up_ready, silu_ready, low_ready, done = (
            sem("sims_ready"), sem("up_ready"), sem("silu_ready"), sem("low_ready"), sem("done"))
        copied = sem("copied")
        groups = [(c, h) for c in range(UC) for h in range(NH)]
        block = ctx.enter_context(nc.Block())

        @block.sync
        def _(sp):
            sp.wait_ge(zeroed, 1)
            for j in range(2):
                sp.dma_start(keys[j * RETR:(j + 1) * RETR, :, j, :], i["keys"][j]).then_inc(keys_loaded, 16)
            sp.dma_start(r.down[:, :], i["down"]).then_inc(r.loaded, 16)
            sp.dma_start(r.up[:, :, :], i["up"]).then_inc(r.loaded, 16)

        @block.gpsimd
        def _(pool):
            nc.gpsimd.memset(keys[:, :, :, :], 0.0).then_inc(zeroed, 1)

        @block.tensor
        def _(pe):
            norm_tensor(nc, pe, ln, ident)
            pe.wait_ge(loaded, PRIVATE_LOADS)
            pe.wait_ge(keys_loaded, 32)
            pe.wait_ge(ln.copied, ln.tiles + NT)
            for n, (c, h) in enumerate(groups):
                if n == len(groups) - 2:
                    for k in range(UC):
                        last = nc.tensor.matmul(low[:, k // 4, (k % 4) * 2 * KEYS:(k % 4 + 1) * 2 * KEYS], w_q[:, k, :],
                                                keys[:, k, :, :].rearrange("p j k -> p (j k)"), start=True, stop=True)
                    last.then_inc(sims_ready, 1)
                if n >= 4:
                    pe.wait_ge(silu_ready, n - 3)
                for d in range(DC):
                    last = nc.tensor.matmul(up[:, n % 4, :], w_up[:, d, c * P:(c + 1) * P],
                                            xT[:, d, h * HALF:(h + 1) * HALF], start=(d == 0), stop=(d == DC - 1))
                last.then_inc(up_ready, 1)
            pe.wait_ge(silu_ready, len(groups))
            pe.wait_ge(copied, 1)
            for h in range(NH):
                for c in range(UC):
                    last = nc.tensor.matmul(low[:, h, :], w_down[:, c, :], wide[:, c, h * HALF:(h + 1) * HALF],
                                            start=(c == 0), stop=(c == UC - 1))
                last.then_inc(low_ready, 1)

        @block.scalar
        def _(act):
            norm_scalar(nc, act, ln, lambda t: xT[:, :, t * P:(t + 1) * P])
            act.wait_ge(loaded, PRIVATE_LOADS)
            for n, (c, h) in enumerate(groups):
                act.wait_ge(up_ready, n + 1)
                nc.scalar.activation(wide[:, c, h * HALF:(h + 1) * HALF], up[:, n % 4, :], ACT.Silu,
                                     bias=b_up[:, c:c + 1]).then_inc(silu_ready, 1)

        @block.vector
        def _(dve):
            chain = Chain(dve, dve_steps)
            norm_vector(nc, dve, ln, x, chain)
            dve.wait_ge(sims_ready, 1)
            nc.vector.tensor_copy(r.to_sims[:, :].rearrange("p (s n) -> p s n", s=2), low[:, :, 0:SIDE]).then_inc(copied, 1)
            dve.wait_ge(loaded, PRIVATE_LOADS)
            for h in range(NH):
                dve.wait_ge(low_ready, h + 1)
                nc.vector.tensor_scalar(r.hT[:, h * HALF:(h + 1) * HALF], low[:, h, :], b_down[:, 0:1], None,
                                        ALU.add).then_inc(done, 1)


def weigh_experts(nc, sh, r):
    x, ident = sh.x, sh.ident
    with ExitStack() as ctx:
        sb, ps, sem = scope(nc, ctx, "r2_")
        RING = 10
        sims = sb("sims", [P, NT, 2 * SIDE])
        pair_sum = sb("pair_sum", [P, 3, PAIRS])
        sums = [pair_sum[:, k, :] for k in range(3)] + [a[:, :, :].rearrange("p c n -> p (c n)")[:, 0:PAIRS] for a in (sh.xT, sh.ctxT)]
        SUMS = len(sums)
        w = sb("w", [P, RING, PAIRS])
        wT = sb("wT", [P, PB, P])
        best = sb("best", [P, 2, HEADS_R, TOP])
        grid = sb("grid", [P, HEADS_R, TOP * TOP])
        kept = sb("kept", [P, 2, HEADS_R, TOP])
        neg_max = sb("neg_max", [P, 2, HEADS_R])
        below_max = sb("below_max", [P, HEADS_R, TOP])
        kept_exp = sb("kept_exp", [P, HEADS_R, TOP])
        scale = sb("scale", [P, 2, HEADS_R])
        head_sum = ps("head_sum", [P, 4, HALF])
        z = ps("z", [P, 4, HALF])
        dve_steps = sem("dve_steps")
        sims_ready, sims_copied, z_ready = sem("sims_ready"), sem("sims_copied"), sem("z_ready")
        best_ready, kept_ready, scale_ready = sem("best_ready"), sem("kept_ready"), sem("scale_ready")
        summed_pairs, exp_done, masked, weighted, silu_done, summed = (
            sem("summed_pairs"), sem("exp_done"), sem("masked"), sem("weighted"), sem("silu_done"), sem("summed"))
        wT_copied, out_ready, out_added = sem("wT_copied"), sem("out_ready"), sem("out_added")
        block = ctx.enter_context(nc.Block())

        @block.gpsimd
        def _(pool):
            for u in range(UNITS):
                t, h = divmod(u, HEADS_R)
                if h == 0:
                    pool.wait_ge(sims_copied, t + 1)
                if u >= SUMS:
                    pool.wait_ge(masked, u - SUMS + 1)
                a = sims[:, t, h * KEYS:(h + 1) * KEYS].rearrange("p (a o) -> p a o", o=1)
                b = sims[:, t, SIDE + h * KEYS:SIDE + (h + 1) * KEYS].rearrange("p (o b) -> p o b", o=1)
                nc.gpsimd.tensor_tensor(sums[u % SUMS].rearrange("p (a b) -> p a b", b=KEYS),
                                        a.broadcast_to([P, KEYS, KEYS]), b.broadcast_to([P, KEYS, KEYS]),
                                        ALU.add).then_inc(summed_pairs, 1)
            norm_pool(nc, pool, sh.ln, sh.ln.norms + 1)

        @block.tensor
        def _(pe):
            pe.wait_ge(r.loaded, 32)

            def projections(t):
                if t >= 1:
                    pe.wait_ge(weighted, HEADS_R * t)
                for j in range(4):
                    lo, hi = j * HALF, min((j + 1) * HALF, PAIRS)
                    last = nc.tensor.matmul(z[:, j, 0:hi - lo], r.hT[:, t * P:(t + 1) * P], r.down[:, lo:hi],
                                            start=True, stop=True)
                last.then_inc(z_ready, 1)

            def output(t):
                pe.wait_ge(wT_copied, t + 1)
                for b in range(PB):
                    k = P if b < PB - 1 else LAST
                    last = nc.tensor.matmul(head_sum[:, 0, 0:D], wT[0:k, b, :], r.up[0:k, b, :],
                                            start=(b == 0), stop=(b == PB - 1))
                last.then_inc(out_ready, 1)

            for t in range(NT):
                if t >= 2:
                    pe.wait_ge(sims_copied, t - 1)
                if t == 2:
                    projections(0)
                for s in range(2):
                    last = nc.tensor.matmul(head_sum[:, t % 2 * 2 + s, 0:SIDE], r.hT[:, t * P:(t + 1) * P],
                                            r.to_sims[:, s * SIDE:(s + 1) * SIDE], start=True, stop=True)
                last.then_inc(sims_ready, 1)
            pe.wait_ge(sims_copied, NT)
            for u in range(UNITS):
                t, h = divmod(u, HEADS_R)
                if h == 2 and t + 1 < NT:
                    projections(t + 1)
                pe.wait_ge(silu_done, u + 1)
                if h == 0 and t >= 1:
                    pe.wait_ge(out_added, t)
                for b in range(PB):
                    m = P if b < PB - 1 else LAST
                    last = nc.tensor.matmul(head_sum[0:m, b // 4, (b % 4) * P:(b % 4 + 1) * P],
                                            w[:, u % RING, b * P:b * P + m], ident[:, :],
                                            start=(h == 0 and b % 4 == 0), stop=(h == HEADS_R - 1), skip_group_check=True)
                last.then_inc(summed, 1)
                if h == HEADS_R - 1:
                    output(t)

        @block.scalar
        def _(act):
            def exp_kept(t):
                act.wait_ge(best_ready, t + 1)
                if t >= 1:
                    act.wait_ge(scale_ready, t)
                nc.scalar.activation(kept_exp[:, :, :], below_max[:, :, :], ACT.Exp).then_inc(kept_ready, 1)

            def copy_sims(t):
                act.wait_ge(sims_ready, t + 1)
                nc.scalar.copy(sims[:, t, :].rearrange("p (s n) -> p s n", s=2),
                               head_sum[:, t % 2 * 2:t % 2 * 2 + 2, 0:SIDE]).then_inc(sims_copied, 1)

            def exps(g):
                for u in range(BATCH * g, BATCH * (g + 1)):
                    t, h = divmod(u, HEADS_R)
                    act.wait_ge(summed_pairs, u + 1)
                    if u >= RING:
                        act.wait_ge(summed, u - RING + 1)
                    nc.scalar.activation(w[:, u % RING, :], sums[u % SUMS], ACT.Exp,
                                         bias=neg_max[:, t % 2, h:h + 1]).then_inc(exp_done, 1)
                    if u + 2 < NT:
                        copy_sims(u + 2)

            def silus(g):
                for u in range(BATCH * g, BATCH * (g + 1)):
                    act.wait_ge(weighted, u + 1)
                    nc.scalar.activation(w[:, u % RING, :], w[:, u % RING, :], ACT.Silu).then_inc(silu_done, 1)

            copy_sims(0)
            copy_sims(1)
            exp_kept(0)
            exps(0)
            exps(1)
            for t in range(NT):
                silus(2 * t)
                if t + 1 < NT:
                    exp_kept(t + 1)
                    exps(2 * t + 2)
                silus(2 * t + 1)
                if t + 1 < NT:
                    exps(2 * t + 3)
                act.wait_ge(summed, HEADS_R * (t + 1))
                if t >= 1:
                    act.wait_ge(out_ready, t)
                nc.scalar.copy(wT[:, 0:PB - 1, :].rearrange("p b n -> p (b n)"),
                               head_sum[:, :, :].rearrange("p a b -> p (a b)")[:, 0:(PB - 1) * P])
                nc.scalar.copy(wT[0:LAST, PB - 1, :], head_sum[0:LAST, 3, 3 * P:4 * P]).then_inc(wT_copied, 1)

        @block.vector
        def _(dve):
            chain = Chain(dve, dve_steps)

            def choose(t):
                dve.wait_ge(sims_copied, t + 1)
                for s in range(2):
                    for h in range(HEADS_R):
                        at = s * SIDE + h * KEYS
                        last = nc.vector.max(best[:, s, h, :], sims[:, t, at:at + KEYS])
                chain.step(last)
                a = best[:, 0, :, :].rearrange("p h (a o) -> p h a o", o=1).broadcast_to([P, HEADS_R, TOP, TOP])
                b = best[:, 1, :, :].rearrange("p h (o b) -> p h o b", o=1).broadcast_to([P, HEADS_R, TOP, TOP])
                chain.step(nc.vector.tensor_tensor(grid[:, :, :].rearrange("p h (a b) -> p h a b", b=TOP), a, b, ALU.add))
                for h in range(HEADS_R):
                    last = nc.vector.max(kept[:, t % 2, h, :], grid[:, h, :])
                chain.step(last)
                if t >= 1:
                    dve.wait_ge(kept_ready, t)
                nc.vector.tensor_scalar(neg_max[:, t % 2, :], kept[:, t % 2, :, 0], -1.0, None, ALU.mult)
                top = kept[:, t % 2, :, 0:1].broadcast_to([P, HEADS_R, TOP])
                nc.vector.tensor_tensor(below_max[:, :, :], kept[:, t % 2, :, :], top, ALU.subtract).then_inc(best_ready, 1)

            def scales(t):
                dve.wait_ge(kept_ready, t + 1)
                chain.step(nc.vector.tensor_reduce(scale[:, t % 2, :], kept_exp[:, :, :], AX.X, ALU.add))
                chain.step(nc.vector.reciprocal(scale[:, t % 2, :], scale[:, t % 2, :]))
                dve.sem_inc(scale_ready, 1)

            def mask(u):
                t, h = divmod(u, HEADS_R)
                dve.wait_ge(exp_done, u + 1)
                nc.vector.scalar_tensor_tensor(w[:, u % RING, :], sums[u % SUMS], kept[:, t % 2, h, TOP - 1:TOP],
                                               w[:, u % RING, :], ALU.is_ge, ALU.mult).then_inc(masked, 1)

            def weigh(u):
                t, h = divmod(u, HEADS_R)
                if h == 0:
                    scales(t)
                    dve.wait_ge(z_ready, t + 1)
                dve.wait_ge(masked, u + 1)
                nc.vector.scalar_tensor_tensor(w[:, u % RING, :], w[:, u % RING, :], scale[:, t % 2, h:h + 1],
                                               z[:, :, :].rearrange("p a b -> p (a b)")[:, 0:PAIRS],
                                               ALU.mult, ALU.mult).then_inc(weighted, 1)

            def residual(t):
                dve.wait_ge(out_ready, t + 1)
                nc.vector.tensor_tensor(x[:, t, :], x[:, t, :], head_sum[:, 0, 0:D], ALU.add).then_inc(out_added, 1)
                dve.wait_ge(out_added, t + 1)
                norm_statistics(nc, dve, sh, t)

            choose(0)
            for u in range(UNITS):
                t, h = divmod(u, HEADS_R)
                mask(u)
                if u >= 1:
                    weigh(u - 1)
                if h == 1 and t + 1 < NT:
                    choose(t + 1)
                if h == 6 and t >= 1:
                    residual(t - 1)
            weigh(UNITS - 1)
            residual(NT - 1)


TAPS = 3
WIDTH = 64
HEADS_B = 8
HD_B = 64
BLOCK = T // 16
WIDE_B = HEADS_B * HD_B
CB = WIDE_B // P
MASKED = -1e9


def block_attention(nc, sh, i):
    with ExitStack() as ctx:
        sb, ps, sem = scope(nc, ctx, "b0_")
        s = Buffers()
        s.qh = sb("qh", [P, CB, N])
        s.kh = sb("kh", [P, CB, N])
        s.vh = sb("vh", [P, NT, WIDE_B])
        s.w_o = sb("w_o", [P, CB, WIDTH])
        s.b_o = sb("b_o", [WIDTH, 1])
        s.proj = sb("proj", [WIDTH + 1, D])
        s.mask = sb("mask", [P, P])
        s.loaded = sem("out_loaded")
        convolve(nc, sh, s, i)
        attend_in_blocks(nc, sh, s)


def convolve(nc, sh, s, i):
    x, ident = sh.x, sh.ident
    with ExitStack() as ctx:
        sb, ps, sem = scope(nc, ctx, "b1_")
        ln = norm_buffers(sb, ps, sh)
        PADDED = T + TAPS - 1
        padded = sb("padded", [P, DC, B, PADDED])
        conv_w, conv_b = sb("conv_w", [P, TAPS, DC, 3 * WIDTH]), sb("conv_b", [P, 2])
        w_qk, b_q, b_k = sb("w_qk", [P, WIDE_B]), sb("b_q", [P, CB]), sb("b_k", [P, CB])
        w_v = sb("w_v", [WIDTH + 1, WIDE_B])
        qk, v = sb("qk", [P, N]), sb("v", [WIDTH + 1, N])
        acc = ps("acc", [P, 6, HALF])
        loaded, dve_steps, zeroed, mask_steps = sem("loaded"), sem("dve_steps"), sem("zeroed"), sem("mask_steps")
        conv_ready, conv_taken, heads_ready, heads_taken = (
            sem("conv_ready"), sem("conv_taken"), sem("heads_ready"), sem("heads_taken"))
        v_heads_ready, v_heads_taken = sem("v_heads_ready"), sem("v_heads_taken")
        loads = ((conv_w[:, :, :, :], "conv_w"), (conv_b[:, :], "conv_b"), (w_qk[:, :], "w_qk"), (b_q[:, :], "b_q"),
                 (b_k[:, :], "b_k"), (w_v[:, :], "w_v"))
        block = ctx.enter_context(nc.Block())

        @block.sync
        def _(sp):
            for dst, src in loads:
                sp.dma_start(dst, i[src]).then_inc(loaded, 16)
            load_context(sp, sh, i)
            for dst, src in ((s.w_o[:, :, :], "w_o"), (s.b_o[:, :], "b_o"), (s.proj[:, :], "proj")):
                sp.dma_start(dst, i[src]).then_inc(s.loaded, 16)

        @block.gpsimd
        def _(pool):
            nc.gpsimd.memset(padded[:, :, :, 0:TAPS - 1], 0.0).then_inc(zeroed, 1)
            pool.wait_ge(zeroed, 1)
            nc.gpsimd.memset(v[WIDTH:WIDTH + 1, :], 1.0).then_inc(zeroed, 1)
            pool.wait_ge(zeroed, 2)
            nc.gpsimd.memset(s.mask[:, :], 0.0).then_inc(mask_steps, 1)
            pool.wait_ge(mask_steps, 1)
            nc.gpsimd.affine_select(out=s.mask[:, :], in_=s.mask[:, :], compare_op=ALU.is_ge, fill=MASKED, base=0,
                                    pattern=[[-1, P]], channel_multiplier=1).then_inc(mask_steps, 1)
            pool.wait_ge(mask_steps, 2)
            view = s.mask[:, :].rearrange("p (g k) -> p g k", k=BLOCK)
            nc.gpsimd.affine_select(out=view, in_=view, compare_op=ALU.is_ge, fill=MASKED, base=BLOCK - 1,
                                    pattern=[[BLOCK, P // BLOCK], [0, BLOCK]], channel_multiplier=-1).then_inc(mask_steps, 1)

        @block.tensor
        def _(pe):
            norm_tensor(nc, pe, ln, ident)
            pe.wait_ge(loaded, 16 * len(loads))
            pe.wait_ge(zeroed, 2)
            pe.wait_ge(ln.copied, ln.tiles + NT)
            for part, m in ((0, 2 * WIDTH), (1, WIDTH)):
                for h in range(NH):
                    for n in range(TAPS * DC):
                        j, d = divmod(n, DC)
                        last = nc.tensor.matmul(
                            acc[0:m, 2 * part + h, :].rearrange("p (b t) -> p b t", t=T),
                            conv_w[:, j, d, part * 2 * WIDTH:part * 2 * WIDTH + m],
                            padded[:, d, 2 * h:2 * h + 2, j:j + T], start=(n == 0), stop=(n == TAPS * DC - 1))
                    last.then_inc(conv_ready, 1)
            n = 0
            for h in range(NH):
                pe.wait_ge(conv_taken, h + 1)
                for c in range(CB):
                    for which in range(2):
                        if n >= 2:
                            pe.wait_ge(heads_taken, n - 1)
                        at = slice(which * WIDTH, (which + 1) * WIDTH)
                        nc.tensor.matmul(acc[:, 4 + n % 2, :], w_qk[at, c * P:(c + 1) * P], qk[at, h * HALF:(h + 1) * HALF],
                                         start=True, stop=True).then_inc(heads_ready, 1)
                        n += 1
            pe.wait_ge(conv_taken, 2 * NH)
            for t in range(NT):
                if t >= 2:
                    pe.wait_ge(v_heads_taken, t - 1)
                nc.tensor.matmul(acc[:, t % 2, :], v[:, t * P:(t + 1) * P], w_v[:, :], start=True, stop=True).then_inc(v_heads_ready, 1)

        @block.scalar
        def _(act):
            norm_scalar(nc, act, ln, lambda t: padded[:, :, t * P // T, TAPS - 1 + t * P % T:TAPS - 1 + t * P % T + P])
            for t in range(NT):
                act.wait_ge(v_heads_ready, t + 1)
                nc.scalar.copy(s.vh[:, t, :], acc[:, t % 2, :]).then_inc(v_heads_taken, 1)

        @block.vector
        def _(dve):
            chain = Chain(dve, dve_steps)
            norm_vector(nc, dve, ln, x, chain)
            dve.wait_ge(loaded, 16 * len(loads))
            for h in range(NH):
                dve.wait_ge(conv_ready, h + 1)
                nc.vector.tensor_scalar(qk[:, h * HALF:(h + 1) * HALF], acc[:, h, :], conv_b[:, 0:1], None,
                                        ALU.add).then_inc(conv_taken, 1)
            for h in range(NH):
                dve.wait_ge(conv_ready, NH + h + 1)
                nc.vector.tensor_scalar(v[0:WIDTH, h * HALF:(h + 1) * HALF], acc[0:WIDTH, 2 + h, :], conv_b[0:WIDTH, 1:2],
                                        None, ALU.add).then_inc(conv_taken, 1)
            n = 0
            for h in range(NH):
                for c in range(CB):
                    for dst, bias, scale in ((s.qh, b_q, HD_B ** -0.5), (s.kh, b_k, 1.0)):
                        dve.wait_ge(heads_ready, n + 1)
                        nc.vector.tensor_scalar(dst[:, c, h * HALF:(h + 1) * HALF], acc[:, 4 + n % 2, :], bias[:, c:c + 1],
                                                scale, ALU.add, ALU.mult).then_inc(heads_taken, 1)
                        n += 1


def attend_in_blocks(nc, sh, s):
    x, ident = sh.x, sh.ident
    with ExitStack() as ctx:
        sb, ps, sem = scope(nc, ctx, "b2_")
        p = sb("p", [P, 2, HEADS_B, P])
        pT = sb("pT", [P, 2, HEADS_B, P])
        row_max, row_sum = sb("row_max", [P, 2, HEADS_B]), sb("row_sum", [P, 2, HEADS_B])
        heads_out, joined = sb("heads_out", [P, 2, WIDE_B]), sb("joined", [WIDTH + 1, 2, P])
        scores = ps("scores", [P, 2, 2, HALF])
        turned = ps("turned", [P, 2, HALF])
        mixed = ps("mixed", [P, 1, HALF])
        out = ps("out", [P, 1, HALF])
        dve_steps, ones_ready = sem("dve_steps"), sem("ones_ready")
        scored, masked, shifted, exp_done, sum_ready, probs_ready = (
            sem("scored"), sem("masked"), sem("shifted"), sem("exp_done"), sem("sum_ready"), sem("probs_ready"))
        turned_ready, turned_copied, mixed_ready, mixed_copied = (
            sem("turned_ready"), sem("turned_copied"), sem("mixed_ready"), sem("mixed_copied"))
        joined_ready, joined_copied, out_ready, out_added = (
            sem("joined_ready"), sem("joined_copied"), sem("out_ready"), sem("out_added"))
        block = ctx.enter_context(nc.Block())

        @block.gpsimd
        def _(pool):
            nc.gpsimd.memset(joined[WIDTH:WIDTH + 1, :, :], 1.0).then_inc(ones_ready, 1)
            pool.wait_ge(ones_ready, 1)
            for t in range(NT):
                pool.wait_ge(sum_ready, t + 1)
                nc.gpsimd.tensor_tensor(p[:, t % 2, :, :], p[:, t % 2, :, :],
                                        row_sum[:, t % 2, :].rearrange("p (h o) -> p h o", o=1).broadcast_to([P, HEADS_B, P]),
                                        ALU.mult).then_inc(probs_ready, 1)
            norm_pool(nc, pool, sh.ln, sh.ln.norms + 1)

        @block.tensor
        def _(pe):
            def score(t):
                if t >= 2:
                    pe.wait_ge(masked, t - 1)
                for h in range(HEADS_B):
                    c, j = divmod(h, 2)
                    at = slice(j * HD_B, (j + 1) * HD_B)
                    last = nc.tensor.matmul(scores[:, t % 2, j, c * P:(c + 1) * P], s.qh[at, c, t * P:(t + 1) * P],
                                            s.kh[at, c, t * P:(t + 1) * P], start=True, stop=True)
                last.then_inc(scored, 1)

            pe.wait_ge(s.loaded, 48)
            pe.wait_ge(ones_ready, 1)
            def turn(t):
                pe.wait_ge(probs_ready, t + 1)
                if t >= 1:
                    pe.wait_ge(turned_copied, t)
                for n in range(HEADS_B):
                    last = nc.tensor.transpose(turned[:, n // CB, (n % CB) * P:(n % CB + 1) * P], p[:, t % 2, n, :], ident[:, :])
                last.then_inc(turned_ready, 1)

            def mix(t):
                pe.wait_ge(turned_copied, t + 1)
                if t >= 1:
                    pe.wait_ge(mixed_copied, t)
                for h in range(HEADS_B):
                    c, j = divmod(h, 2)
                    last = nc.tensor.matmul(mixed[j * HD_B:(j + 1) * HD_B, 0, c * P:(c + 1) * P],
                                            s.vh[:, t, h * HD_B:(h + 1) * HD_B], pT[:, t % 2, j * CB + c, :],
                                            start=True, stop=True)
                last.then_inc(mixed_ready, 1)

            def join(t):
                pe.wait_ge(mixed_copied, t + 1)
                if t >= 1:
                    pe.wait_ge(out_added, t)
                for c in range(CB):
                    last = nc.tensor.matmul(out[0:WIDTH, 0, 0:P], s.w_o[:, c, :], heads_out[:, t % 2, c * P:(c + 1) * P],
                                            start=(c == 0), stop=(c == CB - 1))
                last.then_inc(joined_ready, 1)

            def project(t):
                pe.wait_ge(joined_copied, t + 1)
                nc.tensor.matmul(out[:, 0, 0:D], joined[:, t % 2, :], s.proj[:, :], start=True, stop=True).then_inc(out_ready, 1)

            score(0)
            score(1)
            for t in range(NT):
                turn(t)
                if t + 2 < NT:
                    score(t + 2)
                if t >= 1:
                    join(t - 1)
                mix(t)
                if t >= 1:
                    project(t - 1)
            join(NT - 1)
            project(NT - 1)

        @block.scalar
        def _(act):
            def exps(t):
                act.wait_ge(shifted, t + 1)
                nc.scalar.activation(p[:, t % 2, :, :], p[:, t % 2, :, :], ACT.Exp).then_inc(exp_done, 1)

            exps(0)
            exps(1)
            for t in range(NT):
                act.wait_ge(turned_ready, t + 1)
                nc.scalar.copy(pT[:, t % 2, :, :].rearrange("p h n -> p (h n)"),
                               turned[:, :, :].rearrange("p a b -> p (a b)")).then_inc(turned_copied, 1)
                act.wait_ge(mixed_ready, t + 1)
                nc.scalar.copy(heads_out[:, t % 2, :], mixed[:, 0, :]).then_inc(mixed_copied, 1)
                if t + 2 < NT:
                    exps(t + 2)

        @block.vector
        def _(dve):
            chain = Chain(dve, dve_steps)

            def prepare(t):
                dve.wait_ge(scored, t + 1)
                if t >= 2:
                    dve.wait_ge(turned_ready, t - 1)
                nc.vector.tensor_tensor(p[:, t % 2, :, :], scores[:, t % 2, :, :].rearrange("p j (c n) -> p (j c) n", n=P),
                                        s.mask[:, :].rearrange("p (o n) -> p o n", o=1).broadcast_to([P, HEADS_B, P]),
                                        ALU.add).then_inc(masked, 1)
                dve.wait_ge(masked, t + 1)
                chain.step(nc.vector.tensor_reduce(row_max[:, t % 2, :], p[:, t % 2, :, :], AX.X, ALU.max))
                nc.vector.tensor_tensor(p[:, t % 2, :, :], p[:, t % 2, :, :],
                                        row_max[:, t % 2, :].rearrange("p (h o) -> p h o", o=1).broadcast_to([P, HEADS_B, P]),
                                        ALU.subtract).then_inc(shifted, 1)

            def sums(t):
                dve.wait_ge(exp_done, t + 1)
                chain.step(nc.vector.tensor_reduce(row_sum[:, t % 2, :], p[:, t % 2, :, :], AX.X, ALU.add))
                nc.vector.reciprocal(row_sum[:, t % 2, :], row_sum[:, t % 2, :]).then_inc(sum_ready, 1)

            def residual(t):
                dve.wait_ge(joined_ready, t + 1)
                nc.vector.tensor_scalar(joined[0:WIDTH, t % 2, :], out[0:WIDTH, 0, 0:P], s.b_o[:, 0:1], None,
                                        ALU.add).then_inc(joined_copied, 1)
                dve.wait_ge(out_ready, t + 1)
                nc.vector.tensor_tensor(x[:, t, :], x[:, t, :], out[:, 0, 0:D], ALU.add).then_inc(out_added, 1)
                dve.wait_ge(out_added, t + 1)
                norm_statistics(nc, dve, sh, t)

            dve.wait_ge(s.loaded, 48)
            prepare(0)
            prepare(1)
            sums(0)
            for t in range(NT):
                if t + 1 < NT:
                    sums(t + 1)
                if t + 2 < NT:
                    prepare(t + 2)
                if t >= 1:
                    residual(t - 1)
            residual(NT - 1)

HEADS_C = 16
HD_C = D // HEADS_C
PARTS = 4
LEVELS = 127.0
LEVELS_P = 255.0
SCALE_LEAST = 1e-8
WC = HEADS_C * PARTS * HD_C // P


def context_weights(nc, ctx, sh):
    sb, ps, sem = scope(nc, ctx, "cw_")
    sh.w_kv, sh.b_k, sh.b_v = sb("w_kv", [P, DC, 2 * D]), sb("b_k", [1, D]), sb("b_v", [P, DC])
    sh.context_loaded = sem("context_loaded")


CONTEXT_LOADS = 4 * 16


def load_context(sp, sh, i):
    for dst, src in ((sh.w_kv[:, :, :], "w_kv"), (sh.ctxT[:, :, :], "ctxT"), (sh.b_k[:, :], "b_kc"), (sh.b_v[:, :], "b_v")):
        sp.dma_start(dst, i[src]).then_inc(sh.context_loaded, 16)


def cross_attention(nc, sh, i):
    with ExitStack() as ctx:
        sb, ps, sem = scope(nc, ctx, "c0_")
        s = Buffers()
        s.qT = sb("qT", [P, WC, N], BF16)
        s.kT = sb("kT", [P, WC, N], BF16)
        s.v = sb("v", [P, NT, D], BF16)
        s.q_scale = sb("q_scale", [P, NT, HEADS_C])
        s.v_scale = sb("v_scale", [P, DC])
        s.identb = sb("identb", [P, P], BF16)
        s.w_p = sb("w_p", [P, DC, D])
        s.b_p = sb("b_p", [1, D])
        s.ones = sb("ones", [1, P])
        quantise(nc, sh, s, i)
        load_experts(nc, sh.ew, i)
        attend(nc, sh, s)


def quantise(nc, sh, s, i):
    x, xT, ident, ctxT = sh.x, sh.xT, sh.ident, sh.ctxT
    with ExitStack() as ctx:
        sb, ps, sem = scope(nc, ctx, "c1_")
        ln = norm_buffers(sb, ps, sh)
        w_kv, b_k, b_v = sh.w_kv, sh.b_k, sh.b_v
        w_q, b_q = sb("w_q", [P, DC, D]), sb("b_q", [1, D])
        k, q, vT = sb("k", [P, NT, D]), sb("q", [P, NT, D]), sb("vT", [P, DC, N])
        vTb = sb("vTb", [P, DC, N], BF16)
        HT = NT // 2
        scale, inverse = sb("scale", [P, NT, HEADS_C]), sb("inverse", [P, NT, HEADS_C])
        q_inverse = sb("q_inverse", [P, NT, HEADS_C])
        v_inverse = sb("v_inverse", [P, DC])
        parts = sb("parts", [P, NT, HEADS_C, PARTS, HD_C], BF16)
        rowb = ps("rowb", [P, 2, HALF])
        colb = ps("colb", [P, 2, HALF])
        turnedb = ps("turnedb", [P, 2, 2 * HALF], BF16)
        loaded, dve_steps, zeroed = sem("loaded"), sem("dve_steps"), sem("zeroed")
        rows_ready, rows_taken, cols_ready, cols_taken = sem("rows_ready"), sem("rows_taken"), sem("cols_ready"), sem("cols_taken")
        k_split, q_split, v_rounded, turned_ready, turned_copied = (
            sem("k_split"), sem("q_split"), sem("v_rounded"), sem("turned_ready"), sem("turned_copied"))
        loads = ((w_q[:, :, :], "w_qc"), (b_q[:, :], "b_qc"), (s.w_p[:, :, :], "w_p"), (s.b_p[:, :], "b_p"))
        block = ctx.enter_context(nc.Block())

        @block.sync
        def _(sp):
            for dst, src in loads:
                sp.dma_start(dst, i[src]).then_inc(loaded, 16)

        @block.gpsimd
        def _(pool):
            nc.gpsimd.memset(parts[:, :, :, PARTS - 1, :], 0.0).then_inc(zeroed, 1)
            nc.gpsimd.tensor_copy(s.identb[:, :], ident[:, :]).then_inc(zeroed, 1)
            pool.wait_ge(zeroed, 2)
            nc.gpsimd.memset(s.ones[:, :], 1.0).then_inc(zeroed, 1)

        @block.tensor
        def _(pe):
            pe.wait_ge(sh.context_loaded, CONTEXT_LOADS)
            pe.wait_ge(zeroed, 3)
            for n in range(2 * NT):
                t = n % NT
                if n == NT:
                    pe.wait_ge(loaded, 16 * len(loads))
                    norm_tensor(nc, pe, ln, ident)
                    pe.wait_ge(ln.copied, ln.tiles + NT)
                if n >= 2:
                    pe.wait_ge(rows_taken, n - 1)
                src, w, bias = (ctxT, w_kv, b_k) if n < NT else (xT, w_q, b_q)
                for c in range(DC):
                    nc.tensor.matmul(rowb[:, n % 2, 0:D], src[:, c, t * P:(t + 1) * P], w[:, c, 0:D], start=(c == 0), stop=False)
                nc.tensor.matmul(rowb[:, n % 2, 0:D], s.ones[:, :], bias[:, :], start=False, stop=True).then_inc(rows_ready, 1)
                if n < NT and n % 2 == 1:
                    g = n // 2
                    c, h = divmod(g, NH)
                    if g >= 2:
                        pe.wait_ge(cols_taken, g - 1)
                    for d in range(DC):
                        last = nc.tensor.matmul(colb[:, g % 2, :], w_kv[:, d, D + c * P:D + (c + 1) * P],
                                                ctxT[:, d, h * HALF:(h + 1) * HALF], start=(d == 0), stop=(d == DC - 1))
                    last.then_inc(cols_ready, 1)
            n = 0
            for split, src in ((k_split, parts), (v_rounded, vTb), (q_split, parts)):
                for t in range(NT) if src is not vTb else range(2):
                    pe.wait_ge(split, t // HT + 1)
                    if n >= 2:
                        pe.wait_ge(turned_copied, n - 1)
                    for c in range(WC):
                        if src is vTb:
                            m, d = divmod(4 * DC * t + c, DC)
                            block_in = vTb[:, d, m * P:(m + 1) * P]
                        else:
                            block_in = src[:, t, 2 * c:2 * c + 2, :, :].rearrange("p h r d -> p (h r d)")
                        last = nc.tensor.transpose(turnedb[:, n % 2, c * P:(c + 1) * P], block_in, s.identb[:, :])
                    last.then_inc(turned_ready, 1)
                    n += 1

        @block.scalar
        def _(act):
            act.wait_ge(sh.context_loaded, CONTEXT_LOADS)
            rows_done = 0

            def take_row(n):
                act.wait_ge(rows_ready, n + 1)
                if n < NT:
                    nc.scalar.copy(k[:, n, :], rowb[:, n % 2, 0:D]).then_inc(rows_taken, 1)
                else:
                    nc.scalar.activation(q[:, n - NT, :], rowb[:, n % 2, 0:D], ACT.Copy, scale=HD_C ** -0.5).then_inc(rows_taken, 1)

            for n in range(NT):
                take_row(n)
                if n % 2 == 1:
                    g = n // 2
                    c, h = divmod(g, NH)
                    act.wait_ge(cols_ready, g + 1)
                    nc.scalar.activation(vT[:, c, h * HALF:(h + 1) * HALF], colb[:, g % 2, :], ACT.Identity,
                                         bias=b_v[:, c:c + 1]).then_inc(cols_taken, 1)
            norm_scalar(nc, act, ln, lambda t: xT[:, :, t * P:(t + 1) * P])
            for n in range(NT, 2 * NT):
                take_row(n)
            n = 0
            for dst in (s.kT, s.v, s.qT):
                for t in range(NT) if dst is not s.v else range(2):
                    act.wait_ge(turned_ready, n + 1)
                    src = turnedb[:, n % 2, :]
                    if dst is s.v:
                        nc.scalar.copy(s.v[:, 4 * t:4 * t + 4, :].rearrange("p m n -> p (m n)"), src).then_inc(turned_copied, 1)
                    else:
                        nc.scalar.copy(dst[:, :, t * P:(t + 1) * P], src.rearrange("p (c n) -> p c n", n=P)).then_inc(turned_copied, 1)
                    n += 1

        @block.vector
        def _(dve):
            chain = Chain(dve, dve_steps)
            norm_vector(nc, dve, ln, x, chain)

            def heads(a, at):
                return a[:, at, :].rearrange("p t (h d) -> p (t h) d", d=HD_C)

            def spread(a, at):
                return a[:, at, :].rearrange("p t (h o) -> p (t h) o", o=1).broadcast_to([P, HT * HEADS_C, HD_C])

            def scales(a, at, scale_out, inverse_out):
                chain.step(nc.vector.tensor_reduce(scale_out[:, at, :].rearrange("p t h -> p (t h)"), heads(a, at), AX.X, ALU.max,
                                                   apply_absolute_value=True))
                chain.step(nc.vector.tensor_scalar(scale_out[:, at, :], scale_out[:, at, :], 1.0 / LEVELS, SCALE_LEAST,
                                                   ALU.mult, ALU.max))
                chain.step(nc.vector.reciprocal(inverse_out[:, at, :], scale_out[:, at, :]))

            def integers(a, at, inverse_out):
                chain.step(nc.vector.tensor_tensor(heads(a, at), heads(a, at), spread(inverse_out, at), ALU.mult))
                chain.step(nc.vector.tensor_scalar(a[:, at, :], a[:, at, :], ROUND, ROUND, ALU.add, ALU.subtract))
                chain.step(nc.vector.tensor_scalar(a[:, at, :], a[:, at, :], LEVELS, -LEVELS, ALU.min, ALU.max))

            def part(at, r):
                return parts[:, at, :, r, :].rearrange("p t h d -> p (t h) d")

            dve.wait_ge(zeroed, 1)
            for half in range(NT // HT):
                at = slice(half * HT, (half + 1) * HT)
                dve.wait_ge(rows_taken, (half + 1) * HT)
                scales(k, at, scale, inverse)
                integers(k, at, inverse)
                chain.step(nc.vector.tensor_tensor(heads(k, at), heads(k, at), spread(scale, at), ALU.mult))
                chain.step(nc.vector.tensor_copy(part(at, 0), heads(k, at)))
                chain.step(nc.vector.tensor_tensor(heads(k, at), heads(k, at), part(at, 0), ALU.subtract))
                chain.step(nc.vector.tensor_copy(part(at, 1), heads(k, at)))
                nc.vector.tensor_tensor(part(at, 2), heads(k, at), part(at, 1), ALU.subtract).then_inc(k_split, 1)
            dve.wait_ge(cols_taken, DC * NH)
            chain.step(nc.vector.tensor_reduce(s.v_scale[:, :], vT[:, :, :], AX.X, ALU.max, apply_absolute_value=True))
            chain.step(nc.vector.tensor_scalar(s.v_scale[:, :], s.v_scale[:, :], 1.0 / LEVELS, SCALE_LEAST, ALU.mult, ALU.max))
            chain.step(nc.vector.reciprocal(v_inverse[:, :], s.v_scale[:, :]))
            for c in range(DC):
                last = nc.vector.tensor_scalar(vT[:, c, :], vT[:, c, :], v_inverse[:, c:c + 1], ROUND, ALU.mult, ALU.add)
            chain.step(last)
            chain.step(nc.vector.tensor_scalar(vT[:, :, :], vT[:, :, :], ROUND, None, ALU.subtract))
            nc.vector.tensor_scalar(vTb[:, :, :], vT[:, :, :], LEVELS, -LEVELS, ALU.min, ALU.max).then_inc(v_rounded, 1)
            for half in range(NT // HT):
                at = slice(half * HT, (half + 1) * HT)
                dve.wait_ge(rows_taken, NT + (half + 1) * HT)
                scales(q, at, s.q_scale, q_inverse)
                integers(q, at, q_inverse)
                dve.wait_ge(turned_ready, NT)
                for r in range(PARTS - 1):
                    last = nc.vector.tensor_copy(part(at, r), heads(q, at))
                last.then_inc(q_split, 1)


def attend(nc, sh, s):
    x, ident = sh.x, sh.ident
    with ExitStack() as ctx:
        sb, ps, sem = scope(nc, ctx, "c2_")
        RING = 6
        MIX_LAG = 5
        ON_ACT = 2
        LOG_LEVELS = float(np.log(LEVELS_P))
        UNITS_C = NT * HEADS_C
        probs = sb("probs", [P, RING, N], I16)
        bits = probs[:, :, :].bitcast(BF16)
        pT = sb("pT", [P, RING, NT, P], BF16)
        neg_max, bias = sb("neg_max", [P, NT, HEADS_C]), sb("bias", [P, NT, HEADS_C])
        row_sum = sb("row_sum", [P, NT, HEADS_C])
        o, oT = sb("o", [P, D]), sb("oT", [P, DC, P])
        scores = ps("scores", [P, 2, 2, HALF])
        turned = ps("turned", [P, 2, 2 * HALF], BF16)
        mixed = ps("mixed", [P, 1, HALF])
        tail = ps("tail", [P, 1, HALF])
        dve_steps = sem("dve_steps")
        scored, bias_ready, exp_done, turned_ready, turned_copied = (
            sem("scored"), sem("bias_ready"), sem("exp_done"), sem("turned_ready"), sem("turned_copied"))
        mixed_ready, o_ready, oT_ready, oT_copied, out_ready, out_added = (
            sem("mixed_ready"), sem("o_ready"), sem("oT_ready"), sem("oT_copied"), sem("out_ready"), sem("out_added"))
        turned_copied_act = sem("turned_copied_act")

        def on_act(u):
            return u % ON_ACT == ON_ACT - 1

        def wait_copied(eng, u):
            acts = sum(on_act(v) for v in range(u + 1))
            if acts:
                eng.wait_ge(turned_copied_act, acts)
            if u + 1 > acts:
                eng.wait_ge(turned_copied, u + 1 - acts)

        block = ctx.enter_context(nc.Block())

        @block.gpsimd
        def _(pool):
            norm_pool(nc, pool, sh.ln, sh.ln.norms + 1)

        @block.tensor
        def _(pe):
            def score(u):
                t, h = divmod(u, HEADS_C)
                if u >= 2:
                    pe.wait_ge(exp_done, u - 1)
                at = slice(h % 2 * P // 2, (h % 2 + 1) * P // 2)
                for n in range(2):
                    last = nc.tensor.matmul(scores[:, u % 2, n, :], s.qT[at, h // 2, t * P:(t + 1) * P],
                                            s.kT[at, h // 2, n * HALF:(n + 1) * HALF], start=True, stop=True)
                last.then_inc(scored, 1)

            def turn(u):
                pe.wait_ge(exp_done, u + 1)
                if u >= 2:
                    wait_copied(pe, u - 2)
                for n in range(NT):
                    last = nc.tensor.transpose(turned[:, u % 2, n * P:(n + 1) * P], bits[:, u % RING, n * P:(n + 1) * P],
                                               s.identb[:, :])
                last.then_inc(turned_ready, 1)

            def mix(u):
                t, h = divmod(u, HEADS_C)
                wait_copied(pe, u)
                if h == 0 and t >= 1:
                    pe.wait_ge(o_ready, t)
                for n in range(NT):
                    last = nc.tensor.matmul(mixed[:, 0, h * HD_C:(h + 1) * HD_C], pT[:, u % RING, n, :],
                                            s.v[:, n, h * HD_C:(h + 1) * HD_C], start=(n == 0), stop=(n == NT - 1))
                last.then_inc(mixed_ready, 1)

            def finish_a(t):
                pe.wait_ge(o_ready, t + 1)
                if t >= 1:
                    pe.wait_ge(out_added, t)
                for c in range(DC):
                    last = nc.tensor.transpose(tail[:, 0, c * P:(c + 1) * P], o[:, c * P:(c + 1) * P], ident[:, :])
                last.then_inc(oT_ready, 1)

            def finish_b(t):
                pe.wait_ge(oT_copied, t + 1)
                for c in range(DC):
                    nc.tensor.matmul(tail[:, 0, 0:D], oT[:, c, :], s.w_p[:, c, :], start=(c == 0), stop=False)
                nc.tensor.matmul(tail[:, 0, 0:D], s.ones[:, :], s.b_p[:, :], start=False, stop=True).then_inc(out_ready, 1)

            for u in range(UNITS_C + MIX_LAG):
                if u < UNITS_C:
                    score(u)
                if 2 <= u < UNITS_C + 2:
                    turn(u - 2)
                if u >= MIX_LAG:
                    mix(u - MIX_LAG)
                    t, h = divmod(u - MIX_LAG, HEADS_C)
                    if h == 3 and t >= 1:
                        finish_a(t - 1)
                    if h == 7 and t >= 1:
                        finish_b(t - 1)
            finish_a(NT - 1)
            finish_b(NT - 1)

        @block.scalar
        def _(act):
            def copy_turned(u):
                act.wait_ge(turned_ready, u + 1)
                if u >= RING:
                    act.wait_ge(mixed_ready, u - RING + 1)
                nc.scalar.copy(pT[:, u % RING, :, :].rearrange("p n q -> p (n q)"), turned[:, u % 2, :].bitcast(I16)).then_inc(turned_copied_act, 1)

            for u in range(UNITS_C + 2):
                if u < UNITS_C:
                    t, h = divmod(u, HEADS_C)
                    act.wait_ge(bias_ready, u + 1)
                    if u >= RING:
                        act.wait_ge(turned_ready, u - RING + 1)
                    nc.scalar.activation(probs[:, u % RING, :], scores[:, u % 2, :, :].rearrange("p a b -> p (a b)"), ACT.Exp,
                                         bias=bias[:, t, h:h + 1], scale=s.q_scale[:, t, h:h + 1],
                                         accum_out=row_sum[:, t, h:h + 1]).then_inc(exp_done, 1)
                if u >= 2 and on_act(u - 2):
                    copy_turned(u - 2)

        @block.vector
        def _(dve):
            chain = Chain(dve, dve_steps)

            def row_max(u):
                t, h = divmod(u, HEADS_C)
                dve.wait_ge(scored, u + 1)
                chain.step(nc.vector.tensor_reduce(neg_max[:, t, h:h + 1], scores[:, u % 2, :, :].rearrange("p a b -> p (a b)"),
                                                   AX.X, ALU.max, negate=True))
                nc.vector.tensor_scalar(bias[:, t, h:h + 1], neg_max[:, t, h:h + 1], s.q_scale[:, t, h:h + 1], LOG_LEVELS,
                                        ALU.mult, ALU.add).then_inc(bias_ready, 1)

            def copy_turned(u):
                dve.wait_ge(turned_ready, u + 1)
                if u >= RING:
                    dve.wait_ge(mixed_ready, u - RING + 1)
                nc.vector.tensor_copy(pT[:, u % RING, :, :].rearrange("p n q -> p (n q)"), turned[:, u % 2, :].bitcast(I16)).then_inc(turned_copied, 1)

            def normalise(t):
                dve.wait_ge(exp_done, HEADS_C * (t + 1))
                chain.step(nc.vector.reciprocal(row_sum[:, t, :], row_sum[:, t, :]))
                dve.wait_ge(mixed_ready, HEADS_C * (t + 1))
                if t >= 1:
                    dve.wait_ge(oT_ready, t)
                nc.vector.tensor_tensor(o[:, :].rearrange("p (h d) -> p h d", d=HD_C),
                                        mixed[:, 0, 0:D].rearrange("p (h d) -> p h d", d=HD_C),
                                        row_sum[:, t, :].rearrange("p (h o) -> p h o", o=1).broadcast_to([P, HEADS_C, HD_C]),
                                        ALU.mult).then_inc(o_ready, 1)

            def scale_values(t):
                dve.wait_ge(oT_ready, t + 1)
                if t >= 1:
                    dve.wait_ge(out_ready, t)
                for c in range(DC):
                    last = nc.vector.tensor_scalar(oT[:, c, :], tail[:, 0, c * P:(c + 1) * P], s.v_scale[:, c:c + 1], None, ALU.mult)
                last.then_inc(oT_copied, 1)

            def residual(t):
                dve.wait_ge(out_ready, t + 1)
                nc.vector.tensor_tensor(x[:, t, :], x[:, t, :], tail[:, 0, 0:D], ALU.add).then_inc(out_added, 1)
                dve.wait_ge(out_added, t + 1)
                norm_statistics(nc, dve, sh, t)

            for u in range(UNITS_C + 2):
                if u < UNITS_C:
                    row_max(u)
                if u >= 2 and not on_act(u - 2):
                    copy_turned(u - 2)
                if u >= HEADS_C + 2:
                    t, h = divmod(u - 2, HEADS_C)
                    if h == MIX_LAG - 2:
                        normalise(t - 1)
                    if h == 9:
                        scale_values(t - 1)
                    if h == 12:
                        residual(t - 1)
            normalise(NT - 1)
            scale_values(NT - 1)
            residual(NT - 1)


EXPERTS = 16
KEPT = 2
INNER = 176
RANKS = EXPERTS + 1
PICKS = KEPT * NT
SORTED = KEPT * NT + EXPERTS
GROUP = 4
OUT_STORES = 4
FAR = INNER - P


EW_LOADS = 16 * (DC + 2)


def expert_weights(nc, ctx, sh):
    sb, ps, sem = scope(nc, ctx, "ew_")
    ew = sh.ew = Buffers()
    ew.w13 = sb("w13", [P, DC, RANKS * 2 * INNER])
    ew.w2 = sb("w2", [P, 2, RANKS, D])
    ew.rows_in = nc.dram_tensor("sorted_rows", (SORTED * P, D), F32).ap()
    ew.rows_out = nc.dram_tensor("expert_rows", (SORTED * P, D), F32).ap()
    ew.loaded, ew.zeroed = sem("loaded"), sem("zeroed")
    ew.padded = sem("padded")


def load_experts(nc, ew, i):
    with nc.Block() as block:

        @block.vector
        def _(dve):
            nc.vector.memset(ew.w2[:, 1, :, :], 0.0).then_inc(ew.padded, 1)

        @block.sync
        def _(sp):
            for c in range(DC):
                sp.dma_start(ew.w13[:, c, :], i["w13"][c]).then_inc(ew.loaded, 16)
            sp.dma_start(ew.w2[:, 0, :, :], i["w2_near"]).then_inc(ew.loaded, 16)
            sp.wait_ge(ew.padded, 1)
            sp.dma_start(ew.w2[0:FAR, 1, :, :], i["w2_far"]).then_inc(ew.loaded, 16)
            zeros = ew.w2[P // 2:, 1, 0:1, :].broadcast_to([P // 2, 2 * SORTED, D])
            sp.dma_start(ew.rows_in.rearrange("(j p) d -> p j d", p=P // 2), zeros).then_inc(ew.zeroed, 16)


def routed_experts(nc, sh, i, out_dram, out_stored):
    with ExitStack() as ctx:
        sb, ps, sem = scope(nc, ctx, "e0_")
        s = Buffers()
        s.xn = sb("xn", [P, NT, D])
        s.place = sb("place", [P, PICKS], U32)
        s.weight = sb("weight", [P, KEPT, NT])
        s.tile_expert = sb("tile_expert", [P, SORTED], I32)
        s.gated = sb("gated", [P, 2, 2 * P])
        s.ready = sem("ready")
        route(nc, sh, s, i)
        mix_experts(nc, sh, s, out_dram, out_stored)


def route(nc, sh, s, i):
    x, xT, ident = sh.x, sh.xT, sh.ident
    with ExitStack() as ctx:
        sb, ps, sem = scope(nc, ctx, "e1_")
        ln = norm_buffers(sb, ps, sh)
        ln.xn = s.xn
        gate, bias = sb("gate", [P, DC, EXPERTS]), sb("bias", [P, EXPERTS])
        number, number_i = sb("number", [P, SORTED]), sb("number_i", [P, SORTED], I32)
        score, chosen = sb("score", [P, NT, EXPERTS]), sb("chosen", [P, NT, EXPERTS])
        best, at, atf = sb("best", [P, NT, 8]), sb("at", [P, NT, 8], U32), sb("atf", [P, NT, 8])
        picked = sb("picked", [P, PICKS, EXPERTS])
        pickedb = sb("pickedb", [P, PICKS, EXPERTS], BF16)
        ranked = sb("ranked", [P, PICKS, EXPERTS])
        total, placef = sb("total", [P, NT]), sb("placef", [P, PICKS])
        earlier, onesb = sb("earlier", [P, P], BF16), sb("onesb", [P, P], BF16)
        tiles, end, start = sb("tiles", [P, EXPERTS]), sb("end", [P, EXPERTS]), sb("start", [P, EXPERTS])
        before, ones = sb("before", [P, SORTED, EXPERTS]), sb("ones", [P, EXPERTS])
        expert = sb("expert", [P, SORTED])
        logits = ps("logits", [P, 1, HALF])
        rank = ps("rank", [P, 1, HALF])
        ranks = rank[:, 0, 0:(PICKS + 1) * EXPERTS].rearrange("p (j e) -> p j e", e=EXPERTS)
        loaded, dve_steps, consts = sem("loaded"), sem("dve_steps"), sem("consts")
        logits_ready, score_ready, picked_ready, rank_ready = (
            sem("logits_ready"), sem("score_ready"), sem("picked_ready"), sem("rank_ready"))
        block = ctx.enter_context(nc.Block())

        @block.sync
        def _(sp):
            sp.dma_start(gate[:, :, :], i["gate"]).then_inc(loaded, 16)
            sp.dma_start(bias[:, :], i["bias"].broadcast_to([P, EXPERTS])).then_inc(loaded, 16)

        @block.gpsimd
        def _(pool):
            nc.gpsimd.iota(number_i[:, :], [[1, SORTED]], base=0, channel_multiplier=0).then_inc(consts, 1)
            nc.gpsimd.memset(onesb[:, :], 1.0).then_inc(consts, 1)
            nc.gpsimd.memset(earlier[:, :], 1.0).then_inc(consts, 1)
            nc.gpsimd.memset(ones[:, :], 1.0).then_inc(consts, 1)
            nc.gpsimd.memset(s.gated[:, :, :], 0.0).then_inc(consts, 1)
            pool.wait_ge(consts, 5)
            nc.gpsimd.affine_select(out=earlier[:, :], in_=earlier[:, :], compare_op=ALU.is_gt, fill=0.0, base=0,
                                    pattern=[[1, P]], channel_multiplier=-1).then_inc(consts, 1)
            pool.wait_ge(consts, 6)

        @block.tensor
        def _(pe):
            norm_tensor(nc, pe, ln, ident)
            pe.wait_ge(loaded, 32)
            pe.wait_ge(ln.copied, ln.tiles + NT)
            for t in range(NT):
                for c in range(DC):
                    last = nc.tensor.matmul(logits[:, 0, t * EXPERTS:(t + 1) * EXPERTS], xT[:, c, t * P:(t + 1) * P],
                                            gate[:, c, :], start=(c == 0), stop=(c == DC - 1))
            last.then_inc(logits_ready, 1)
            pe.wait_ge(consts, 6)
            pe.wait_ge(picked_ready, 1)
            nc.tensor.matmul(ranks[:, 0:PICKS, :], earlier[:, :], pickedb[:, :, :], start=True, stop=False,
                             skip_group_check=True)
            for j in range(PICKS):
                last = nc.tensor.matmul(ranks[:, j + 1:, :], onesb[:, :],
                                        pickedb[:, j:j + 1, :].broadcast_to([P, PICKS - j, EXPERTS]),
                                        start=False, stop=(j == PICKS - 1), skip_group_check=True)
            last.then_inc(rank_ready, 1)

        @block.scalar
        def _(act):
            norm_scalar(nc, act, ln, lambda t: xT[:, :, t * P:(t + 1) * P])
            act.wait_ge(logits_ready, 1)
            nc.scalar.activation(score[:, :, :].rearrange("p t e -> p (t e)"), logits[:, 0, 0:NT * EXPERTS],
                                 ACT.Sigmoid).then_inc(score_ready, 1)

        @block.vector
        def _(dve):
            chain = Chain(dve, dve_steps)
            norm_vector(nc, dve, ln, x, chain)
            dve.wait_ge(consts, 4)
            nc.vector.tensor_copy(number[:, :], number_i[:, :])
            dve.wait_ge(loaded, 32)
            dve.wait_ge(score_ready, 1)
            chain.step(nc.vector.tensor_tensor(chosen[:, :, :], score[:, :, :],
                                               bias[:, :].rearrange("p (o e) -> p o e", o=1).broadcast_to([P, NT, EXPERTS]), ALU.add))
            for t in range(NT):
                last = nc.vector.max(best[:, t, :], chosen[:, t, :])
            chain.step(last)
            for t in range(NT):
                last = nc.vector.max_index(at[:, t, :], best[:, t, :], chosen[:, t, :])
            chain.step(last)
            chain.step(nc.vector.tensor_copy(atf[:, :, :], at[:, :, :]))
            numbers = number[:, 0:EXPERTS].rearrange("p (o e) -> p o e", o=1)
            for k in range(KEPT):
                last = nc.vector.tensor_tensor(picked[:, k * NT:(k + 1) * NT, :], atf[:, :, k:k + 1].broadcast_to([P, NT, EXPERTS]),
                                               numbers.broadcast_to([P, NT, EXPERTS]), ALU.is_equal)
            chain.step(last)
            nc.vector.tensor_copy(pickedb[:, :, :], picked[:, :, :]).then_inc(picked_ready, 1)
            for k in range(KEPT):
                last = nc.vector.tensor_tensor(ranked[:, k * NT:(k + 1) * NT, :], picked[:, k * NT:(k + 1) * NT, :],
                                               score[:, :, :], ALU.mult)
            chain.step(last)
            chain.step(nc.vector.tensor_reduce(s.weight[:, :, :].rearrange("p k t -> p (k t)"), ranked[:, :, :], AX.X, ALU.add))
            chain.step(nc.vector.tensor_tensor(total[:, :], s.weight[:, 0, :], s.weight[:, 1, :], ALU.add))
            chain.step(nc.vector.reciprocal(total[:, :], total[:, :]))
            for k in range(KEPT):
                nc.vector.tensor_tensor(s.weight[:, k, :], s.weight[:, k, :], total[:, :], ALU.mult)
            dve.wait_ge(rank_ready, 1)
            chain.step(nc.vector.tensor_scalar(tiles[:, :], ranks[:, PICKS, :], 1.0 / P, (P - 1.0) / P - 0.5 + 0.25 / P,
                                               ALU.mult, ALU.add))
            chain.step(nc.vector.tensor_scalar(tiles[:, :], tiles[:, :], ROUND, ROUND, ALU.add, ALU.subtract))
            chain.step(nc.vector.tensor_tensor_scan(end[:, :], ones[:, :], tiles[:, :], 0.0, ALU.mult, ALU.add))
            nc.vector.tensor_tensor(before[:, :, :], end[:, :].rearrange("p (o e) -> p o e", o=1).broadcast_to([P, SORTED, EXPERTS]),
                                    number[:, :].rearrange("p (j o) -> p j o", o=1).broadcast_to([P, SORTED, EXPERTS]), ALU.is_le)
            chain.step(nc.vector.tensor_tensor(start[:, :], end[:, :], tiles[:, :], ALU.subtract))
            chain.step(nc.vector.scalar_tensor_tensor(ranked[:, :, :], start[:, :].rearrange("p (o e) -> p o e", o=1).broadcast_to([P, PICKS, EXPERTS]),
                                                      float(P), ranks[:, 0:PICKS, :], ALU.mult, ALU.add))
            chain.step(nc.vector.tensor_tensor(ranked[:, :, :], ranked[:, :, :], picked[:, :, :], ALU.mult))
            chain.step(nc.vector.tensor_reduce(placef[:, :], ranked[:, :, :], AX.X, ALU.add))
            nc.vector.tensor_copy(s.place[:, :], placef[:, :]).then_inc(s.ready, 1)
            chain.step(nc.vector.tensor_reduce(expert[:, :], before[:, :, :], AX.X, ALU.add))
            nc.vector.tensor_scalar(s.tile_expert[:, :], expert[:, :], EXPERTS - 1.0, None, ALU.min).then_inc(s.ready, 1)


def mix_experts(nc, sh, s, out_dram, out_stored):
    x, xT, ident, ew = sh.x, sh.xT, sh.ident, sh.ew
    with ExitStack() as ctx:
        sb, ps, sem = scope(nc, ctx, "e2_")
        units = NT + SORTED
        row = sb("row", [P, SORTED, D])
        rowT = sb("rowT", [P, 2, DC, P])
        gatedT = sb("gatedT", [P, 2, 2, P])
        made = sb("made", [P, SORTED, D])
        turned = ps("turned", [P, 2, HALF])
        hidden = ps("hidden", [P, 2, HALF])
        gated_turned = ps("gated_turned", [P, 2, HALF])
        y = ps("y", [P, 2, HALF])
        scattered, stored = sem("scattered"), sem("stored")
        fetched = [sem("fetched%d" % j) for j in range(NT // 2)]
        row_loaded = [sem("row_loaded%d" % j) for j in range(SORTED // GROUP)]
        turned_ready, turned_copied, hidden_ready, silu_ready, gated_ready = (
            sem("turned_ready"), sem("turned_copied"), sem("hidden_ready"), sem("silu_ready"), sem("gated_ready"))
        gated_turned_ready, gated_copied, y_ready, y_taken, added = (
            sem("gated_turned_ready"), sem("gated_copied"), sem("y_ready"), sem("y_taken"), sem("added"))
        block = ctx.enter_context(nc.Block())

        @block.gpsimd
        def _(pool):
            pool.wait_ge(s.ready, 1)
            pool.wait_ge(ew.zeroed, 16)
            for j in range(PICKS):
                nc.gpsimd.indirect_dma_start(ew.rows_in, bass.IndirectOffsetOnAxis(s.place[:, j:j + 1], 0),
                                             s.xn[:, j % NT, :], None).then_inc(scattered, 16)
            pool.wait_ge(stored, 16 * (SORTED // GROUP))
            for t in range(NT):
                for k in range(KEPT):
                    j = k * NT + t
                    nc.gpsimd.indirect_dma_start(row[:, j, :], None, ew.rows_out,
                                                 bass.IndirectOffsetOnAxis(s.place[:, j:j + 1], 0)).then_inc(fetched[t // 2], 16)

        @block.sync
        def _(sp):
            sp.wait_ge(scattered, 16 * PICKS)
            for g in range(SORTED // GROUP):
                sp.dma_start(row[:, g * GROUP:(g + 1) * GROUP, :],
                             ew.rows_in[g * GROUP * P:(g + 1) * GROUP * P, :].rearrange("(j p) d -> p j d", p=P)
                             ).then_inc(row_loaded[g], 16)
            for g in range(SORTED // GROUP):
                sp.wait_ge(y_taken, NT + (g + 1) * GROUP)
                sp.dma_start(ew.rows_out[g * GROUP * P:(g + 1) * GROUP * P, :].rearrange("(j p) d -> p j d", p=P),
                             made[:, g * GROUP:(g + 1) * GROUP, :]).then_inc(stored, 16)
            sp.wait_ge(stored, 16 * (SORTED // GROUP))
            for n in range(OUT_STORES):
                at = slice(n * NT // OUT_STORES, (n + 1) * NT // OUT_STORES)
                sp.wait_ge(added, KEPT * at.stop)
                sp.dma_start(out_dram[:, at, :], x[:, at, :]).then_inc(out_stored, 16)
            sp.wait_ge(out_stored, 16 * OUT_STORES)

        @block.tensor
        def _(pe):
            expert = {}

            def turn(j):
                if j % GROUP == 0:
                    pe.wait_ge(row_loaded[j // GROUP], 16)
                if j >= 2:
                    pe.wait_ge(turned_copied, j - 1)
                for c in range(DC):
                    last = nc.tensor.transpose(turned[:, j % 2, c * P:(c + 1) * P], row[:, j, c * P:(c + 1) * P], ident[:, :])
                last.then_inc(turned_ready, 1)

            def up(u):
                j = u - NT
                if j >= 0:
                    pe.wait_ge(turned_copied, j + 1)
                    expert[j] = pe.value_load(s.tile_expert[0:1, j:j + 1], min_val=0, max_val=EXPERTS - 1)
                if u >= 2:
                    pe.wait_ge(gated_ready, u - 1)
                for c in range(DC):
                    if j < 0:
                        left = xT[:, c, u * P:(u + 1) * P]
                        right = ew.w13[:, c, EXPERTS * 2 * INNER:]
                    else:
                        left = rowT[:, j % 2, c, :]
                        right = ew.w13[:, c, bass.ds(expert[j] * (2 * INNER), 2 * INNER)]
                    last = nc.tensor.matmul(hidden[:, u % 2, 0:2 * INNER], left, right, start=(c == 0), stop=(c == DC - 1))
                last.then_inc(hidden_ready, 1)

            def turn_gated(u):
                pe.wait_ge(gated_ready, u + 1)
                if u >= 2:
                    pe.wait_ge(gated_copied, u - 1)
                for c in range(2):
                    last = nc.tensor.transpose(gated_turned[:, u % 2, c * P:(c + 1) * P], s.gated[:, u % 2, c * P:(c + 1) * P], ident[:, :])
                last.then_inc(gated_turned_ready, 1)

            def down(u):
                j = u - NT
                pe.wait_ge(gated_copied, u + 1)
                if u >= 2:
                    pe.wait_ge(y_taken, u - 1)
                for c in range(2):
                    right = ew.w2[:, c, EXPERTS, :] if j < 0 else ew.w2[:, c, bass.ds(expert[j], 1), :]
                    last = nc.tensor.matmul(y[:, u % 2, 0:D], gatedT[:, u % 2, c, :], right, start=(c == 0), stop=(c == 1))
                last.then_inc(y_ready, 1)

            pe.wait_ge(ew.loaded, EW_LOADS)
            pe.wait_ge(s.ready, 2)
            for n in range(units + 3):
                if NT <= n < units:
                    turn(n - NT)
                if 1 <= n <= units:
                    up(n - 1)
                if 2 <= n <= units + 1:
                    turn_gated(n - 2)
                if n >= 3:
                    down(n - 3)

        @block.scalar
        def _(act):
            def copy_turned(j):
                act.wait_ge(turned_ready, j + 1)
                if j >= 2:
                    act.wait_ge(hidden_ready, NT + j - 1)
                nc.scalar.copy(rowT[:, j % 2, :, :].rearrange("p c n -> p (c n)"), turned[:, j % 2, 0:D]).then_inc(turned_copied, 1)

            for n in range(units + 1):
                if NT <= n < units:
                    copy_turned(n - NT)
                if n >= 1:
                    u = n - 1
                    act.wait_ge(hidden_ready, u + 1)
                    if u >= 2:
                        act.wait_ge(gated_turned_ready, u - 1)
                    nc.scalar.activation(s.gated[:, u % 2, 0:INNER], hidden[:, u % 2, 0:INNER], ACT.Silu).then_inc(silu_ready, 1)

        @block.vector
        def _(dve):
            def gate(u):
                dve.wait_ge(silu_ready, u + 1)
                nc.vector.tensor_tensor(s.gated[:, u % 2, 0:INNER], hidden[:, u % 2, INNER:2 * INNER],
                                        s.gated[:, u % 2, 0:INNER], ALU.mult).then_inc(gated_ready, 1)

            def copy_gated(u):
                dve.wait_ge(gated_turned_ready, u + 1)
                if u >= 2:
                    dve.wait_ge(y_ready, u - 1)
                nc.vector.tensor_copy(gatedT[:, u % 2, :, :].rearrange("p c n -> p (c n)"),
                                      gated_turned[:, u % 2, 0:2 * P]).then_inc(gated_copied, 1)

            def take(u):
                dve.wait_ge(y_ready, u + 1)
                if u < NT:
                    nc.vector.tensor_tensor(x[:, u, :], x[:, u, :], y[:, u % 2, 0:D], ALU.add).then_inc(y_taken, 1)
                else:
                    nc.vector.tensor_copy(made[:, u - NT, :], y[:, u % 2, 0:D]).then_inc(y_taken, 1)

            for n in range(units + 2):
                if n < units:
                    gate(n)
                if 1 <= n <= units:
                    copy_gated(n - 1)
                if n >= 2:
                    take(n - 2)
            dve.wait_ge(y_taken, NT)
            for t in range(NT):
                for k in range(KEPT):
                    dve.wait_ge(fetched[t // 2], 16 * 2 * KEPT)
                    if k >= 1:
                        dve.wait_ge(added, t * KEPT + k)
                    nc.vector.scalar_tensor_tensor(x[:, t, :], row[:, k * NT + t, :], s.weight[:, k, t:t + 1], x[:, t, :],
                                                   ALU.mult, ALU.add).then_inc(added, 1)



def decoder(nc, i, out):
    with ExitStack() as ctx:
        sb, ps, sem = scope(nc, ctx, "")
        stored = sem("stored")
        sh = Buffers()
        sh.ln = norm_shared(sb, sem)
        sh.x = sb("x", [P, NT, D])
        sh.xT = sb("xT", [P, DC, N])
        sh.ident = sb("ident", [P, P])
        sh.ctxT = sb("ctxT", [P, DC, EXPERTS_T * D])
        sh.tokens_loaded = sem("tokens_loaded")
        start_stage(nc, sh.x, sh.ident, i["x"])
        with ExitStack() as layer0:
            retrieval_tables(nc, layer0, sh)
            with ExitStack() as early:
                early_weights(nc, early, sh)
                linear_attention(nc, sh, i)
                token_experts(nc, sh, i)
                private_state(nc, sh, sh.r, i)
            weigh_experts(nc, sh, sh.r)
        context_weights(nc, ctx, sh)
        block_attention(nc, sh, i)
        expert_weights(nc, ctx, sh)
        cross_attention(nc, sh, i)
        routed_experts(nc, sh, i, out, stored)


def rows(a):
    a = np.asarray(a)
    return np.ascontiguousarray(a.reshape(-1, P, a.shape[-1]).transpose(1, 0, 2))


def column(a):
    return np.ascontiguousarray(np.asarray(a).reshape(-1, P).T)


def layouts(g):
    a = {}
    a["x"] = rows(np.asarray(g["x"]).reshape(N, D))
    a["w_qkv"] = rows(g["L0_attn_w_qkv"])
    a["w_out"] = rows(g["L0_attn_w_out"])
    a["decay"] = column(np.repeat(np.asarray(g["L0_attn_decay_param"]), HD0))
    a["ids"] = np.ascontiguousarray(np.asarray(g["itok_BxS_13_99985"]).reshape(1, N))
    a["ctxT"] = rows(np.asarray(g["ctx_2048"]).reshape(N, D).T)
    a["w_up"] = rows(np.asarray(g["L0_ffn_W_up"]).T)
    a["b_up"] = column(g["L0_ffn_b_up"])
    a["w_down"] = rows(np.asarray(g["L0_ffn_W_down"]).T)
    a["b_down"] = column(g["L0_ffn_b_down"])
    a["w_q"] = rows(g["L0_ffn_W_q"])
    k = np.asarray(g["L0_ffn_keys"]).reshape(HEADS_R // 2, 2, KEYS, 2, RETR)
    a["keys"] = np.ascontiguousarray(k.transpose(1, 4, 3, 0, 2).reshape(2, RETR, UC, KEYS))
    a["down"] = np.ascontiguousarray(np.asarray(g["L0_ffn_down_embed"]).T)
    a["up"] = rows(g["L0_ffn_up_embed"])
    w = np.asarray(g["L1_attn_conv_w"]).reshape(TAPS, DC, P, 3 * WIDTH)
    a["conv_w"] = np.ascontiguousarray(w.transpose(2, 0, 1, 3))
    b = np.asarray(g["L1_attn_conv_b"])
    a["conv_b"] = column(np.concatenate([b, np.zeros(P - WIDTH, b.dtype)]))
    a["w_qk"] = np.concatenate([np.asarray(g["L1_attn_" + n]).reshape(WIDTH, WIDE_B) for n in ("wq", "wk")])
    a["b_q"] = column(np.asarray(g["L1_attn_bq"]).reshape(-1))
    a["b_k"] = column(np.asarray(g["L1_attn_bk"]).reshape(-1))
    a["w_v"] = np.concatenate([np.asarray(g["L1_attn_wv"]).reshape(WIDTH, WIDE_B),
                               np.asarray(g["L1_attn_bv"]).reshape(1, WIDE_B)])
    a["w_o"] = rows(np.asarray(g["L1_attn_wo"]).reshape(WIDE_B, WIDTH))
    a["b_o"] = np.asarray(g["L1_attn_bo"]).reshape(WIDTH, 1)
    a["proj"] = np.concatenate([np.asarray(g["L1_attn_proj_w"]), np.asarray(g["L1_attn_proj_b"]).reshape(1, D)])
    a["w_kv"] = rows(g["L1_xattn_Wkv"])
    a["w_qc"] = rows(g["L1_xattn_Wq"])
    a["w_p"] = rows(g["L1_xattn_Wp"])
    b = np.asarray(g["L1_xattn_bkv"])
    a["b_kc"] = b[:D].reshape(1, D)
    a["b_v"] = column(b[D:])
    a["b_qc"] = np.asarray(g["L1_xattn_bq"]).reshape(1, D)
    a["b_p"] = np.asarray(g["L1_xattn_bp"]).reshape(1, D)
    a["gate"] = rows(np.asarray(g["L1_ffn_gate_w"]).T)
    a["bias"] = np.asarray(g["L1_ffn_bias"]).reshape(1, EXPERTS)
    w1 = np.concatenate([np.asarray(g["L1_ffn_w1"]), np.asarray(g["L1_ffn_shared_w1"])[None]])
    w3 = np.concatenate([np.asarray(g["L1_ffn_w3"]), np.asarray(g["L1_ffn_shared_w3"])[None]])
    w = np.concatenate([w1, w3], axis=1).reshape(RANKS * 2 * INNER, D)
    a["w13"] = np.ascontiguousarray(w.T.reshape(DC, P, RANKS * 2 * INNER))
    w2 = np.concatenate([np.asarray(g["L1_ffn_w2"]), np.asarray(g["L1_ffn_shared_w2"])[None]]).transpose(2, 0, 1)
    a["w2_near"], a["w2_far"] = np.ascontiguousarray(w2[:P]), np.ascontiguousarray(w2[P:])
    return a


def kernel(**inputs):
    import concourse.bacc as bacc
    from concourse.bass_utils import run_bass_kernel_spmd

    nc = bacc.Bacc("TRN2", target_bir_lowering=False, num_devices=1)
    arrays, aps = {}, {}
    for name, a in layouts(inputs).items():
        arrays["in_" + name] = a
        aps[name] = nc.dram_tensor("in_" + name, a.shape, mybir.dt.from_np(a.dtype), kind="ExternalInput").ap()
    out = nc.dram_tensor("out", (P, NT, D), F32, kind="ExternalOutput").ap()
    decoder(nc, aps, out)
    r = run_bass_kernel_spmd(nc, [arrays], core_ids=[0])
    return np.asarray(r.results[0]["out"]).transpose(1, 0, 2).reshape(B, T, D)
```
